# Optimizing a Trainium2 kernel written in Bass

```python
import numpy as np
import jax
import jax.numpy as jnp

def _softmax(x, axis=-1):
    return jax.nn.softmax(x, axis=axis)

def _gelu(x):
    return jax.nn.gelu(x, approximate=True)

def _silu(x):
    return jax.nn.silu(x)

def _sigmoid(x):
    return jax.nn.sigmoid(x)

def _layernorm(x, axis=-1, eps=1e-05):
    m = jnp.mean(x, axis=axis, keepdims=True)
    v = jnp.var(x, axis=axis, keepdims=True)
    return (x - m) / jnp.sqrt(v + eps)

def _scatter_add(tgt, idx, src, axis=0):
    return tgt.at[idx].add(src)

def _segment_sum(src, seg, n):
    return jax.ops.segment_sum(src, seg, n)
kernel_name = 'mk_flamingo_gated_d2_seqx_r4_918ffd'

def setup_inputs(seed: int=0):
    np.random.seed(seed)
    _w = jnp.asarray

    def _rec_inputs():
        import jax
        import jax.numpy as jnp
        _rk = jax.random.key(seed)
        x = -0.0003929 + 0.9999 * jax.random.normal(jax.random.fold_in(_rk, 1), (8, 256, 256), jnp.float32)
        _lenS = 256 - jax.random.randint(jax.random.fold_in(_rk, 7), (8,), 0, max(1, 256 // 4) + 1, jnp.int32)
        _lenS2 = 256 - jax.random.randint(jax.random.fold_in(_rk, 8), (8,), 0, max(1, 256 // 4) + 1, jnp.int32)
        _ctx_1024P = jax.random.normal(jax.random.fold_in(_rk, 11), (8, 16, 256), jnp.float32)
        _ctx_1024c = jax.random.dirichlet(jax.random.fold_in(_rk, 511), 0.3 * jnp.ones((16,), jnp.float32), (8, 256))
        _ctx_1024t = jnp.einsum('bsk,bkd->bsd', _ctx_1024c, _ctx_1024P)
        _ctx_1024t = _ctx_1024t * jax.lax.rsqrt(jnp.mean(jnp.square(_ctx_1024t)) + 1e-12) * 0.953939
        ctx_1024 = 2.81802e-05 + 1.00001 * (_ctx_1024t + 0.3 * jax.random.normal(jax.random.fold_in(_rk, 611), (8, 256, 256), jnp.float32))
        _g = jax.random.normal(jax.random.fold_in(_rk, 9001), (2, 2), jnp.float32)
        _g = jnp.sign(_g) * jnp.maximum(jnp.abs(_g), 1.0) + (_g == 0) * 1.0
        g_xattn = _g[0]
        g_ffn = _g[1]
        return (x, ctx_1024, g_xattn, g_ffn)
    x, ctx_1024, g_xattn, g_ffn = _rec_inputs()

    def _L0_xattn_setup():
        import jax, jax.numpy as jnp
        import numpy as np
        D1, D2, D3 = (256, 256, 256)
        key = jax.random.key(seed)
        k1, k2, kw, kb = jax.random.split(key, 4)
        x1 = jax.random.normal(k1, (8, 512, D1), dtype=jnp.float32)
        x2 = jax.random.normal(k2, (8, 512, D2), dtype=jnp.float32)
        bound = 1.0 / np.sqrt(D1 + D2)
        W = jax.random.uniform(kw, (D3, D1 + D2), minval=-bound, maxval=bound, dtype=jnp.float32)
        b = jax.random.uniform(kb, (D3,), minval=-bound, maxval=bound, dtype=jnp.float32)
        return {'x1': x1, 'x2': x2, 'W': W, 'b': b}
    _L0_xattn_all = _L0_xattn_setup()
    _L0_xattn_in = {k: v for k, v in _L0_xattn_all.items() if k in ('W', 'b')}
    del _L0_xattn_all

    def _L0_ffn_setup():
        import jax, jax.numpy as jnp
        import numpy as np
        BLOCK = 32
        W_BITS = 4
        ACT_BITS = 16

        def act_qdq(x):
            qmax = 2.0 ** (ACT_BITS - 1) - 1.0
            scale = jnp.maximum(jnp.max(jnp.abs(x)) / qmax, 1e-12)
            return jnp.clip(jnp.round(x / scale), -qmax - 1.0, qmax) * scale

        def fixed_qdq_u16(x):
            scale = 1.0 / 65536.0
            return jnp.clip(jnp.round(x / scale), 0.0, 65535.0) * scale

        def lpbq_dequant(w):
            O, I = w.shape
            qmax = 2.0 ** (W_BITS - 1) - 1.0
            wb = w.reshape(O, I // BLOCK, BLOCK)
            s = jnp.maximum(jnp.max(jnp.abs(wb), axis=-1, keepdims=True) / qmax, 1e-12)
            wq = jnp.clip(jnp.round(wb / s), -qmax - 1.0, qmax) * s
            return wq.reshape(O, I)
        key = jax.random.key(seed)
        k1, k2, k3, k4 = jax.random.split(key, 4)
        B, S, H, I = (2, 1024, 256, 768)
        x = jax.random.normal(k1, (B, S, H), jnp.float32)
        w_gate = jax.random.normal(k2, (I, H), jnp.float32) * 0.02
        w_up = jax.random.normal(k3, (I, H), jnp.float32) * 0.02
        w_down = jax.random.normal(k4, (H, I), jnp.float32) * 0.02
        return {'x': x, 'w_gate': w_gate, 'w_up': w_up, 'w_down': w_down}
    _L0_ffn_all = _L0_ffn_setup()
    _L0_ffn_in = {k: v for k, v in _L0_ffn_all.items() if k in ('w_gate', 'w_up', 'w_down')}
    del _L0_ffn_all

    def _L1_xattn_setup():
        import jax, jax.numpy as jnp
        import numpy as np
        B, LQ, LK, D1, D2 = (16, 512, 512, 256, 256)
        key = jax.random.key(seed)
        k1, k2, k3, k4 = jax.random.split(key, 4)
        keys = jax.random.normal(k1, (B, LK, D2), dtype=jnp.float32)
        queries = jax.random.normal(k2, (B, LQ, D1), dtype=jnp.float32)
        W = jax.random.normal(k3, (D2, D1), dtype=jnp.float32) / np.sqrt(D1)
        b = jax.random.normal(k4, (D2,), dtype=jnp.float32) * 0.01
        return {'keys': keys, 'queries': queries, 'W': W, 'b': b}
    _L1_xattn_all = _L1_xattn_setup()
    _L1_xattn_in = {k: v for k, v in _L1_xattn_all.items() if k in ('W', 'b')}
    del _L1_xattn_all

    def _L1_ffn_setup():
        import jax, jax.numpy as jnp
        import numpy as np
        D = 256
        HD = 128
        EA = 8
        KA = 2
        EF = 16
        KF = 2
        FH = 128
        MAXP = 64
        B, S = (4, 256)
        EPS = 1e-05

        def _layer_norm(x, w, b):
            mu = x.mean(-1, keepdims=True)
            var = ((x - mu) ** 2).mean(-1, keepdims=True)
            return (x - mu) * jax.lax.rsqrt(var + EPS) * w + b

        def _topk_gates(logits, k):
            top_vals, top_idx = jax.lax.top_k(logits, k)
            g = jax.nn.softmax(top_vals, axis=-1)
            onehot = jax.nn.one_hot(top_idx, logits.shape[-1], dtype=logits.dtype)
            return jnp.einsum('...k,...ke->...e', g, onehot)

        def _moa(x, gate_w, q_w, q_b, k_w, k_b, v_w, v_b, o_w, o_b, rel_table):
            S_ = x.shape[1]
            gates = _topk_gates(x @ gate_w, KA)
            q = (jnp.einsum('bsd,edh->bseh', x, q_w) + q_b) * HD ** (-0.5)
            k = x @ k_w + k_b
            v = x @ v_w + v_b
            scores = jnp.einsum('bqeh,bkh->beqk', q, k)
            rel_s = jnp.einsum('bqeh,rh->beqr', q, rel_table)
            pos = jnp.arange(S_)
            rel_idx = jnp.clip(pos[None, :] - pos[:, None], -MAXP, MAXP) + MAXP
            scores = scores + jnp.take_along_axis(rel_s, rel_idx[None, None], axis=-1)
            p = jax.nn.softmax(scores, axis=-1)
            ctx = jnp.einsum('beqk,bkh->bqeh', p, v)
            out = jnp.einsum('bqeh,ehd,bqe->bqd', ctx, o_w, gates)
            return out + jnp.einsum('bqe,ed->bqd', gates, o_b)

        def _moe_ffn(x, gate_w, w1, b1, w2, b2):
            gates = _topk_gates(x @ gate_w, KF)
            h = jax.nn.relu(jnp.einsum('bsd,edh->bseh', x, w1) + b1)
            out = jnp.einsum('bseh,ehd,bse->bsd', h, w2, gates)
            return out + jnp.einsum('bse,ed->bsd', gates, b2)
        key = jax.random.key(seed)
        ks = jax.random.split(key, 12)
        r = lambda i, shape, scale=0.02: jax.random.normal(ks[i], shape, jnp.float32) * scale
        return {'src': jax.random.normal(ks[0], (B, S, D), jnp.float32), 'ln1_w': jnp.ones((D,), jnp.float32), 'ln1_b': jnp.zeros((D,), jnp.float32), 'ln2_w': jnp.ones((D,), jnp.float32), 'ln2_b': jnp.zeros((D,), jnp.float32), 'attn_gate_w': r(1, (D, EA)), 'q_w': r(2, (EA, D, HD)), 'q_b': jnp.zeros((EA, HD), jnp.float32), 'k_w': r(3, (D, HD)), 'k_b': jnp.zeros((HD,), jnp.float32), 'v_w': r(4, (D, HD)), 'v_b': jnp.zeros((HD,), jnp.float32), 'o_w': r(5, (EA, HD, D)), 'o_b': jnp.zeros((EA, D), jnp.float32), 'rel_table': r(6, (2 * MAXP + 1, HD)), 'ff_gate_w': r(7, (D, EF)), 'ff_w1': r(8, (EF, D, FH)), 'ff_b1': jnp.zeros((EF, FH), jnp.float32), 'ff_w2': r(9, (EF, FH, D)), 'ff_b2': jnp.zeros((EF, D), jnp.float32)}
    _L1_ffn_all = _L1_ffn_setup()
    _L1_ffn_in = {k: v for k, v in _L1_ffn_all.items() if k in ('ln1_w', 'ln1_b', 'ln2_w', 'ln2_b', 'attn_gate_w', 'q_w', 'q_b', 'k_w', 'k_b', 'v_w', 'v_b', 'o_w', 'o_b', 'rel_table', 'ff_gate_w', 'ff_w1', 'ff_b1', 'ff_w2', 'ff_b2')}
    del _L1_ffn_all
    return {'x': x, 'ctx_1024': ctx_1024, 'g_xattn': g_xattn, 'g_ffn': g_ffn, 'L0_xattn_W': _L0_xattn_in['W'], 'L0_xattn_b': _L0_xattn_in['b'], 'L0_ffn_w_gate': _L0_ffn_in['w_gate'], 'L0_ffn_w_up': _L0_ffn_in['w_up'], 'L0_ffn_w_down': _L0_ffn_in['w_down'], 'L1_xattn_W': _L1_xattn_in['W'], 'L1_xattn_b': _L1_xattn_in['b'], 'L1_ffn_ln1_w': _L1_ffn_in['ln1_w'], 'L1_ffn_ln1_b': _L1_ffn_in['ln1_b'], 'L1_ffn_ln2_w': _L1_ffn_in['ln2_w'], 'L1_ffn_ln2_b': _L1_ffn_in['ln2_b'], 'L1_ffn_attn_gate_w': _L1_ffn_in['attn_gate_w'], 'L1_ffn_q_w': _L1_ffn_in['q_w'], 'L1_ffn_q_b': _L1_ffn_in['q_b'], 'L1_ffn_k_w': _L1_ffn_in['k_w'], 'L1_ffn_k_b': _L1_ffn_in['k_b'], 'L1_ffn_v_w': _L1_ffn_in['v_w'], 'L1_ffn_v_b': _L1_ffn_in['v_b'], 'L1_ffn_o_w': _L1_ffn_in['o_w'], 'L1_ffn_o_b': _L1_ffn_in['o_b'], 'L1_ffn_rel_table': _L1_ffn_in['rel_table'], 'L1_ffn_ff_gate_w': _L1_ffn_in['ff_gate_w'], 'L1_ffn_ff_w1': _L1_ffn_in['ff_w1'], 'L1_ffn_ff_b1': _L1_ffn_in['ff_b1'], 'L1_ffn_ff_w2': _L1_ffn_in['ff_w2'], 'L1_ffn_ff_b2': _L1_ffn_in['ff_b2']}

def reference(x, ctx_1024, g_xattn, g_ffn, L0_xattn_W, L0_xattn_b, L0_ffn_w_gate, L0_ffn_w_up, L0_ffn_w_down, L1_xattn_W, L1_xattn_b, L1_ffn_ln1_w, L1_ffn_ln1_b, L1_ffn_ln2_w, L1_ffn_ln2_b, L1_ffn_attn_gate_w, L1_ffn_q_w, L1_ffn_q_b, L1_ffn_k_w, L1_ffn_k_b, L1_ffn_v_w, L1_ffn_v_b, L1_ffn_o_w, L1_ffn_o_b, L1_ffn_rel_table, L1_ffn_ff_gate_w, L1_ffn_ff_w1, L1_ffn_ff_b1, L1_ffn_ff_w2, L1_ffn_ff_b2):
    import jax
    import jax.numpy as jnp

    def _L0_xattn_ref(x1, x2, W, b):
        import jax, jax.numpy as jnp
        import numpy as np
        D1, D2, D3 = (256, 256, 256)
        d1 = x1.shape[-1]
        W1 = W[:, :d1]
        W2 = W[:, d1:]
        part1 = jnp.einsum('bld,ed->ble', x1, W1)
        part2 = jnp.einsum('bld,ed->be', x2, W2) / x2.shape[1]
        return part1 + part2[:, None, :] + b

    def _L0_ffn_ref(x, w_gate, w_up, w_down):
        import jax, jax.numpy as jnp
        import numpy as np
        BLOCK = 32
        W_BITS = 4
        ACT_BITS = 16

        def act_qdq(x):
            qmax = 2.0 ** (ACT_BITS - 1) - 1.0
            scale = jnp.maximum(jnp.max(jnp.abs(x)) / qmax, 1e-12)
            return jnp.clip(jnp.round(x / scale), -qmax - 1.0, qmax) * scale

        def fixed_qdq_u16(x):
            scale = 1.0 / 65536.0
            return jnp.clip(jnp.round(x / scale), 0.0, 65535.0) * scale

        def lpbq_dequant(w):
            O, I = w.shape
            qmax = 2.0 ** (W_BITS - 1) - 1.0
            wb = w.reshape(O, I // BLOCK, BLOCK)
            s = jnp.maximum(jnp.max(jnp.abs(wb), axis=-1, keepdims=True) / qmax, 1e-12)
            wq = jnp.clip(jnp.round(wb / s), -qmax - 1.0, qmax) * s
            return wq.reshape(O, I)
        x = act_qdq(x)
        up = act_qdq(x @ lpbq_dequant(w_up).T)
        gate = act_qdq(x @ lpbq_dequant(w_gate).T)
        sig = fixed_qdq_u16(jax.nn.sigmoid(gate))
        gate = act_qdq(gate * sig)
        o = act_qdq(gate * up)
        return o @ lpbq_dequant(w_down).T

    def _L1_xattn_ref(keys, queries, W, b):
        import jax, jax.numpy as jnp
        import numpy as np
        B, LQ, LK, D1, D2 = (16, 512, 512, 256, 256)
        neg_inf = jnp.float32(-jnp.inf)
        values = jnp.where(keys == neg_inf, jnp.float32(0.0), keys)
        q = jnp.einsum('bqd,ed->bqe', queries, W) + b
        scores = jnp.einsum('bqe,bke->bqk', q, keys)
        scores = jnp.where(jnp.isnan(scores), neg_inf, scores)
        weights = jax.nn.softmax(scores, axis=2)
        return jnp.einsum('bqk,bke->bqe', weights, values)

    def _L1_ffn_ref(src, ln1_w, ln1_b, ln2_w, ln2_b, attn_gate_w, q_w, q_b, k_w, k_b, v_w, v_b, o_w, o_b, rel_table, ff_gate_w, ff_w1, ff_b1, ff_w2, ff_b2):
        import jax, jax.numpy as jnp
        import numpy as np
        D = 256
        HD = 128
        EA = 8
        KA = 2
        EF = 16
        KF = 2
        FH = 128
        MAXP = 64
        B, S = (4, 256)
        EPS = 1e-05

        def _layer_norm(x, w, b):
            mu = x.mean(-1, keepdims=True)
            var = ((x - mu) ** 2).mean(-1, keepdims=True)
            return (x - mu) * jax.lax.rsqrt(var + EPS) * w + b

        def _topk_gates(logits, k):
            top_vals, top_idx = jax.lax.top_k(logits, k)
            g = jax.nn.softmax(top_vals, axis=-1)
            onehot = jax.nn.one_hot(top_idx, logits.shape[-1], dtype=logits.dtype)
            return jnp.einsum('...k,...ke->...e', g, onehot)

        def _moa(x, gate_w, q_w, q_b, k_w, k_b, v_w, v_b, o_w, o_b, rel_table):
            S_ = x.shape[1]
            gates = _topk_gates(x @ gate_w, KA)
            q = (jnp.einsum('bsd,edh->bseh', x, q_w) + q_b) * HD ** (-0.5)
            k = x @ k_w + k_b
            v = x @ v_w + v_b
            scores = jnp.einsum('bqeh,bkh->beqk', q, k)
            rel_s = jnp.einsum('bqeh,rh->beqr', q, rel_table)
            pos = jnp.arange(S_)
            rel_idx = jnp.clip(pos[None, :] - pos[:, None], -MAXP, MAXP) + MAXP
            scores = scores + jnp.take_along_axis(rel_s, rel_idx[None, None], axis=-1)
            p = jax.nn.softmax(scores, axis=-1)
            ctx = jnp.einsum('beqk,bkh->bqeh', p, v)
            out = jnp.einsum('bqeh,ehd,bqe->bqd', ctx, o_w, gates)
            return out + jnp.einsum('bqe,ed->bqd', gates, o_b)

        def _moe_ffn(x, gate_w, w1, b1, w2, b2):
            gates = _topk_gates(x @ gate_w, KF)
            h = jax.nn.relu(jnp.einsum('bsd,edh->bseh', x, w1) + b1)
            out = jnp.einsum('bseh,ehd,bse->bsd', h, w2, gates)
            return out + jnp.einsum('bse,ed->bsd', gates, b2)
        res = src
        xn = _layer_norm(src, ln1_w, ln1_b)
        x = res + _moa(xn, attn_gate_w, q_w, q_b, k_w, k_b, v_w, v_b, o_w, o_b, rel_table)
        res = x
        xn = _layer_norm(x, ln2_w, ln2_b)
        return res + _moe_ffn(xn, ff_gate_w, ff_w1, ff_b1, ff_w2, ff_b2)
    x = x + jnp.tanh(g_xattn[0]) * _L0_xattn_ref(_layernorm(x, axis=-1), ctx_1024, L0_xattn_W, L0_xattn_b)
    x = x + jnp.tanh(g_ffn[0]) * _L0_ffn_ref(_layernorm(x, axis=-1), L0_ffn_w_gate, L0_ffn_w_up, L0_ffn_w_down)
    x = x + jnp.tanh(g_xattn[1]) * _L1_xattn_ref(ctx_1024, _layernorm(x, axis=-1), L1_xattn_W, L1_xattn_b)
    x = x + jnp.tanh(g_ffn[1]) * _L1_ffn_ref(_layernorm(x, axis=-1), L1_ffn_ln1_w, L1_ffn_ln1_b, L1_ffn_ln2_w, L1_ffn_ln2_b, L1_ffn_attn_gate_w, L1_ffn_q_w, L1_ffn_q_b, L1_ffn_k_w, L1_ffn_k_b, L1_ffn_v_w, L1_ffn_v_b, L1_ffn_o_w, L1_ffn_o_b, L1_ffn_rel_table, L1_ffn_ff_gate_w, L1_ffn_ff_w1, L1_ffn_ff_b1, L1_ffn_ff_w2, L1_ffn_ff_b2)
    return x

_drawn_inputs = setup_inputs


def setup_inputs(seed=0):
    import zlib

    import numpy as np

    out = dict(_drawn_inputs(seed))
    spreads = {'g_ffn': (-1.0, 0.2),
     'L1_ffn_ln1_w': (1.0, 0.2),
     'L1_ffn_ln1_b': (0.0, 0.274),
     'L1_ffn_ln2_w': (1.0, 0.2),
     'L1_ffn_ln2_b': (0.0, 0.1),
     'L1_ffn_q_b': (0.0, 0.8),
     'L1_ffn_k_b': (0.0, 2.0),
     'L1_ffn_v_b': (0.0, 0.382),
     'L1_ffn_o_b': (0.0, 0.1),
     'L1_ffn_ff_b1': (0.0, 0.644),
     'L1_ffn_ff_b2': (0.0, 0.1)}
    factors = {'L1_ffn_q_w': 8.0, 'L1_ffn_k_w': 8.0, 'L1_ffn_rel_table': 53.701}
    for name, (base, spread) in spreads.items():
        noise = np.random.default_rng([zlib.crc32(name.encode()), seed]).standard_normal(out[name].shape)
        drawn = base * np.exp(spread * noise) if base else spread * noise
        out[name] = jnp.asarray(drawn.astype(out[name].dtype))
    for name, factor in factors.items():
        out[name] = (out[name] * factor).astype(out[name].dtype)
    return out
```

```python
from contextlib import ExitStack

import numpy as np

import concourse.bass as bass
from concourse import mybir

F32 = mybir.dt.float32
BF16 = mybir.dt.bfloat16
U16 = mybir.dt.uint16
U32 = mybir.dt.uint32
ALU = mybir.AluOpType
ACT = mybir.ActivationFunctionType
AX = mybir.AxisListType
RMAX = bass.bass_isa.ReduceOp.max

P = 128
NB, S, D = 8, 256, 256
N = NB * S
NT = N // P
KD = D // P
FF = 768
KF = FF // P
BLK = 32
EA, HD, MAXP = 8, 128, 64
EF, FH = 16, 128
EPS = 1e-5
MAGIC = 12582912.0
QMAX = 32767.0
CH = 512
NCH = N // CH
RELW = 192
RELROW = 384
UP_BANKS = 6


def hold(eng, sem, value):
    eng.wait_ge(sem, value)
    eng.nop(nofuse=True)


def chained(eng, sem, before):
    count = [0]

    def link(ins):
        count[0] += 1
        ins.then_inc(sem, 1)
        hold(eng, sem, before + count[0])
    return link


def gated_block_kernel(nc, a, out):
    with ExitStack() as ctx:
        def sb(name, shape, dt=F32):
            return ctx.enter_context(nc.sbuf_tensor(name, shape, dt))

        def sem(name):
            return ctx.enter_context(nc.semaphore(name))

        ps = ctx.enter_context(nc.psum_tensor("ps", [P, 8, 512], F32))
        x = sb("x", [P, NT, D])
        lnb = sb("lnb", [P, NT, D])
        xqT = sb("xqT", [P, KD, N])
        up = sb("up", [P, KF, N])
        gate = sb("gate", [P, KF, N])
        ctxT = gate[:, 0:2, :]
        w0 = gate[:, 2, 0:4 * D].rearrange("p (k e) -> p k e", k=4)
        b0 = gate[0:1, 3, 0:D]
        rb = up[0:1, 0, 0:NB * D].rearrange("p (b e) -> p b e", b=NB)
        csum = sb("csum", [P, KD, NB])
        gates = sb("gates", [P, 4])
        tg = sb("tg", [P, 4])
        wnat = up[:, 1:4, :].rearrange("p m n -> p (m n)")[:, 0:18 * D].rearrange("p (g n) -> p g n", n=D)
        wabs = sb("wabs", [P, 144])
        winv = sb("winv", [P, 144])
        wT = sb("wT", [P, 2, KD, FF])
        wdT = sb("wdT", [P, KF, D])
        ident = sb("ident", [P, P])
        ones1 = sb("ones1", [1, P])
        magic = sb("magic", [P, 1])
        neghalf = sb("neghalf", [P, 2])
        st = sb("st", [P, 2, 6])
        mv = sb("mv", [P, 2, 2, 2])
        ve = sb("ve", [P, 2, 2])
        rs = sb("rs", [P, 2, 2])
        xn = sb("xn", [P, 2, 2, D])
        xnT = sb("xnT", [P, 2, KD, S])
        amx = sb("amx", [P, 64])
        pmax = sb("pmax", [P, 2])
        gmx = sb("gmx", [P, 2])
        sx = sb("sx", [P, 2])
        sug = sb("sug", [P, 2, 2])
        sp = sb("sp", [P, 2])
        so = sb("so", [P, 3])
        sig = sb("sig", [P, 2, N])
        oq = up[:, 3:6, :].rearrange("p m n -> p (m n)").rearrange("p (u m c) -> p u m c", u=2, m=KF)

        kvals = lnb
        keysT = xqT
        w1x = sb("w1x", [P, KD, D])
        b1x = sb("b1x", [P, KD])
        infm = sig[:, 0, 0:4 * D].bitcast(U32).rearrange("p (t d) -> p t d", t=4)
        zero = sb("zero", [P, 1])
        c_buf = sig.rearrange("p u n -> p (u n)")
        qx = c_buf[:, 0:1024].rearrange("p (u e s) -> p u e s", u=2, e=KD)
        px = c_buf[:, 1024:2048].rearrange("p (u t s) -> p u t s", u=2, t=2)
        pxT = c_buf[:, 2048:3072].rearrange("p (u k s) -> p u k s", u=2, k=2)
        cmx = sb("cmx", [P, 2, 2]); cnm = sb("cnm", [P, 2, 2]); cz = sb("cz", [P, 2, 2]); crz = sb("crz", [P, 2, 2])
        gflat = gate.rearrange("p m n -> p (m n)")
        qw = gflat[:, 0:2048].rearrange("p (k e) -> p k e", k=KD)
        ow = gflat[:, 2048:4096].rearrange("p (e d) -> p e d", e=EA)
        w1 = gflat[:, 4096:8192].rearrange("p (k f) -> p k f", k=KD)
        w2 = gflat[:, 8192:12288].rearrange("p (e d) -> p e d", e=EF)
        inner = up[:, 0:2, :].rearrange("p a n -> p (a n)").rearrange("p (t d) -> p t d", d=D)
        xmT = up[:, 2:4, :]
        ln = sb("ln", [P, 4, D])
        gw = sb("gw", [P, KD, EA]); kw = sb("kw", [P, KD, HD]); vw = sb("vw", [P, KD, HD])
        gw2 = sb("gw2", [P, KD, EF]); qb = sb("qb", [EA, HD]); ob = sb("ob", [EA, D]); b2 = sb("b2", [EF, D])
        kb = sb("kb", [P, 1]); vb = sb("vb", [P, HD]); b1 = sb("b1", [P, EF])
        relx = sb("relx", [P, 2, RELW]); rele = sb("rele", [P, 2])
        iota = sb("iota", [P, EF]); sel8 = sb("sel8", [EA, EA, P], BF16)
        ghot = sb("ghot", [P, 2, 2, 2, EF])
        G = sb("G", [P, 2, 2, EF])
        hot = sb("hot", [P, 2, 2, 2, EF])
        top = sb("top", [P, 2, 8]); tidx = sb("tidx", [P, 2, 8], U32); tif = sb("tif", [P, 2, 2])
        td = sb("td", [P, 2]); te = sb("te", [P, 2]); gj = sb("gj", [P, 2, 2, 2])
        wdflat = wdT.rearrange("p m d -> p (m d)")
        hotT = wdflat[0:EA, 0:512]; hotTb = wdflat[0:EA, 512:768].bitcast(BF16)
        GT = wdflat[0:EA, 768:1280].rearrange("p (u s) -> p u s", u=2)
        mask = up[:, 4:6, :].rearrange("p a n -> p (a n)").bitcast(BF16)\
            .rearrange("p (u e j s) -> p u e j s", u=2, e=EA, j=2)
        lflat = lnb.rearrange("p t d -> p (t d)")
        xflat = xqT.rearrange("p k n -> p (k n)")
        qsel = lflat[:, 0:512].rearrange("p (j s) -> p j s", j=2)
        qT = lflat[:, 512:1024].rearrange("p (j s) -> p j s", j=2)
        kT = lflat[:, 1024:1280]
        val = lflat[:, 1280:1792].rearrange("p (u k h) -> p u k h", u=2, k=2)
        R = lflat[:, 1792:2560].rearrange("p (t j c) -> p t j c", t=2, j=2)
        B = xflat[:, 0:1024].rearrange("p (j t s) -> p j t s", j=2, t=2)
        pm = xflat[:, 1024:2048].rearrange("p (j t s) -> p j t s", j=2, t=2)
        pmT = xflat[:, 2048:3072].rearrange("p (k c) -> p k c", k=2)
        ctxE = c_buf[:, 0:2048].rearrange("p (e s) -> p e s", e=EA)
        zrow = c_buf[:, 2048:2048 + RELW]
        mmx = sb("mmx", [P, 4]); mnm = sb("mnm", [P, 4]); mz = sb("mz", [P, 4]); mrz = sb("mrz", [P, 4])
        GTa = wT.rearrange("p g k f -> p (g k f)")[0:EF, 0:N]
        gbc = [xflat[:, 2048 * n:2048 * n + 2048] for n in range(2)] + [lflat[:, 2048 * n:2048 * n + 2048] for n in range(2)]
        gbc = [g_.rearrange("p (e c) -> p e c", e=4) for g_ in gbc]
        hg = c_buf[:, 0:1024].rearrange("p (r c) -> p r c", r=2)
        hr = c_buf[:, 1024:2560].rearrange("p (r c) -> p r c", r=3)
        yT = c_buf[:, 2560:3584].rearrange("p (k c) -> p k c", k=KD)
        skew = a["skew"]
        gscr = a["gscr"]

        ld_k = sem("ld_k"); ld_kT = sem("ld_kT"); ld_c = sem("ld_c"); ld_m = sem("ld_m"); ld_q = sem("ld_q")
        ld_e = sem("ld_e"); z_dma = sem("z_dma"); z_set = sem("z_set")
        v_inf = sem("v_inf"); v_ready = sem("v_ready"); rel_ready = sem("rel_ready"); selz = sem("selz")
        c_st = sem("c_st"); c_var = sem("c_var"); c_rstd = sem("c_rstd"); c_xn = sem("c_xn"); c_turned = sem("c_turned")
        c_xnT = sem("c_xnT"); c_qmm = sem("c_qmm"); c_q = sem("c_q"); c_smm = sem("c_smm"); c_max = sem("c_max")
        c_nmax = sem("c_nmax"); c_exp = sem("c_exp"); c_pturn = sem("c_pturn"); c_pT = sem("c_pT"); c_pv = sem("c_pv")
        c_rz = sem("c_rz"); c_x3 = sem("c_x3")
        m_st = sem("m_st"); m_var = sem("m_var"); m_rstd = sem("m_rstd"); m_src = sem("m_src"); m_st2 = sem("m_st2")
        m_var2 = sem("m_var2"); m_rstd2 = sem("m_rstd2"); m_ln = sem("m_ln"); m_w = sem("m_w"); m_xn = sem("m_xn")
        m_turned = sem("m_turned"); m_xnT = sem("m_xnT"); m_log = sem("m_log"); m_top = sem("m_top")
        m_d = sem("m_d"); m_e = sem("m_e"); m_gate = sem("m_gate"); m_hturn = sem("m_hturn"); m_hT = sem("m_hT")
        m_maskmm = sem("m_maskmm"); m_mask = sem("m_mask"); m_kmm = sem("m_kmm"); m_k = sem("m_k"); m_vmm = sem("m_vmm")
        m_v = sem("m_v"); m_qmm = sem("m_qmm"); m_qsel = sem("m_qsel"); m_qT = sem("m_qT"); m_rmm = sem("m_rmm")
        m_r = sem("m_r"); m_rout = sem("m_rout"); m_rin = sem("m_rin"); m_smm = sem("m_smm"); m_max = sem("m_max")
        m_nmax = sem("m_nmax"); m_exp = sem("m_exp"); m_rz = sem("m_rz"); m_p = sem("m_p"); m_pturn = sem("m_pturn")
        m_pT = sem("m_pT"); m_pv = sem("m_pv"); m_cE = sem("m_cE"); m_omm = sem("m_omm"); m_out = sem("m_out")
        n_st = sem("n_st"); n_var = sem("n_var"); n_rstd = sem("n_rstd"); n_ln = sem("n_ln"); n_w = sem("n_w")
        n_xn = sem("n_xn"); n_turned = sem("n_turned"); n_xnT = sem("n_xnT"); n_all = sem("n_all"); n_log = sem("n_log")
        n_top = sem("n_top"); n_d = sem("n_d"); n_e = sem("n_e"); n_gate = sem("n_gate"); n_gturn = sem("n_gturn")
        n_GT = sem("n_GT"); n_base = sem("n_base"); g_out = sem("g_out")
        g_in = [sem(f"g_in{n}") for n in range(4)]
        e_hmm = sem("e_hmm"); e_hg = sem("e_hg"); e_h = sem("e_h"); e_ymm = sem("e_ymm"); e_y = sem("e_y")
        e_yturn = sem("e_yturn"); e_x4 = sem("e_x4")
        ld_x = sem("ld_x"); ld_w0 = sem("ld_w0"); ld_ctxT = sem("ld_ctxT"); ld_g = sem("ld_g")
        ld_wq = sem("ld_wq")
        const_ready = sem("const_ready"); ident_zero = sem("ident_zero")
        tanh_ready = sem("tanh_ready")
        dve0 = sem("dve0")
        csum_ready = sem("csum_ready"); rb_mm = sem("rb_mm"); rb_ready = sem("rb_ready")
        wstep = sem("wstep"); wscaled = sem("wscaled"); wround = sem("wround"); wdq = sem("wdq")
        w_turned = sem("w_turned"); w_ready = sem("w_ready")
        a_st = sem("a_st"); a_var = sem("a_var"); a_rstd = sem("a_rstd"); a_xn = sem("a_xn")
        a_turned = sem("a_turned"); a_xnT = sem("a_xnT"); a_mm = sem("a_mm"); a_x1 = sem("a_x1")
        f_st = sem("f_st"); f_var = sem("f_var"); f_rstd = sem("f_rstd"); f_ln = sem("f_ln")
        f_red = sem("f_red"); f_pmax = sem("f_pmax"); f_gmax = sem("f_gmax"); f_scale = sem("f_scale")
        f_q1 = sem("f_q1"); f_xq = sem("f_xq"); f_turned = sem("f_turned"); f_xqT = sem("f_xqT")
        f_mm = sem("f_mm"); f_ev = sem("f_ev")
        f_g1 = sem("f_g1"); f_g2 = sem("f_g2"); f_sig = sem("f_sig"); f_s1 = sem("f_s1"); f_s2 = sem("f_s2")
        f_prod = sem("f_prod"); f_p1 = sem("f_p1"); f_p2 = sem("f_p2"); f_o = sem("f_o")
        f_o1 = sem("f_o1"); f_oq = sem("f_oq"); f_down = sem("f_down"); f_x2 = sem("f_x2")
        stored = sem("stored")

        x_tok = a["x"].rearrange("b (t p) d -> p (b t) d", p=P)
        out_tok = out.rearrange("b (t p) d -> p (b t) d", p=P)

        def bank(n):
            return ps[:, n, :]

        def bank2(n):
            return ps[:, n, :].rearrange("p (a c) -> p a c", a=2)

        block = ctx.enter_context(nc.Block())

        @block.sync
        def _(sp_):
            for h in range(4):
                sp_.dma_start(x[:, 4 * h:4 * h + 4, :], x_tok[:, 4 * h:4 * h + 4, :]).then_inc(ld_x, 16)
                if h == 0:
                    sp_.dma_start(gates[:, 0:2], a["g_xattn"].partition_broadcast(P)).then_inc(ld_g, 16)
                    sp_.dma_start(gates[:, 2:4], a["g_ffn"].partition_broadcast(P)).then_inc(ld_g, 16)
                    sp_.dma_start(ctxT, a["ctxT"].rearrange("(k p) n -> p k n", p=P)).then_inc(ld_ctxT, 16)
                    sp_.dma_start(w0, a["L0_xattn_WT"].rearrange("(k p) e -> p k e", p=P)).then_inc(ld_w0, 16)
                    sp_.dma_start(b0, a["L0_xattn_b"].rearrange("(a e) -> a e", a=1)).then_inc(ld_w0, 16)
            for n, name in enumerate(("L0_ffn_w_up", "L0_ffn_w_gate")):
                sp_.dma_start(wnat[:, 6 * n:6 * n + 6, :], a[name].rearrange("(g p) n -> p g n", p=P)).then_inc(ld_wq, 16)
            sp_.dma_start(wnat[:, 12:18, :].rearrange("p (h m) n -> p h (m n)", h=2),
                          a["L0_ffn_w_down"].rearrange("(h p) i -> p h i", p=P)).then_inc(ld_wq, 16)
            sp_.dma_start(w1x[:], a["L1_xattn_WT"].rearrange("(k p) e -> p k e", p=P)).then_inc(ld_c, 16)
            sp_.dma_start(b1x[:], a["xattn1_bT"]).then_inc(ld_c, 16)
            for n, name in enumerate(("ln1_w", "ln1_b", "ln2_w", "ln2_b")):
                sp_.dma_start(ln[:, n, :], a["L1_ffn_" + name].partition_broadcast(P)).then_inc(ld_m, 16)
            for dst, name in ((gw, "attn_gate_w"), (kw, "k_w"), (vw, "v_w"), (gw2, "ff_gate_w")):
                sp_.dma_start(dst[:], a["L1_ffn_" + name].rearrange("(k p) e -> p k e", p=P)).then_inc(ld_m, 16)
            for dst, name in ((qb, "q_b"), (ob, "o_b"), (b2, "ff_b2")):
                sp_.dma_start(dst[:], a["L1_ffn_" + name]).then_inc(ld_m, 16)
            sp_.dma_start(kb[:], a["L1_ffn_k_b"].rearrange("(h a) -> h a", a=1)).then_inc(ld_m, 16)
            sp_.dma_start(vb[:], a["L1_ffn_v_b"].partition_broadcast(P)).then_inc(ld_m, 16)
            sp_.dma_start(b1[:], a["ff_b1T"]).then_inc(ld_m, 16)
            sp_.dma_start(relx[:], a["relx"]).then_inc(ld_m, 16)
            sp_.dma_start(rele[:], a["rele"]).then_inc(ld_m, 16)
            sp_.wait_ge(f_xq, NB)
            sp_.dma_start(kvals[:], a["ctx_1024"].rearrange("b (t p) d -> p (b t) d", p=P)).then_inc(ld_k, 16)
            sp_.wait_ge(f_mm, 2 * KF * NCH)
            sp_.dma_start(keysT[:], a["ctxT"].rearrange("(k p) n -> p k n", p=P)).then_inc(ld_kT, 16)
            sp_.wait_ge(f_o1, NCH)
            sp_.dma_start(qw.rearrange("p k (e h) -> p k e h", e=EA)[:, 0], a["L1_ffn_q_w"][:, 0:P, :].rearrange("e p h -> p e h")).then_inc(ld_q, 16)
            sp_.dma_start(qw.rearrange("p k (e h) -> p k e h", e=EA)[:, 1], a["L1_ffn_q_w"][:, P:D, :].rearrange("e p h -> p e h")).then_inc(ld_q, 16)
            sp_.dma_start(ow, a["L1_ffn_o_w"].rearrange("e h d -> h e d")).then_inc(ld_q, 16)
            for k in range(KD):
                sp_.dma_start(w1[:, k, :].rearrange("p (e f) -> p e f", e=EF),
                              a["L1_ffn_ff_w1"][:, k * P:(k + 1) * P, :].rearrange("e p f -> p e f")).then_inc(ld_e, 16)
            sp_.dma_start(w2, a["L1_ffn_ff_w2"].rearrange("e f d -> f e d")).then_inc(ld_e, 16)
            sp_.wait_ge(z_set, 1)
            for jt in range(4):
                lo = (1 - jt % 2) * RELW
                sp_.dma_start(skew[jt, :, lo:lo + RELW - jt % 2], zrow[:, 0:RELW - jt % 2]).then_inc(z_dma, 16)
            sp_.wait_ge(z_dma, 64)

            def skew_batch(b, first):
                for t in range(2):
                    lo = t * (RELW - 1)
                    hold(sp_, m_r, 2 * b + t + 1)
                    if not first and t == 0:
                        hold(sp_, m_rin, 16 * b)
                    sp_.dma_start(skew.rearrange("(j t) q c -> t q j c", t=2)[t, :, :, lo:lo + RELW], R[:, t])\
                        .then_inc(m_rout, 16)
                hold(sp_, m_rout, 32 * b + 32)
                if not first:
                    hold(sp_, m_max, 4 * b)
                sp_.dma_start(B.rearrange("p j t s -> p (j t) s"),
                              bass.AP(tensor=skew.tensor, offset=skew.offset + P - 1,
                                      ap=[[RELROW - 1, P], [P * RELROW, 4], [1, S]])).then_inc(m_rin, 16)

            skew_batch(0, True)
            with sp_.Fori(1, NB) as b:
                skew_batch(b, False)

            with sp_.Fori(0, NB) as b:
                hold(sp_, n_GT, b + 1)
                sp_.dma_start(gscr[:, bass.ds(S * b, S)], GTa[:, bass.ds(S * b, S)]).then_inc(g_out, 16)
            sp_.wait_ge(g_out, 16 * NB)
            def gates_in(j, first):
                for n in range(4):
                    if not first:
                        hold(sp_, e_hg, EF * j - EF + 4 * n + 4)
                    sp_.dma_start(gbc[n], gscr[4 * n:4 * n + 4, bass.ds(CH * j, CH)].partition_broadcast(P))\
                        .then_inc(g_in[n], 16)
            gates_in(0, True)
            with sp_.Fori(1, NCH) as j:
                gates_in(j, False)
            with sp_.Fori(0, NCH) as j:
                hold(sp_, e_x4, 2 * j + 2)
                sp_.dma_start(out_tok[:, bass.ds(4 * j, 4), :], x[:, bass.ds(4 * j, 4), :]).then_inc(stored, 16)
            sp_.wait_ge(stored, 16 * NCH)

        @block.gpsimd
        def _(pool):
            nc.gpsimd.memset(ident[:], 0.0).then_inc(ident_zero, 1)
            nc.gpsimd.memset(neghalf[:], -0.5).then_inc(ident_zero, 1)
            nc.gpsimd.memset(magic[:], MAGIC).then_inc(ident_zero, 1)
            nc.gpsimd.memset(ones1[:], 1.0).then_inc(ident_zero, 1)
            nc.gpsimd.memset(zero[:], 0.0).then_inc(ident_zero, 1)
            nc.gpsimd.memset(sel8[:], 0.0).then_inc(ident_zero, 1)
            nc.gpsimd.iota(iota[:], [[1, EF]], base=0, channel_multiplier=0, allow_small_or_imprecise_dtypes=True)\
                .then_inc(ident_zero, 1)
            pool.wait_ge(ident_zero, 7)
            nc.gpsimd.affine_select(out=sel8[:], in_=sel8[:], compare_op=ALU.not_equal, fill=1.0, base=0,
                                    pattern=[[1, EA], [0, P]], channel_multiplier=-1).then_inc(selz, 1)
            pool.wait_ge(selz, 1)
            nc.gpsimd.affine_select(out=ident[:], in_=ident[:], compare_op=ALU.not_equal, fill=1.0, base=0,
                                    pattern=[[-1, P]], channel_multiplier=1).then_inc(const_ready, 1)

            def ln_pow(b, u, var, rstd):
                pool.wait_ge(var, b + 1)
                nc.gpsimd.tensor_tensor(rs[:, u, :], ve[:, u, :], neghalf[:], ALU.pow).then_inc(rstd, 1)

            pool.wait_ge(const_ready, 1)
            ln_pow(0, 0, a_var, a_rstd)
            pool.wait_ge(wstep, 3)
            wv = wnat.rearrange("p g (c k) -> p (g c) k", k=BLK)
            nc.gpsimd.tensor_tensor(wv, wv, winv[:].unsqueeze(2).to_broadcast([P, 144, BLK]),
                                    ALU.mult).then_inc(wscaled, 1)
            ln_pow(1, 1, a_var, a_rstd)
            with pool.Fori(1, NB // 2) as i:
                for u in range(2):
                    ln_pow(2 * i + u, u, a_var, a_rstd)
            pool.wait_ge(wround, 1)
            nc.gpsimd.tensor_tensor(wv, wv, wabs[:].unsqueeze(2).to_broadcast([P, 144, BLK]),
                                    ALU.mult).then_inc(wdq, 1)
            with pool.Fori(0, NB // 2) as i:
                for u in range(2):
                    ln_pow(2 * i + u, u, f_var, f_rstd)
            for k in range(4):
                w = 2 if k == 1 else 1
                pool.wait_ge(f_pmax, k + 1)
                nc.gpsimd.partition_all_reduce(gmx[:, 0:w], pmax[:, 0:w], P, RMAX).then_inc(f_gmax, 1)

            with pool.Fori(0, NB // 2) as i:
                for u in range(2):
                    ln_pow(2 * i + u, u, c_var, c_rstd)
            pool.wait_ge(c_x3, NB)
            nc.gpsimd.memset(zrow, 0.0).then_inc(z_set, 1)

            def affine(b, u, n, ln_done, w_done, xn_done):
                pool.wait_ge(ln_done, 2 * b + 2)
                nc.gpsimd.tensor_tensor(xn[:, u], xn[:, u], ln[:, n, :].unsqueeze(1).to_broadcast([P, 2, D]), ALU.mult)\
                    .then_inc(w_done, 1)
                pool.wait_ge(w_done, b + 1)
                nc.gpsimd.tensor_tensor(xn[:, u], xn[:, u], ln[:, n + 1, :].unsqueeze(1).to_broadcast([P, 2, D]), ALU.add)\
                    .then_inc(xn_done, 1)

            with pool.Fori(0, NB // 2) as i:
                for u in range(2):
                    b = 2 * i + u
                    ln_pow(b, u, m_var, m_rstd)
                    ln_pow(b, u, m_var2, m_rstd2)
                    affine(b, u, 0, m_ln, m_w, m_xn)
            with pool.Fori(0, NB // 2) as i:
                for u in range(2):
                    b = 2 * i + u
                    ln_pow(b, u, n_var, n_rstd)
                    affine(b, u, 2, n_ln, n_w, n_xn)
                    pool.wait_ge(n_xnT, b + 1)
                    nc.gpsimd.tensor_copy(xmT[:, :, bass.ds(S * b, S)], xnT[:, u]).then_inc(n_all, 1)

        @block.vector
        def _(dve):
            def ln_stats(src, b, u, chain, var):
                link = chained(dve, chain, b * 2)
                nc.vector.bn_stats(st[:, 0, :], src[0])
                link(nc.vector.bn_stats(st[:, 1, :], src[1]))
                nc.vector.bn_aggr(mv[:, u, 0, :], st[:, 0, :])
                link(nc.vector.bn_aggr(mv[:, u, 1, :], st[:, 1, :]))
                nc.vector.tensor_scalar(ve[:, u, :], mv[:, u, :, 1], EPS, None, ALU.add).then_inc(var, 1)

            def ln_norm(dst, src, b, u, rstd, done):
                dve.wait_ge(rstd, b + 1)
                for t in range(2):
                    nc.vector.tensor_scalar(dst[t], src[t], mv[:, u, t, 0:1], rs[:, u, t:t + 1],
                                            ALU.subtract, ALU.mult).then_inc(done, 1)

            def tiles(buf, b):
                return [buf[:, 2 * b + t, :] for t in range(2)]

            def a_norm(b, u):
                ln_stats(tiles(x, b), b, u, a_st, a_var)
                ln_norm([xn[:, u, t, :] for t in range(2)], tiles(x, b), b, u, a_rstd, a_xn)

            def a_fin(b, u):
                dve.wait_ge(a_mm, b + 1)
                xb = x[:, bass.ds(2 * b, 2), :]
                nc.vector.scalar_tensor_tensor(xb, bank2(2 + u), tg[:, 0:1], xb, ALU.mult, ALU.add).then_inc(a_x1, 1)

            dve.wait_ge(ld_x, 64)
            a_norm(0, 0)
            dve.wait_ge(ld_wq, 48)
            wv = wnat.rearrange("p g (c k) -> p (g c) k", k=BLK)
            nc.vector.tensor_reduce(wabs[:], wv, AX.X, ALU.max, apply_absolute_value=True).then_inc(wstep, 1)
            dve.wait_ge(wstep, 1)
            nc.vector.tensor_scalar(wabs[:], wabs[:], 1.0 / 7.0, 1e-12, ALU.mult, ALU.max).then_inc(wstep, 1)
            dve.wait_ge(wstep, 2)
            nc.vector.reciprocal(winv[:], wabs[:]).then_inc(wstep, 1)
            dve.wait_ge(ld_ctxT, 16)
            nc.vector.tensor_reduce(csum[:], ctxT.rearrange("p k (b s) -> p k b s", b=NB), AX.X, ALU.add)\
                .then_inc(csum_ready, 1)
            dve.wait_ge(rb_mm, 1)
            dve.wait_ge(ld_w0, 32)
            nc.vector.scalar_tensor_tensor(rb, ps[0:1, 4:8, :].rearrange("p a (c e) -> p (a c) e", c=2), 1.0 / S,
                                           b0.unsqueeze(1).to_broadcast([1, NB, D]), ALU.mult, ALU.add)\
                .then_inc(rb_ready, 1)
            dve.wait_ge(tanh_ready, 1)
            with dve.Fori(0, NB // 2 - 1) as i:
                for u in range(2):
                    a_norm(2 * i + u + 1, 1 - u)
                    a_fin(2 * i + u, u)
            a_norm(NB - 1, 1)
            a_fin(NB - 2, 0)
            a_fin(NB - 1, 1)
            dve.wait_ge(wscaled, 1)
            nc.vector.tensor_scalar(wnat, wnat, MAGIC, -MAGIC, ALU.add, ALU.add).then_inc(dve0, 1)
            dve.wait_ge(dve0, 1)
            nc.vector.tensor_scalar(wnat, wnat, 7.0, -8.0, ALU.min, ALU.max).then_inc(wround, 1)

            def f_norm(b, u):
                ln_stats(tiles(x, b), b, u, f_st, f_var)
                ln_norm(tiles(lnb, b), tiles(x, b), b, u, f_rstd, f_ln)

            def f_absmax(b):
                hold(dve, f_ln, 2 * b + 2)
                nc.vector.tensor_reduce(amx[:, bass.ds(b, 1)], lnb[:, bass.ds(2 * b, 2), :], AX.XY, ALU.max,
                                        apply_absolute_value=True).then_inc(f_red, 1)

            dve.wait_ge(a_x1, NB)
            f_norm(0, 0)
            with dve.Fori(0, NB // 2 - 1) as i:
                for u in range(2):
                    f_norm(2 * i + u + 1, 1 - u)
                    f_absmax(2 * i + u)
            f_norm(NB - 1, 1)
            f_absmax(NB - 2)
            f_absmax(NB - 1)

            def quant_scale(k, w, srcs, reds, scale, inv):
                dve.wait_ge(f_red, reds)
                for n, s_ in enumerate(srcs):
                    ins = nc.vector.tensor_reduce(pmax[:, n:n + 1], s_, AX.X, ALU.max)
                ins.then_inc(f_pmax, 1)
                dve.wait_ge(f_gmax, k + 1)
                nc.vector.tensor_scalar(scale, gmx[:, 0:w], 1.0 / QMAX, 1e-12, ALU.mult, ALU.max).then_inc(dve0, 1)
                dve.wait_ge(dve0, 2 + k)
                nc.vector.reciprocal(inv, scale).then_inc(f_scale, 1)
                dve.wait_ge(f_scale, k + 1)

            quant_scale(0, 1, [amx[:, 0:NB]], NB, sx[:, 0:1], sx[:, 1:2])
            def x_quant(b, u, first):
                xb = lnb[:, bass.ds(2 * b, 2), :]
                nc.vector.tensor_scalar(xb, xb, sx[:, 1:2], MAGIC, ALU.mult, ALU.add).then_inc(f_q1, 1)
                hold(dve, f_q1, b + 1)
                if not first:
                    hold(dve, f_turned, b - 1)
                nc.vector.tensor_scalar(xn[:, u], xb, -MAGIC, None, ALU.add).then_inc(f_xq, 1)

            x_quant(0, 0, True)
            x_quant(1, 1, True)
            with dve.Fori(1, NB // 2) as i:
                for u in range(2):
                    x_quant(2 * i + u, u, False)
            dve.wait_ge(ld_k, 16)
            for n in range(4):
                part = kvals[:, 4 * n:4 * n + 4, :]
                if n:
                    hold(dve, v_ready, n)
                nc.vector.tensor_scalar(infm, part, -3.4028234663852886e38, None, ALU.is_lt).then_inc(v_inf, 1)
                hold(dve, v_inf, n + 1)
                nc.vector.copy_predicated(part, infm, zero[:].unsqueeze(2).to_broadcast([P, 4, D])).then_inc(v_ready, 1)
            dve.wait_ge(ld_m, 16 * 16)
            for t in range(2):
                nc.vector.tensor_scalar(relx[:, t, :], relx[:, t, :], rele[:, t:t + 1], None, ALU.subtract)\
                    .then_inc(rel_ready, 1)
            with dve.Fori(0, NCH) as j:
                for m in range(2 * KF):
                    hold(dve, f_ev, 2 * KF * j + m + 1)
                    src = (up if m < KF else gate)[:, m % KF, bass.ds(CH * j, CH)]
                    nc.vector.tensor_reduce(amx[:, bass.ds(m * NCH + j, 1)], src, AX.X, ALU.max,
                                            apply_absolute_value=True).then_inc(f_red, 1)
            R1 = NB + NCH * 2 * KF
            quant_scale(1, 2, [amx[:, 0:KF * NCH], amx[:, KF * NCH:2 * KF * NCH]], R1, sug[:, 0, :], sug[:, 1, :])

            def g_dequant(m):
                hold(dve, f_g1, m + 1)
                g = gate[:, m, :]
                nc.vector.tensor_scalar(g, g, -MAGIC, sug[:, 0, 1:2], ALU.add, ALU.mult).then_inc(f_g2, 1)

            def g_prod(m, u):
                hold(dve, f_s1, m + 1)
                nc.vector.tensor_scalar(sig[:, u, :], sig[:, u, :], -MAGIC, 65535.0, ALU.add, ALU.min).then_inc(f_s2, 1)
                hold(dve, f_s2, m + 1)
                g = gate[:, m, :]
                nc.vector.scalar_tensor_tensor(g, sig[:, u, :], 1.0 / 65536.0, g, ALU.mult, ALU.mult).then_inc(f_prod, 1)
                hold(dve, f_prod, m + 1)
                nc.vector.tensor_reduce(amx[:, bass.ds(m, 1)], g, AX.X, ALU.max,
                                        apply_absolute_value=True).then_inc(f_red, 1)

            g_dequant(0)
            with dve.Fori(0, KF // 2 - 1) as i:
                for u in range(2):
                    g_dequant(2 * i + u + 1)
                    g_prod(2 * i + u, u)
            g_dequant(KF - 1)
            g_prod(KF - 2, 0)
            g_prod(KF - 1, 1)
            quant_scale(2, 1, [amx[:, 0:KF]], R1 + KF, sp[:, 0:1], sp[:, 1:2])

            with dve.Fori(0, KF) as m:
                g = gate[:, m, :]
                v = up[:, m, :]
                hold(dve, f_p1, 2 * m + 2)
                nc.vector.tensor_scalar(g, g, -MAGIC, None, ALU.add).then_inc(f_p2, 1)
                hold(dve, f_p2, m + 1)
                nc.vector.scalar_tensor_tensor(g, v, -MAGIC, g, ALU.add, ALU.mult).then_inc(f_o, 1)
                hold(dve, f_o, m + 1)
                nc.vector.tensor_reduce(amx[:, bass.ds(m, 1)], g, AX.X, ALU.max,
                                        apply_absolute_value=True).then_inc(f_red, 1)
            dve.wait_ge(f_red, R1 + 2 * KF)
            nc.vector.tensor_tensor(so[:, 2:3], sp[:, 0:1], sug[:, 0, 0:1], ALU.mult).then_inc(dve0, 1)
            dve.wait_ge(dve0, 5)
            nc.vector.tensor_reduce(pmax[:, 0:1], amx[:, 0:KF], AX.X, ALU.max).then_inc(f_pmax, 1)
            dve.wait_ge(f_gmax, 4)
            nc.vector.tensor_scalar(so[:, 0:1], gmx[:, 0:1], so[:, 2:3], 1.0 / QMAX, ALU.mult, ALU.mult).then_inc(dve0, 1)
            dve.wait_ge(dve0, 6)
            nc.vector.tensor_scalar(so[:, 0:1], so[:, 0:1], 1e-12, None, ALU.max).then_inc(dve0, 1)
            dve.wait_ge(dve0, 7)
            nc.vector.reciprocal(so[:, 1:2], so[:, 0:1]).then_inc(dve0, 1)
            dve.wait_ge(dve0, 8)
            nc.vector.tensor_tensor(so[:, 1:2], so[:, 1:2], so[:, 2:3], ALU.mult).then_inc(f_scale, 1)

            def o_dequant(j, u):
                hold(dve, f_o1, j + 1)
                nc.vector.tensor_scalar(oq[:, u], oq[:, u], -MAGIC, so[:, 0:1], ALU.add, ALU.mult).then_inc(f_oq, 1)

            def f_fin(j, u):
                for h in range(2):
                    hold(dve, f_down, 2 * j + h + 1)
                    xb = x[:, bass.ds(4 * j + 2 * h, 2), :]
                    nc.vector.scalar_tensor_tensor(xb, bank2(2 * u + h), tg[:, 2:3], xb, ALU.mult, ALU.add)\
                        .then_inc(f_x2, 1)

            o_dequant(0, 0)
            with dve.Fori(0, NCH // 2 - 1) as i:
                for u in range(2):
                    o_dequant(2 * i + u + 1, 1 - u)
                    f_fin(2 * i + u, u)
            o_dequant(NCH - 1, 1)
            f_fin(NCH - 2, 0)
            f_fin(NCH - 1, 1)

            dve.wait_ge(f_x2, NB)

            def c_norm(b, u):
                ln_stats(tiles(x, b), b, u, c_st, c_var)
                ln_norm([xn[:, u, t, :] for t in range(2)], tiles(x, b), b, u, c_rstd, c_xn)

            def c_smax(b, u):
                hold(dve, c_smm, b + 1)
                for t in range(2):
                    nc.vector.tensor_scalar(px[:, u, t, :], bank2(3)[:, t, :], float("-inf"), None, ALU.max, ALU.max,
                                            accum_out=cmx[:, u, t:t + 1]).then_inc(c_max, 1)
                hold(dve, c_max, 2 * b + 2)
                nc.vector.tensor_scalar(cnm[:, u, :], cmx[:, u, :], -1.0, None, ALU.mult).then_inc(c_nmax, 1)

            def c_fin(b, u):
                link = chained(dve, c_rz, 2 * b)
                hold(dve, c_exp, 2 * b + 2)
                link(nc.vector.reciprocal(crz[:, u, :], cz[:, u, :]))
                link(nc.vector.tensor_scalar(crz[:, u, :], crz[:, u, :], tg[:, 1:2], None, ALU.mult))
                hold(dve, c_pv, b + 1)
                for t in range(2):
                    xt = x[:, 2 * b + t, :]
                    ins = nc.vector.scalar_tensor_tensor(xt, bank2(5 + u)[:, t, :], crz[:, u, t:t + 1], xt, ALU.mult, ALU.add)
                ins.then_inc(c_x3, 1)

            c_norm(0, 0)
            c_norm(1, 1)
            c_smax(0, 0)
            with dve.Fori(0, NB // 2 - 1) as i:
                for u in range(2):
                    b = 2 * i + u
                    c_norm(b + 2, u)
                    c_smax(b + 1, 1 - u)
                    c_fin(b, u)
            c_smax(NB - 1, 1)
            c_fin(NB - 2, 0)
            c_fin(NB - 1, 1)

            def m_norm(b, u):
                ln_stats(tiles(x, b), b, u, m_st, m_var)
                ln_norm(tiles(inner, b), tiles(x, b), b, u, m_rstd, m_src)
                hold(dve, m_src, 2 * b + 2)
                ln_stats(tiles(inner, b), b, u, m_st2, m_var2)
                ln_norm([xn[:, u, t, :] for t in range(2)], tiles(inner, b), b, u, m_rstd2, m_ln)

            def gating(b, u, ne, log, chain, d, e_, gate_done):
                hold(dve, log, b + 1)
                link = chained(dve, chain, 6 * b)
                lg = [ps[:, 0, ne * t:ne * t + ne] for t in range(2)]
                nc.vector.max(top[:, 0, :], lg[0])
                link(nc.vector.max(top[:, 1, :], lg[1]))
                nc.vector.tensor_tensor(td[:], top[:, :, 1], top[:, :, 0], ALU.subtract).then_inc(d, 1)
                nc.vector.max_index(tidx[:, 0, :], top[:, 0, :], lg[0])
                link(nc.vector.max_index(tidx[:, 1, :], top[:, 1, :], lg[1]))
                link(nc.vector.tensor_copy(tif[:], tidx[:, :, 0:2]))
                nc.vector.tensor_tensor(hot[:, u, :, :, 0:ne].rearrange("p t j e -> p (t j) e"),
                                        iota[:, 0:ne].unsqueeze(1).to_broadcast([P, 4, ne]),
                                        tif[:].rearrange("p t j -> p (t j)").unsqueeze(2).to_broadcast([P, 4, ne]),
                                        ALU.is_equal)
                hold(dve, e_, b + 1)
                link(nc.vector.tensor_scalar(td[:], te[:], 1.0, None, ALU.add))
                link(nc.vector.reciprocal(gj[:, u, :, 0], td[:]))
                nc.vector.tensor_tensor(gj[:, u, :, 1], gj[:, u, :, 0], te[:], ALU.mult)\
                    .then_inc(chain, 1)
                hold(dve, chain, 6 * b + 6)
                nc.vector.tensor_tensor(ghot[:, u, :, :, 0:ne].rearrange("p t j e -> p (t j) e"),
                                        hot[:, u, :, :, 0:ne].rearrange("p t j e -> p (t j) e"),
                                        gj[:, u].rearrange("p t j -> p (t j)").unsqueeze(2).to_broadcast([P, 4, ne]),
                                        ALU.mult).then_inc(gate_done, 1)
                hold(dve, gate_done, 2 * b + 1)
                nc.vector.tensor_tensor(G[:, u, :, 0:ne], ghot[:, u, :, 0, 0:ne], ghot[:, u, :, 1, 0:ne], ALU.add)\
                    .then_inc(gate_done, 1)

            def m_softmax(b):
                hold(dve, m_rin, 16 * b + 16)
                hold(dve, m_smm, b + 1)
                for j in range(2):
                    for t in range(2):
                        n = 2 * j + t
                        nc.vector.tensor_tensor_reduce(pm[:, j, t, :], bank2(6 + j)[:, t, :], B[:, j, t, :], 1.0, -3.0e38,
                                                       ALU.add, ALU.max, mmx[:, n:n + 1]).then_inc(m_max, 1)
                hold(dve, m_max, 4 * b + 4)
                nc.vector.tensor_scalar(mnm[:], mmx[:], -float(HD) ** -0.5, None, ALU.mult).then_inc(m_nmax, 1)

            def m_value(b, u):
                hold(dve, m_vmm, b + 1)
                nc.vector.tensor_tensor(val[:, u], ps[:, 1, 0:2 * HD].rearrange("p (k h) -> p k h", k=2),
                                        vb[:].unsqueeze(1).to_broadcast([P, 2, HD]), ALU.add).then_inc(m_v, 1)

            def m_scale(b, u):
                hold(dve, m_exp, 4 * b + 4)
                link = chained(dve, m_rz, 2 * b)
                link(nc.vector.reciprocal(mrz[:], mz[:]))
                link(nc.vector.tensor_tensor(mrz[:].rearrange("p (j t) -> p j t", j=2), mrz[:].rearrange("p (j t) -> p j t", j=2),
                                             gj[:, u].rearrange("p t j -> p j t"), ALU.mult))
                for n in range(4):
                    nc.vector.tensor_scalar(pm[:, n // 2, n % 2, :], pm[:, n // 2, n % 2, :], mrz[:, n:n + 1], None, ALU.mult)\
                        .then_inc(m_p, 1)

            def m_select(b, u):
                for e in range(EA):
                    hold(dve, m_qmm, 5 * b + e // 2 + 1)
                    data = bank2(2 + e // 2 % 2)[:, e % 2, :].unsqueeze(1).to_broadcast([P, 2, S])
                    if e == 0:
                        ins = nc.vector.tensor_copy(qsel, data)
                    else:
                        hold(dve, m_mask, 8 * b + e + 1)
                        hold(dve, m_qsel, 8 * b + e)
                        ins = nc.vector.copy_predicated(qsel, mask[:, u, e].bitcast(U16), data)
                    ins.then_inc(m_qsel, 1)
                hold(dve, m_qsel, 8 * b + 8)
                hold(dve, m_qmm, 5 * b + 5)
                nc.vector.tensor_tensor(qT, qsel, bank2(2), ALU.add).then_inc(m_qT, 1)

            def m_spread(b, u):
                hold(dve, m_pv, b + 1)
                c = ps[:, 1, :].rearrange("p (j s) -> p j s", j=2)
                nc.vector.tensor_tensor(ctxE, mask[:, u, :, 0, :], c[:, 0, :].unsqueeze(1).to_broadcast([P, EA, S]), ALU.mult)\
                    .then_inc(m_cE, 1)
                hold(dve, m_cE, 2 * b + 1)
                nc.vector.copy_predicated(ctxE, mask[:, u, :, 1, :].bitcast(U16), c[:, 1, :].unsqueeze(1).to_broadcast([P, EA, S]))\
                    .then_inc(m_cE, 1)

            def m_add(b):
                hold(dve, m_omm, b + 1)
                sb_ = inner[:, bass.ds(2 * b, 2), :]
                nc.vector.tensor_tensor(sb_, sb_, bank2(3), ALU.add).then_inc(m_out, 1)

            def m_gating(b, u):
                gating(b, u, EA, m_log, m_top, m_d, m_e, m_gate)

            m_norm(0, 0)
            m_norm(1, 1)
            m_gating(0, 0)
            m_value(0, 0)
            m_select(0, 0)
            m_gating(1, 1)

            def m_step(b, u, more):
                m_softmax(b)
                m_value(b + 1, 1 - u)
                m_scale(b, u)
                if more:
                    m_norm(b + 2, u)
                m_select(b + 1, 1 - u)
                m_spread(b, u)
                if more:
                    m_gating(b + 2, u)
                m_add(b)

            with dve.Fori(0, NB // 2 - 1) as i:
                for u in range(2):
                    m_step(2 * i + u, u, True)
            m_step(NB - 2, 0, False)
            m_softmax(NB - 1)
            m_scale(NB - 1, 1)
            m_spread(NB - 1, 1)
            m_add(NB - 1)

            def n_norm(b, u):
                ln_stats(tiles(inner, b), b, u, n_st, n_var)
                ln_norm([xn[:, u, t, :] for t in range(2)], tiles(inner, b), b, u, n_rstd, n_ln)

            def n_gating(b, u):
                gating(b, u, EF, n_log, n_top, n_d, n_e, n_gate)
                xb = x[:, bass.ds(2 * b, 2), :]
                nc.vector.scalar_tensor_tensor(xb, inner[:, bass.ds(2 * b, 2), :], tg[:, 3:4], xb, ALU.mult, ALU.add)\
                    .then_inc(n_base, 1)

            dve.wait_ge(m_out, NB)
            n_norm(0, 0)
            with dve.Fori(0, NB // 2 - 1) as i:
                for u in range(2):
                    n_norm(2 * i + u + 1, 1 - u)
                    n_gating(2 * i + u, u)
            n_norm(NB - 1, 1)
            n_gating(NB - 2, 0)
            n_gating(NB - 1, 1)

            def e_gate(j, e):
                if e % 4 == 0:
                    hold(dve, g_in[e // 4], 16 * j + 16)
                n = EF * j + e
                if e >= 2:
                    hold(dve, e_h, n - 1)
                hold(dve, e_hmm, n + 1)
                nc.vector.scalar_tensor_tensor(hg[:, e % 2, :], bank(e % 3), b1[:, e:e + 1], gbc[e // 4][:, e % 4, :],
                                               ALU.add, ALU.mult).then_inc(e_hg, 1)

            dve.wait_ge(n_base, NB)
            with dve.Fori(0, NCH) as j:
                for e in range(EF):
                    e_gate(j, e)
                for h in range(2):
                    hold(dve, e_yturn, 2 * j + h + 1)
                    xb = x[:, bass.ds(4 * j + 2 * h, 2), :]
                    nc.vector.scalar_tensor_tensor(xb, bank2(6 + h), tg[:, 3:4], xb, ALU.mult, ALU.add).then_inc(e_x4, 1)

        @block.scalar
        def _(act):
            act.wait_ge(ld_g, 32)
            nc.scalar.activation(tg[:], gates[:], ACT.Tanh).then_inc(tanh_ready, 1)

            def a_evac(b, u):
                hold(act, a_turned, b + 1)
                nc.scalar.copy(xnT[:, u].rearrange("p k s -> p (k s)"), bank(u)).then_inc(a_xnT, 1)

            with act.Fori(0, NB // 2) as i:
                for u in range(2):
                    a_evac(2 * i + u, u)
            for n in range(9):
                act.wait_ge(w_turned, n + 1)
                if n < 6:
                    w, h, k = n // 3 % 2, n % 3, 0
                    dst = wT[:, n // 3, :, 256 * h:256 * h + 256]
                    src = bank2(4 + n % 4)
                else:
                    dst = wdT[:, 2 * (n - 6):2 * (n - 6) + 2, :]
                    src = bank2(4 + n % 4)
                nc.scalar.copy(dst, src).then_inc(w_ready, 1)

            act.wait_ge(f_scale, 1)
            with act.Fori(0, NB // 2) as i:
                for u in range(2):
                    b = 2 * i + u
                    hold(act, f_turned, b + 1)
                    nc.scalar.activation(xqT[:, :, bass.ds(S * b, S)], bank2(u), ACT.Copy, scale=sx[:, 0:1])\
                        .then_inc(f_xqT, 1)
            with act.Fori(0, NCH) as j:
                for m in range(2 * KF):
                    hold(act, f_mm, 2 * KF * j + m + 1)
                    dst = (up if m < KF else gate)[:, m % KF, bass.ds(CH * j, CH)]
                    nc.scalar.copy(dst, bank(2 + m % UP_BANKS)).then_inc(f_ev, 1)

            def g_round(m):
                g = gate[:, m, :]
                nc.scalar.activation(g, g, ACT.Identity, scale=sug[:, 1, 1:2], bias=magic[:]).then_inc(f_g1, 1)

            def g_sigmoid(m, u):
                hold(act, f_g2, m + 1)
                nc.scalar.activation(sig[:, u, :], gate[:, m, :], ACT.Sigmoid).then_inc(f_sig, 1)
                hold(act, f_sig, m + 1)
                nc.scalar.activation(sig[:, u, :], sig[:, u, :], ACT.Identity, scale=65536.0, bias=magic[:])\
                    .then_inc(f_s1, 1)

            act.wait_ge(f_scale, 2)
            act.wait_ge(const_ready, 1)
            g_round(0)
            with act.Fori(0, KF // 2 - 1) as i:
                for u in range(2):
                    g_round(2 * i + u + 1)
                    g_sigmoid(2 * i + u, u)
            g_round(KF - 1)
            g_sigmoid(KF - 2, 0)
            g_sigmoid(KF - 1, 1)
            act.wait_ge(f_scale, 3)
            with act.Fori(0, KF) as m:
                g = gate[:, m, :]
                v = up[:, m, :]
                nc.scalar.activation(g, g, ACT.Identity, scale=sp[:, 1:2], bias=magic[:]).then_inc(f_p1, 1)
                nc.scalar.activation(v, v, ACT.Identity, scale=sug[:, 1, 0:1], bias=magic[:]).then_inc(f_p1, 1)
            act.wait_ge(f_scale, 4)

            def o_round(j, u):
                nc.scalar.activation(oq[:, u], gate[:, :, bass.ds(CH * j, CH)], ACT.Identity, scale=so[:, 1:2],
                                     bias=magic[:]).then_inc(f_o1, 1)

            for j in range(2):
                o_round(j, j)
            with act.Fori(1, NCH // 2) as i:
                for u in range(2):
                    j = 2 * i + u
                    hold(act, f_down, 2 * j - 2)
                    o_round(j, u)

            act.wait_ge(ld_c, 32)

            def c_turned_out(b, u):
                hold(act, c_turned, b + 1)
                nc.scalar.copy(xnT[:, u].rearrange("p k s -> p (k s)"), bank(u)).then_inc(c_xnT, 1)

            def c_query(b, u):
                hold(act, c_qmm, b + 1)
                for k in range(KD):
                    nc.scalar.activation(qx[:, u, k, :], bank2(2)[:, k, :], ACT.Identity, bias=b1x[:, k:k + 1]).then_inc(c_q, 1)

            def c_exps(b, u):
                hold(act, c_nmax, b + 1)
                for t in range(2):
                    nc.scalar.activation(px[:, u, t, :], px[:, u, t, :], ACT.Exp, bias=cnm[:, u, t:t + 1],
                                         accum_out=cz[:, u, t:t + 1]).then_inc(c_exp, 1)

            def c_weights(b, u):
                hold(act, c_pturn, b + 1)
                nc.scalar.copy(pxT[:, u].rearrange("p k s -> p (k s)"), bank(4)).then_inc(c_pT, 1)

            c_turned_out(0, 0)
            c_turned_out(1, 1)
            c_query(0, 0)
            c_exps(0, 0)
            with act.Fori(0, NB // 2 - 1) as i:
                for u in range(2):
                    b = 2 * i + u
                    c_query(b + 1, 1 - u)
                    c_weights(b, u)
                    c_exps(b + 1, 1 - u)
                    c_turned_out(b + 2, u)
            c_query(NB - 1, 1)
            c_weights(NB - 2, 0)
            c_exps(NB - 1, 1)
            c_weights(NB - 1, 1)

            def m_turned_out(b, u):
                hold(act, m_turned, b + 1)
                nc.scalar.copy(xnT[:, u].rearrange("p k s -> p (k s)"), bank(0)).then_inc(m_xnT, 1)

            def m_gexp(b):
                hold(act, m_d, b + 1)
                nc.scalar.activation(te[:], td[:], ACT.Exp).then_inc(m_e, 1)

            def m_hots(b, u):
                hold(act, m_hturn, b + 1)
                nc.scalar.copy(hotT, ps[0:EA, 0, :]).then_inc(m_hT, 1)
                nc.scalar.copy(hotTb, ps[0:EA, 0, :]).then_inc(m_hT, 1)
                nc.scalar.copy(GT[:, u, :], ps[0:EA, 1, 0:S]).then_inc(m_hT, 1)

            def m_masks(b, u):
                for e in range(EA):
                    hold(act, m_maskmm, 8 * b + e + 1)
                    nc.scalar.copy(mask[:, u, e], bank2(2 + e % 2)).then_inc(m_mask, 1)

            def m_key(b):
                hold(act, m_kmm, b + 1)
                nc.scalar.activation(kT, ps[:, 0, 0:S], ACT.Identity, bias=kb[:]).then_inc(m_k, 1)

            def m_exps(b):
                hold(act, m_nmax, b + 1)
                for n in range(4):
                    p_ = pm[:, n // 2, n % 2, :]
                    nc.scalar.activation(p_, p_, ACT.Exp, scale=float(HD) ** -0.5, bias=mnm[:, n:n + 1],
                                         accum_out=mz[:, n:n + 1]).then_inc(m_exp, 1)

            def m_weights(b):
                hold(act, m_pturn, b + 1)
                for k in range(2):
                    nc.scalar.copy(pmT[:, k, :], bank(4 + k)).then_inc(m_pT, 1)

            def m_band(b, first):
                hold(act, m_rmm, b + 1)
                if not first:
                    hold(act, m_rout, 32 * b)
                for t in range(2):
                    nc.scalar.copy(R[:, t], ps[:, 4 + t, 0:2 * RELW].rearrange("p (j c) -> p j c", j=2)).then_inc(m_r, 1)

            act.wait_ge(ld_m, 16 * 16)
            m_turned_out(0, 0)
            m_gexp(0)
            m_hots(0, 0)
            m_masks(0, 0)
            m_key(0)
            m_turned_out(1, 1)
            m_band(0, True)
            m_gexp(1)

            def m_step(b, u, more):
                m_hots(b + 1, 1 - u)
                m_masks(b + 1, 1 - u)
                m_key(b + 1)
                m_exps(b)
                m_weights(b)
                if more:
                    m_turned_out(b + 2, u)
                m_band(b + 1, False)
                if more:
                    m_gexp(b + 2)

            with act.Fori(0, NB // 2 - 1) as i:
                for u in range(2):
                    m_step(2 * i + u, u, True)
            m_step(NB - 2, 0, False)
            m_exps(NB - 1)
            m_weights(NB - 1)

            def n_turned_out(b, u, first):
                hold(act, n_turned, b + 1)
                if not first:
                    hold(act, n_all, b - 1)
                nc.scalar.copy(xnT[:, u].rearrange("p k s -> p (k s)"), bank(6 + u)).then_inc(n_xnT, 1)

            def n_gates(b, u):
                hold(act, n_d, b + 1)
                nc.scalar.activation(te[:], td[:], ACT.Exp).then_inc(n_e, 1)
                hold(act, n_gturn, b + 1)
                nc.scalar.copy(GTa[:, bass.ds(S * b, S)], ps[0:EF, 4 + u, 0:S]).then_inc(n_GT, 1)

            n_turned_out(0, 0, True)
            n_turned_out(1, 1, True)
            n_gates(0, 0)
            with act.Fori(1, NB // 2) as i:
                for u in range(2):
                    b = 2 * i + u
                    n_turned_out(b, u, False)
                    n_gates(b - 1, 1 - u)
            n_gates(NB - 1, 1)

            with act.Fori(0, NCH) as j:
                for e in range(EF):
                    hold(act, e_hg, EF * j + e + 1)
                    if e >= 3:
                        hold(act, e_ymm, EF * j + e - 2)
                    nc.scalar.activation(hr[:, e % 3, :], hg[:, e % 2, :], ACT.Relu).then_inc(e_h, 1)
                hold(act, e_ymm, EF * j + EF)
                nc.scalar.copy(yT, ps[:, 4:6, :]).then_inc(e_y, 1)

        @block.tensor
        def _(pe):
            mm = nc.tensor.matmul

            def turn(dst_bank, src, done):
                for k in range(KD):
                    for t in range(2):
                        ins = nc.tensor.transpose(ps[:, dst_bank, k * S + t * P:k * S + t * P + P],
                                                  src[t][:, k * P:(k + 1) * P], ident[:])
                ins.then_inc(done, 1)

            def a_turn(b, u):
                pe.wait_ge(a_xn, 2 * b + 2)
                turn(u, [xn[:, u, t, :] for t in range(2)], a_turned)

            def a_product(b, u):
                pe.wait_ge(a_xnT, b + 1)
                for t in range(2):
                    o = ps[:, 2 + u, t * D:(t + 1) * D]
                    for k in range(KD):
                        mm(o, xnT[:, u, k, t * P:(t + 1) * P], w0[:, k, :], start=(k == 0), stop=False)
                    ins = mm(o, ones1[:], rb[:, b, :], start=False, stop=True)
                ins.then_inc(a_mm, 1)

            pe.wait_ge(const_ready, 1)
            a_turn(0, 0)
            pe.wait_ge(ld_w0, 32)
            pe.wait_ge(csum_ready, 1)
            for b in range(NB):
                for k in range(KD):
                    ins = mm(ps[0:1, 4 + b // 2, b % 2 * D:(b % 2 + 1) * D], csum[:, k, b:b + 1], w0[:, 2 + k, :],
                             start=(k == 0), stop=(k == 1))
            ins.then_inc(rb_mm, 1)
            pe.wait_ge(rb_ready, 1)
            with pe.Fori(0, NB // 2 - 1) as i:
                for u in range(2):
                    a_turn(2 * i + u + 1, 1 - u)
                    a_product(2 * i + u, u)
            a_turn(NB - 1, 1)
            a_product(NB - 2, 0)
            a_product(NB - 1, 1)
            pe.wait_ge(wdq, 1)
            for n in range(9):
                if n >= 4:
                    pe.wait_ge(w_ready, n - 3)
                for k in range(2):
                    for c in range(2):
                        if n < 6:
                            src = wnat[:, 6 * (n // 3) + 2 * (n % 3) + c, k * P:(k + 1) * P]
                        else:
                            m = 2 * (n - 6) + k
                            src = wnat[:, 12 + 3 * c + m // 2, (m % 2) * P:(m % 2 + 1) * P]
                        ins = nc.tensor.transpose(ps[:, 4 + n % 4, k * 256 + c * P:k * 256 + c * P + P], src, ident[:])
                ins.then_inc(w_turned, 1)

            def f_turn(b, u):
                pe.wait_ge(f_xq, b + 1)
                turn(u, [xn[:, u, t, :] for t in range(2)], f_turned)

            f_turn(0, 0)
            f_turn(1, 1)
            with pe.Fori(1, NB // 2) as i:
                for u in range(2):
                    b = 2 * i + u
                    pe.wait_ge(f_xqT, b - 1)
                    f_turn(b, u)

            def upgate(j, first):
                pe.wait_ge(f_xqT, 2 * j + 2)
                for m in range(2 * KF):
                    if not (first and m < UP_BANKS):
                        pe.wait_ge(f_ev, 2 * KF * j + m + 1 - UP_BANKS)
                    for k in range(KD):
                        ins = mm(bank(2 + m % UP_BANKS), wT[:, m // KF, k, m % KF * P:(m % KF + 1) * P],
                                 xqT[:, k, bass.ds(CH * j, CH)], start=(k == 0), stop=(k == KD - 1))
                    ins.then_inc(f_mm, 1)

            pe.wait_ge(w_ready, 9)
            upgate(0, True)
            with pe.Fori(1, NCH) as j:
                upgate(j, False)

            def down(j, u, first):
                pe.wait_ge(f_oq, j + 1)
                for h in range(2):
                    if not first:
                        pe.wait_ge(f_x2, 2 * j + h - 3)
                    for t in range(2):
                        for m in range(KF):
                            c = (2 * h + t) * P
                            ins = mm(ps[:, 2 * u + h, t * D:(t + 1) * D], oq[:, u, m, c:c + P], wdT[:, m, :],
                                     start=(m == 0), stop=(m == KF - 1))
                    ins.then_inc(f_down, 1)

            down(0, 0, True)
            down(1, 1, True)
            with pe.Fori(1, NCH // 2) as i:
                for u in range(2):
                    down(2 * i + u, u, False)

            def c_turn(b, u):
                pe.wait_ge(c_xn, 2 * b + 2)
                turn(u, [xn[:, u, t, :] for t in range(2)], c_turned)

            def c_qproduct(b, u):
                pe.wait_ge(c_xnT, b + 1)
                for h in range(2):
                    for k in range(KD):
                        ins = mm(bank2(2)[:, h, :], w1x[:, k, h * P:(h + 1) * P], xnT[:, u, k, :],
                                 start=(k == 0), stop=(k == 1))
                ins.then_inc(c_qmm, 1)

            def c_scores(b, u):
                pe.wait_ge(c_q, 2 * b + 2)
                for t in range(2):
                    for k in range(KD):
                        ins = mm(bank2(3)[:, t, :], qx[:, u, k, t * P:(t + 1) * P], keysT[:, k, bass.ds(S * b, S)],
                                 start=(k == 0), stop=(k == 1))
                ins.then_inc(c_smm, 1)

            def c_pturns(b, u):
                pe.wait_ge(c_exp, 2 * b + 2)
                turn(4, [px[:, u, t, :] for t in range(2)], c_pturn)

            def c_context(b, u):
                pe.wait_ge(c_pT, b + 1)
                for t in range(2):
                    for k in range(2):
                        ins = mm(bank2(5 + u)[:, t, :], pxT[:, u, k, t * P:(t + 1) * P], kvals[:, 2 * b + k, :],
                                 start=(k == 0), stop=(k == 1))
                ins.then_inc(c_pv, 1)

            c_turn(0, 0)
            c_turn(1, 1)
            pe.wait_ge(ld_c, 32)
            c_qproduct(0, 0)
            pe.wait_ge(ld_kT, 16)
            c_scores(0, 0)
            pe.wait_ge(v_ready, 4)
            with pe.Fori(0, NB // 2 - 1) as i:
                for u in range(2):
                    b = 2 * i + u
                    c_qproduct(b + 1, 1 - u)
                    c_pturns(b, u)
                    c_scores(b + 1, 1 - u)
                    c_context(b, u)
                    c_turn(b + 2, u)
            c_qproduct(NB - 1, 1)
            c_pturns(NB - 2, 0)
            c_scores(NB - 1, 1)
            c_context(NB - 2, 0)
            c_pturns(NB - 1, 1)
            c_context(NB - 1, 1)

            def logits(b, u, w, ne, log):
                for t in range(2):
                    for k in range(KD):
                        ins = mm(ps[:, 0, ne * t:ne * t + ne], xnT[:, u, k, t * P:(t + 1) * P], w[:, k, :],
                                 start=(k == 0), stop=(k == 1))
                ins.then_inc(log, 1)

            def m_input(b, u):
                pe.wait_ge(m_xn, b + 1)
                turn(0, [xn[:, u, t, :] for t in range(2)], m_turned)
                pe.wait_ge(m_xnT, b + 1)
                logits(b, u, gw, EA, m_log)

            def m_hotturn(b, u):
                pe.wait_ge(m_gate, 2 * b + 2)
                for j in range(2):
                    for t in range(2):
                        nc.tensor.transpose(ps[0:EA, 0, j * S + t * P:j * S + t * P + P], hot[:, u, t, j, 0:EA], ident[:])
                for t in range(2):
                    ins = nc.tensor.transpose(ps[0:EA, 1, t * P:t * P + P], G[:, u, t, 0:EA], ident[:])
                ins.then_inc(m_hturn, 1)

            def m_maskproduct(b, first):
                pe.wait_ge(m_hT, 3 * b + 3)
                for e in range(EA):
                    if e == 1 and not first:
                        pe.wait_ge(m_out, b - 1)
                    if e >= 2:
                        pe.wait_ge(m_mask, 8 * b + e - 1)
                    mm(bank(2 + e % 2), sel8[:, e, :], hotTb, start=True, stop=True).then_inc(m_maskmm, 1)

            def m_kv(b, u):
                for k in range(KD):
                    ins = mm(ps[:, 0, 0:S], kw[:, k, :], xnT[:, u, k, :], start=(k == 0), stop=(k == 1))
                ins.then_inc(m_kmm, 1)
                for t in range(2):
                    for k in range(KD):
                        ins = mm(ps[:, 1, t * HD:(t + 1) * HD], xnT[:, u, k, t * P:(t + 1) * P], vw[:, k, :],
                                 start=(k == 0), stop=(k == 1))
                ins.then_inc(m_vmm, 1)

            def m_queries(b, u, half):
                for e in range(4 * half, 4 * half + 4):
                    if e % 2 == 0:
                        if e < 4:
                            pe.wait_ge(m_mask, 8 * b + 7 + e // 2)
                        else:
                            pe.wait_ge(m_qsel, 8 * b + e - 2)
                    for k in range(KD):
                        ins = mm(bank2(2 + e // 2 % 2)[:, e % 2, :], qw[:, k, e * HD:(e + 1) * HD], xnT[:, u, k, :],
                                 start=(k == 0), stop=(k == 1))
                    if e % 2:
                        ins.then_inc(m_qmm, 1)
                if half:
                    pe.wait_ge(m_qsel, 8 * b + 6)
                    mm(bank(2), qb[:], hotT, start=True, stop=True).then_inc(m_qmm, 1)

            def m_bandproduct(b):
                pe.wait_ge(m_qT, b + 1)
                for t in range(2):
                    for j in range(2):
                        ins = mm(ps[:, 4 + t, j * RELW:(j + 1) * RELW], qT[:, j, t * P:(t + 1) * P], relx[:, t, :],
                                 start=True, stop=True)
                ins.then_inc(m_rmm, 1)

            def m_scores(b):
                pe.wait_ge(m_k, b + 1)
                for j in range(2):
                    for t in range(2):
                        ins = mm(bank2(6 + j)[:, t, :], qT[:, j, t * P:(t + 1) * P], kT, start=True, stop=True)
                ins.then_inc(m_smm, 1)

            def m_pturns(b):
                pe.wait_ge(m_p, 4 * b + 4)
                for k in range(2):
                    for n in range(4):
                        ins = nc.tensor.transpose(ps[:, 4 + k, n * P:(n + 1) * P], pm[:, n // 2, n % 2, k * P:(k + 1) * P],
                                                  ident[:])
                ins.then_inc(m_pturn, 1)

            def m_context(b, u):
                pe.wait_ge(m_pT, 2 * b + 2)
                for k in range(2):
                    ins = mm(bank(1), val[:, u, k, :], pmT[:, k, :], start=(k == 0), stop=(k == 1))
                ins.then_inc(m_pv, 1)

            def m_output(b, u):
                pe.wait_ge(m_cE, 2 * b + 2)
                for t in range(2):
                    for e in range(EA):
                        mm(bank2(3)[:, t, :], ctxE[:, e, t * P:(t + 1) * P], ow[:, e, :], start=(e == 0), stop=False)
                    ins = mm(bank2(3)[:, t, :], GT[:, u, t * P:(t + 1) * P], ob[:], start=False, stop=True)
                ins.then_inc(m_omm, 1)

            pe.wait_ge(ld_m, 16 * 16)
            pe.wait_ge(ld_q, 48)
            pe.wait_ge(selz, 1)
            m_input(0, 0)
            m_hotturn(0, 0)
            m_maskproduct(0, True)
            m_kv(0, 0)
            m_queries(0, 0, 0)
            m_queries(0, 0, 1)
            pe.wait_ge(m_k, 1)
            m_input(1, 1)
            m_bandproduct(0)
            m_scores(0)

            def m_step(b, u, more, first):
                m_hotturn(b + 1, 1 - u)
                m_maskproduct(b + 1, first)
                m_kv(b + 1, 1 - u)
                m_pturns(b)
                m_queries(b + 1, 1 - u, 0)
                m_context(b, u)
                m_queries(b + 1, 1 - u, 1)
                if more:
                    pe.wait_ge(m_k, b + 2)
                    m_input(b + 2, u)
                m_bandproduct(b + 1)
                m_scores(b + 1)
                m_output(b, u)

            m_step(0, 0, True, True)
            m_step(1, 1, True, False)
            with pe.Fori(1, NB // 2 - 1) as i:
                for u in range(2):
                    m_step(2 * i + u, u, True, False)
            m_step(NB - 2, 0, False, False)
            m_pturns(NB - 1)
            m_context(NB - 1, 1)
            pe.wait_ge(m_out, NB - 1)
            m_output(NB - 1, 1)

            def n_input(b, u):
                pe.wait_ge(n_xn, b + 1)
                turn(6 + u, [xn[:, u, t, :] for t in range(2)], n_turned)

            def n_logits(b, u, first):
                pe.wait_ge(n_xnT, b + 1)
                if not first:
                    pe.wait_ge(n_gate, 2 * b)
                logits(b, u, gw2, EF, n_log)

            def n_gateturn(b, u):
                pe.wait_ge(n_gate, 2 * b + 2)
                for t in range(2):
                    ins = nc.tensor.transpose(ps[0:EF, 4 + u, t * P:t * P + P], G[:, u, t, :], ident[:])
                ins.then_inc(n_gturn, 1)

            n_input(0, 0)
            n_logits(0, 0, True)
            n_input(1, 1)
            n_gateturn(0, 0)
            n_logits(1, 1, False)
            with pe.Fori(1, NB // 2) as i:
                for u in range(2):
                    b = 2 * i + u
                    n_input(b, u)
                    n_gateturn(b - 1, 1 - u)
                    n_logits(b, u, False)
            n_gateturn(NB - 1, 1)

            def e_hidden(j, e):
                n = EF * j + e
                if e >= 3:
                    pe.wait_ge(e_hg, n - 2)
                for k in range(KD):
                    ins = mm(bank(e % 3), w1[:, k, e * FH:(e + 1) * FH], xmT[:, k, bass.ds(CH * j, CH)],
                             start=(k == 0), stop=(k == 1))
                ins.then_inc(e_hmm, 1)

            def e_out(j, e):
                pe.wait_ge(e_h, EF * j + e + 1)
                for h in range(2):
                    ins = mm(bank(4 + h), w2[:, e, h * P:(h + 1) * P], hr[:, e % 3, :], start=(e == 0), stop=False,
                             skip_group_check=True)
                if e == EF - 1:
                    for h in range(2):
                        ins = mm(bank(4 + h), b2[:, h * P:(h + 1) * P], GTa[:, bass.ds(CH * j, CH)], start=False, stop=True,
                                 skip_group_check=True)
                ins.then_inc(e_ymm, 1)

            pe.wait_ge(ld_e, 48)
            pe.wait_ge(n_all, NB)
            pe.wait_ge(n_GT, NB)
            with pe.Fori(0, NCH) as j:
                e_hidden(j, 0)
                e_hidden(j, 1)
                for e in range(EF):
                    if e + 2 < EF:
                        e_hidden(j, e + 2)
                    e_out(j, e)
                pe.wait_ge(e_y, j + 1)
                for t in range(4):
                    for k in range(KD):
                        ins = nc.tensor.transpose(bank2(6 + t // 2)[:, t % 2, k * P:(k + 1) * P], yT[:, k, t * P:(t + 1) * P],
                                                  ident[:])
                    if t % 2:
                        ins.then_inc(e_yturn, 1)


def kernel(**inputs):
    import concourse.bacc as bacc
    from concourse.bass_utils import run_bass_kernel_spmd as run

    a = {k: np.asarray(v) for k, v in inputs.items()}
    a["ctxT"] = np.ascontiguousarray(a["ctx_1024"].reshape(N, D).T)
    a["L0_xattn_WT"] = np.ascontiguousarray(a["L0_xattn_W"].T)
    a["L1_xattn_WT"] = np.ascontiguousarray(a["L1_xattn_W"].T)
    a["xattn1_bT"] = np.ascontiguousarray(a["L1_xattn_b"].reshape(KD, P).T)
    a["ff_b1T"] = np.ascontiguousarray(a["L1_ffn_ff_b1"].T)
    relT = a["L1_ffn_rel_table"].T
    band = [np.clip(np.arange(RELW) - (P - 1), -MAXP, MAXP) + MAXP, np.clip(np.arange(RELW) - MAXP, -MAXP, MAXP) + MAXP]
    a["relx"] = np.ascontiguousarray(relT[:, np.stack(band)])
    a["rele"] = np.ascontiguousarray(relT[:, [2 * MAXP, 0]])
    names = ["x", "g_xattn", "g_ffn", "ctxT", "L0_xattn_WT", "L0_xattn_b", "L0_ffn_w_up", "L0_ffn_w_gate",
             "L0_ffn_w_down", "L1_xattn_WT", "xattn1_bT", "ctx_1024", "ff_b1T", "relx", "rele"]
    names += ["L1_ffn_" + n for n in ("ln1_w", "ln1_b", "ln2_w", "ln2_b", "attn_gate_w", "q_w", "q_b", "k_w", "k_b", "v_w",
                                      "v_b", "o_w", "o_b", "ff_gate_w", "ff_w1", "ff_w2", "ff_b2")]
    nc = bacc.Bacc("TRN2", target_bir_lowering=False, num_devices=1)
    arrays, args = {}, {}
    for name in names:
        v = np.ascontiguousarray(a[name])
        arrays[f"in_{name}"] = v
        args[name] = nc.dram_tensor(f"in_{name}", v.shape, mybir.dt.from_np(v.dtype), kind="ExternalInput").ap()
    args["skew"] = nc.dram_tensor("skew", (4, P, RELROW), F32, kind="Internal").ap()
    args["gscr"] = nc.dram_tensor("gscr", (EF, N), F32, kind="Internal").ap()
    out = nc.dram_tensor("out", (NB, S, D), F32, kind="ExternalOutput").ap()
    gated_block_kernel(nc, args, out)
    r = run(nc, [arrays], core_ids=[0])
    return r.results[0]["out"]
```

```python
from contextlib import ExitStack

import numpy as np

import concourse.bass as bass
from concourse import mybir

F32 = mybir.dt.float32
BF16 = mybir.dt.bfloat16
U16 = mybir.dt.uint16
U32 = mybir.dt.uint32
F32R = mybir.dt.float32r
ALU = mybir.AluOpType
ACT = mybir.ActivationFunctionType
AX = mybir.AxisListType
RMAX = bass.bass_isa.ReduceOp.max

P = 128
NB, S, D = 8, 256, 256
N = NB * S
NT = N // P
KD = D // P
FF = 768
KF = FF // P
BLK = 32
EA, HD, MAXP = 8, 128, 64
EF, FH = 16, 128
EPS = 1e-5
MAGIC = 12582912.0
QMAX = 32767.0
CH = 512
NCH = N // CH
RELW = 192
RELROW = 384
UP_BANKS = 6


def hold(eng, sem, value):
    eng.wait_ge(sem, value)
    eng.nop(nofuse=True)


def chained(eng, sem, before):
    count = [0]

    def link(ins):
        count[0] += 1
        ins.then_inc(sem, 1)
        hold(eng, sem, before + count[0])
    return link


def gated_block_kernel(nc, a, out):
    with ExitStack() as ctx:
        base = {}

        def sb(name, shape, dt=F32):
            base[name] = -(-nc.sbuf_base // 32) * 32
            return ctx.enter_context(nc.sbuf_tensor(name, shape, dt))

        def over(name, shape, at, floats=0):
            return nc.alloc_sbuf_tensor_at(name, shape, F32R, offset=base[at] + 4 * floats)

        def sem(name):
            return ctx.enter_context(nc.semaphore(name))

        ps = ctx.enter_context(nc.psum_tensor("ps", [P, 8, 512], F32))
        x = sb("x", [P, NT, D])
        lnb = sb("lnb", [P, NT, D])
        xqT = sb("xqT", [P, KD, N])
        up = sb("up", [P, KF, N])
        gate = sb("gate", [P, KF, N])
        ctxT = gate[:, 0:2, :]
        w0 = gate[:, 2, 0:4 * D].rearrange("p (k e) -> p k e", k=4)
        b0 = gate[0:1, 3, 0:D]
        rb = up[0:1, 0, 0:NB * D].rearrange("p (b e) -> p b e", b=NB)
        csum = sb("csum", [P, KD, NB])
        gates = sb("gates", [P, 4])
        tg = sb("tg", [P, 4])
        wnat = up[:, 1:4, :].rearrange("p m n -> p (m n)")[:, 0:18 * D].rearrange("p (g n) -> p g n", n=D)
        wabs = sb("wabs", [P, 144])
        winv = sb("winv", [P, 144])
        wT = sb("wT", [P, 2, KD, FF])
        wdT = sb("wdT", [P, KF, D])
        ident = sb("ident", [P, P])
        ones1 = sb("ones1", [1, P])
        magic = sb("magic", [P, 1])
        neghalf = sb("neghalf", [P, 2])
        st = sb("st", [P, 2, 6])
        mv = sb("mv", [P, 2, 2, 2])
        ve = sb("ve", [P, 2, 2])
        rs = sb("rs", [P, 2, 2])
        xn = sb("xn", [P, 2, 2, D])
        xnT = sb("xnT", [P, 2, KD, S])
        amx = sb("amx", [P, 64])
        pmax = sb("pmax", [P, 2])
        gmx = sb("gmx", [P, 2])
        sx = sb("sx", [P, 2])
        sug = sb("sug", [P, 2, 2])
        sp = sb("sp", [P, 2])
        so = sb("so", [P, 3])
        sig = sb("sig", [P, 2, N])
        oq = up[:, 3:6, :].rearrange("p m n -> p (m n)").rearrange("p (u m c) -> p u m c", u=2, m=KF)

        kvals = lnb
        keysT = xqT
        w1x = sb("w1x", [P, KD, D])
        b1x = sb("b1x", [P, KD])
        infm = sig[:, 0, 0:4 * D].bitcast(U32).rearrange("p (t d) -> p t d", t=4)
        zero = sb("zero", [P, 1])
        c_buf = sig.rearrange("p u n -> p (u n)")
        qx = c_buf[:, 0:1024].rearrange("p (u e s) -> p u e s", u=2, e=KD)
        px = c_buf[:, 1024:2048].rearrange("p (u t s) -> p u t s", u=2, t=2)
        pxT = c_buf[:, 2048:3072].rearrange("p (u k s) -> p u k s", u=2, k=2)
        cmx = sb("cmx", [P, 2, 2]); cnm = sb("cnm", [P, 2, 2]); cz = sb("cz", [P, 2, 2]); crz = sb("crz", [P, 2, 2])
        gflat = gate.rearrange("p m n -> p (m n)")
        qw = gflat[:, 0:2048].rearrange("p (k e) -> p k e", k=KD)
        ow = gflat[:, 2048:4096].rearrange("p (e d) -> p e d", e=EA)
        w1 = gflat[:, 4096:8192].rearrange("p (k f) -> p k f", k=KD)
        w2 = gflat[:, 8192:12288].rearrange("p (e d) -> p e d", e=EF)
        inner = up[:, 0:2, :].rearrange("p a n -> p (a n)").rearrange("p (t d) -> p t d", d=D)
        nxn = up[:, 2:4, :].rearrange("p a n -> p (a n)").rearrange("p (t d) -> p t d", d=D)
        ln = sb("ln", [P, 4, D])
        gw = sb("gw", [P, KD, EA]); kw = sb("kw", [P, KD, HD]); vw = sb("vw", [P, KD, HD])
        gw2 = sb("gw2", [P, KD, EF]); qb = sb("qb", [EA, HD]); ob = sb("ob", [EA, D]); b2 = sb("b2", [EF, D])
        kb = sb("kb", [P, 1]); vb = sb("vb", [P, HD]); b1 = sb("b1", [P, EF])
        relx = sb("relx", [P, 2, RELW]); rele = sb("rele", [P, 2])
        iota = sb("iota", [P, EF]); sel8 = sb("sel8", [EA, EA, P], BF16)
        ghot = sb("ghot", [P, 2, 2, 2, EF])
        G = sb("G", [P, 2, 2, EF])
        hot = sb("hot", [P, 2, 2, 2, EF])
        top = sb("top", [P, 2, 8]); tidx = sb("tidx", [P, 2, 8], U32); tif = sb("tif", [P, 2, 2])
        td = sb("td", [P, 2]); te = sb("te", [P, 2]); gj = sb("gj", [P, 2, 2, 2])
        wdflat = wdT.rearrange("p m d -> p (m d)")
        hotT = wdflat[0:EA, 0:512]; hotTb = wdflat[0:EA, 512:768].bitcast(BF16)
        GT = wdflat[0:EA, 768:1280].rearrange("p (u s) -> p u s", u=2)
        mask = up[:, 4:6, :].rearrange("p a n -> p (a n)").bitcast(BF16)\
            .rearrange("p (u e j s) -> p u e j s", u=2, e=EA, j=2)
        lflat = lnb.rearrange("p t d -> p (t d)")
        xflat = xqT.rearrange("p k n -> p (k n)")
        qsel = lflat[:, 0:512].rearrange("p (j s) -> p j s", j=2)
        qT = lflat[:, 512:1024].rearrange("p (j s) -> p j s", j=2)
        kT = lflat[:, 1024:1280]
        val = lflat[:, 1280:1792].rearrange("p (u k h) -> p u k h", u=2, k=2)
        R = lflat[:, 1792:2560].rearrange("p (t j c) -> p t j c", t=2, j=2)
        B = xflat[:, 0:1024].rearrange("p (j t s) -> p j t s", j=2, t=2)
        pm = xflat[:, 1024:2048].rearrange("p (j t s) -> p j t s", j=2, t=2)
        pmT = xflat[:, 2048:3072].rearrange("p (k c) -> p k c", k=2)
        ctxE = c_buf[:, 0:2048].rearrange("p (e s) -> p e s", e=EA)
        zrow = c_buf[:, 2048:2048 + RELW]
        w1h = over("w1h", [P, KD, EF * FH], "gate"); w1l = over("w1l", [P, KD, EF * FH], "gate", 4096)
        w2h = over("w2h", [P, EF, D], "up", 4 * N); w2l = over("w2l", [P, EF, D], "gate", 8192)
        xmh = over("xmh", [P, KD, N], "wT"); xml = over("xml", [P, KD, N], "up")
        hrh = over("hrh", [P, 3, CH], "sig", 3 * CH); hrl = over("hrl", [P, 3, CH], "xn")
        nmv = sb("nmv", [P, 2, 2, 2]); nve = sb("nve", [P, 2, 2]); nrs = sb("nrs", [P, 2, 2])
        nhot = xn[:, 0].rearrange("p t d -> p (t d)").rearrange("p (t j e) -> p t j e", t=NT, j=2)
        nghot = xn[:, 1].rearrange("p t d -> p (t d)").rearrange("p (t j e) -> p t j e", t=NT, j=2)
        def piece(at, floats):
            return c_buf[:, at:at + floats]
        ntop = piece(0, 128).rearrange("p (t m) -> p t m", t=NT)
        ntidx = piece(128, 128).bitcast(U32).rearrange("p (t m) -> p t m", t=NT)
        ntif = piece(256, 32).rearrange("p (t j) -> p t j", t=NT)
        ngj = piece(288, 32).rearrange("p (t j) -> p t j", t=NT)
        ntd = piece(320, 16); nte = piece(336, 16)
        nG = piece(352, 256).rearrange("p (t e) -> p t e", t=NT)
        mmx = sb("mmx", [P, 4]); mnm = sb("mnm", [P, 4]); mz = sb("mz", [P, 4]); mrz = sb("mrz", [P, 4])
        GTa = up[0:EF, 2, :]
        gbc = [xflat[:, 2048 * n:2048 * n + 2048] for n in range(2)] + [lflat[:, 2048 * n:2048 * n + 2048] for n in range(2)]
        gbc = [g_.rearrange("p (e c) -> p e c", e=4) for g_ in gbc]
        hg = c_buf[:, 0:3 * CH].rearrange("p (r c) -> p r c", r=3)
        yT = up[:, 3, 0:KD * CH].rearrange("p (k c) -> p k c", k=KD)
        skew = a["skew"]
        gscr = a["gscr"]

        ld_k = sem("ld_k"); ld_kT = sem("ld_kT"); ld_c = sem("ld_c"); ld_m = sem("ld_m"); ld_q = sem("ld_q")
        ld_e = sem("ld_e"); z_dma = sem("z_dma"); z_set = sem("z_set")
        v_inf = sem("v_inf"); v_ready = sem("v_ready"); rel_ready = sem("rel_ready"); selz = sem("selz")
        c_var = sem("c_var"); c_rstd = sem("c_rstd"); c_xn = sem("c_xn"); c_turned = sem("c_turned")
        c_xnT = sem("c_xnT"); c_qmm = sem("c_qmm"); c_q = sem("c_q"); c_smm = sem("c_smm"); c_max = sem("c_max")
        c_nmax = sem("c_nmax"); c_exp = sem("c_exp"); c_pturn = sem("c_pturn"); c_pT = sem("c_pT"); c_pv = sem("c_pv")
        c_rz = sem("c_rz"); c_x3 = sem("c_x3")
        m_st = sem("m_st"); m_var = sem("m_var"); m_rstd = sem("m_rstd"); m_src = sem("m_src"); m_st2 = sem("m_st2")
        m_var2 = sem("m_var2"); m_rstd2 = sem("m_rstd2"); m_ln = sem("m_ln"); m_w = sem("m_w"); m_xn = sem("m_xn")
        m_turned = sem("m_turned"); m_xnT = sem("m_xnT"); m_log = sem("m_log"); m_top = sem("m_top")
        m_d = sem("m_d"); m_e = sem("m_e"); m_gate = sem("m_gate"); m_hturn = sem("m_hturn"); m_hT = sem("m_hT")
        m_maskmm = sem("m_maskmm"); m_mask = sem("m_mask"); m_kmm = sem("m_kmm"); m_k = sem("m_k"); m_vmm = sem("m_vmm")
        m_v = sem("m_v"); m_qmm = sem("m_qmm"); m_qsel = sem("m_qsel"); m_qT = sem("m_qT"); m_rmm = sem("m_rmm")
        m_r = sem("m_r"); m_rout = sem("m_rout"); m_rin = sem("m_rin"); m_smm = sem("m_smm"); m_max = sem("m_max")
        m_nmax = sem("m_nmax"); m_exp = sem("m_exp"); m_rz = sem("m_rz"); m_p = sem("m_p"); m_pturn = sem("m_pturn")
        m_pT = sem("m_pT"); m_pv = sem("m_pv"); m_cE = sem("m_cE"); m_omm = sem("m_omm"); m_out = sem("m_out")
        n_st = sem("n_st"); n_var = sem("n_var"); n_rstd = sem("n_rstd"); n_ln = sem("n_ln"); n_w = sem("n_w")
        n_xn = sem("n_xn"); n_turned = sem("n_turned"); n_xnT = sem("n_xnT"); n_all = sem("n_all"); n_log = sem("n_log")
        e_l = sem("e_l"); n_top = sem("n_top");
        w_high = sem("w_high"); w_low = sem("w_low"); n_d = sem("n_d"); n_e = sem("n_e"); n_gate = sem("n_gate"); n_gturn = sem("n_gturn")
        n_GT = sem("n_GT"); n_base = sem("n_base"); g_out = sem("g_out")
        g_in = [sem(f"g_in{n}") for n in range(4)]
        e_hmm = sem("e_hmm"); e_hg = sem("e_hg"); e_h = sem("e_h"); e_ymm = sem("e_ymm"); e_y = sem("e_y")
        e_yturn = sem("e_yturn"); e_x4 = sem("e_x4")
        ld_x = sem("ld_x"); ld_w0 = sem("ld_w0"); ld_ctxT = sem("ld_ctxT"); ld_g = sem("ld_g")
        ld_wq = sem("ld_wq")
        const_ready = sem("const_ready"); ident_zero = sem("ident_zero")
        tanh_ready = sem("tanh_ready")
        dve0 = sem("dve0")
        csum_ready = sem("csum_ready"); rb_mm = sem("rb_mm"); rb_ready = sem("rb_ready")
        wstep = sem("wstep"); wscaled = sem("wscaled"); wround = sem("wround"); wdq = sem("wdq")
        w_turned = sem("w_turned"); w_ready = sem("w_ready")
        ln_link = sem("ln_link"); a_var = sem("a_var"); a_rstd = sem("a_rstd"); a_xn = sem("a_xn")
        a_turned = sem("a_turned"); a_xnT = sem("a_xnT"); a_mm = sem("a_mm"); a_x1 = sem("a_x1")
        f_var = sem("f_var"); f_rstd = sem("f_rstd"); f_ln = sem("f_ln")
        f_red = sem("f_red"); f_pmax = sem("f_pmax"); f_gmax = sem("f_gmax"); f_scale = sem("f_scale")
        f_q1 = sem("f_q1"); f_xq = sem("f_xq"); f_turned = sem("f_turned"); f_xqT = sem("f_xqT")
        f_mm = sem("f_mm"); f_ev = sem("f_ev")
        f_g1 = sem("f_g1"); f_g2 = sem("f_g2"); f_sig = sem("f_sig"); f_s1 = sem("f_s1"); f_s2 = sem("f_s2")
        f_prod = sem("f_prod"); f_p1 = sem("f_p1"); f_p2 = sem("f_p2"); f_o = sem("f_o")
        f_o1 = sem("f_o1"); f_oq = sem("f_oq"); f_down = sem("f_down"); f_x2 = sem("f_x2")
        stored = sem("stored")

        x_tok = a["x"].rearrange("b (t p) d -> p (b t) d", p=P)
        out_tok = out.rearrange("b (t p) d -> p (b t) d", p=P)

        def bank(n):
            return ps[:, n, :]

        def bank2(n):
            return ps[:, n, :].rearrange("p (a c) -> p a c", a=2)

        block = ctx.enter_context(nc.Block())

        @block.sync
        def _(sp_):
            for h in range(4):
                sp_.dma_start(x[:, 4 * h:4 * h + 4, :], x_tok[:, 4 * h:4 * h + 4, :]).then_inc(ld_x, 16)
                if h == 0:
                    sp_.dma_start(gates[:, 0:2], a["g_xattn"].partition_broadcast(P)).then_inc(ld_g, 16)
                    sp_.dma_start(gates[:, 2:4], a["g_ffn"].partition_broadcast(P)).then_inc(ld_g, 16)
                    sp_.dma_start(ctxT, a["ctxT"].rearrange("(k p) n -> p k n", p=P)).then_inc(ld_ctxT, 16)
                    sp_.dma_start(w0, a["L0_xattn_WT"].rearrange("(k p) e -> p k e", p=P)).then_inc(ld_w0, 16)
                    sp_.dma_start(b0, a["L0_xattn_b"].rearrange("(a e) -> a e", a=1)).then_inc(ld_w0, 16)
            for n, name in enumerate(("L0_ffn_w_up", "L0_ffn_w_gate")):
                sp_.dma_start(wnat[:, 6 * n:6 * n + 6, :], a[name].rearrange("(g p) n -> p g n", p=P)).then_inc(ld_wq, 16)
            sp_.dma_start(wnat[:, 12:18, :].rearrange("p (h m) n -> p h (m n)", h=2),
                          a["L0_ffn_w_down"].rearrange("(h p) i -> p h i", p=P)).then_inc(ld_wq, 16)
            sp_.dma_start(w1x[:], a["L1_xattn_WT"].rearrange("(k p) e -> p k e", p=P)).then_inc(ld_c, 16)
            sp_.dma_start(b1x[:], a["xattn1_bT"]).then_inc(ld_c, 16)
            for n, name in enumerate(("ln1_w", "ln1_b", "ln2_w", "ln2_b")):
                sp_.dma_start(ln[:, n, :], a["L1_ffn_" + name].partition_broadcast(P)).then_inc(ld_m, 16)
            for dst, name in ((gw, "attn_gate_w"), (kw, "k_w"), (vw, "v_w"), (gw2, "ff_gate_w")):
                sp_.dma_start(dst[:], a["L1_ffn_" + name].rearrange("(k p) e -> p k e", p=P)).then_inc(ld_m, 16)
            for dst, name in ((qb, "q_b"), (ob, "o_b"), (b2, "ff_b2")):
                sp_.dma_start(dst[:], a["L1_ffn_" + name]).then_inc(ld_m, 16)
            sp_.dma_start(kb[:], a["L1_ffn_k_b"].rearrange("(h a) -> h a", a=1)).then_inc(ld_m, 16)
            sp_.dma_start(vb[:], a["L1_ffn_v_b"].partition_broadcast(P)).then_inc(ld_m, 16)
            sp_.dma_start(b1[:], a["ff_b1T"]).then_inc(ld_m, 16)
            sp_.dma_start(relx[:], a["relx"]).then_inc(ld_m, 16)
            sp_.dma_start(rele[:], a["rele"]).then_inc(ld_m, 16)
            sp_.wait_ge(f_xq, NB)
            sp_.dma_start(kvals[:], a["ctx_1024"].rearrange("b (t p) d -> p (b t) d", p=P)).then_inc(ld_k, 16)
            sp_.wait_ge(f_mm, 2 * KF * NCH)
            sp_.dma_start(keysT[:], a["ctxT"].rearrange("(k p) n -> p k n", p=P)).then_inc(ld_kT, 16)
            sp_.wait_ge(f_o1, NCH)
            sp_.dma_start(qw.rearrange("p k (e h) -> p k e h", e=EA)[:, 0], a["L1_ffn_q_w"][:, 0:P, :].rearrange("e p h -> p e h")).then_inc(ld_q, 16)
            sp_.dma_start(qw.rearrange("p k (e h) -> p k e h", e=EA)[:, 1], a["L1_ffn_q_w"][:, P:D, :].rearrange("e p h -> p e h")).then_inc(ld_q, 16)
            sp_.dma_start(ow, a["L1_ffn_o_w"].rearrange("e h d -> h e d")).then_inc(ld_q, 16)
            for k in range(KD):
                sp_.dma_start(w1[:, k, :].rearrange("p (e f) -> p e f", e=EF),
                              a["L1_ffn_ff_w1"][:, k * P:(k + 1) * P, :].rearrange("e p f -> p e f")).then_inc(ld_e, 16)
            sp_.dma_start(w2, a["L1_ffn_ff_w2"].rearrange("e f d -> f e d")).then_inc(ld_e, 16)
            sp_.wait_ge(z_set, 1)
            for jt in range(4):
                lo = (1 - jt % 2) * RELW
                sp_.dma_start(skew[jt, :, lo:lo + RELW - jt % 2], zrow[:, 0:RELW - jt % 2]).then_inc(z_dma, 16)
            sp_.wait_ge(z_dma, 64)

            def skew_batch(b, first):
                for t in range(2):
                    lo = t * (RELW - 1)
                    hold(sp_, m_r, 2 * b + t + 1)
                    if not first and t == 0:
                        hold(sp_, m_rin, 16 * b)
                    sp_.dma_start(skew.rearrange("(j t) q c -> t q j c", t=2)[t, :, :, lo:lo + RELW], R[:, t])\
                        .then_inc(m_rout, 16)
                hold(sp_, m_rout, 32 * b + 32)
                if not first:
                    hold(sp_, m_max, 4 * b)
                sp_.dma_start(B.rearrange("p j t s -> p (j t) s"),
                              bass.AP(tensor=skew.tensor, offset=skew.offset + P - 1,
                                      ap=[[RELROW - 1, P], [P * RELROW, 4], [1, S]])).then_inc(m_rin, 16)

            skew_batch(0, True)
            with sp_.Fori(1, NB) as b:
                skew_batch(b, False)

            sp_.wait_ge(n_GT, NCH)
            sp_.dma_start(gscr, GTa).then_inc(g_out, 16)
            sp_.wait_ge(g_out, 16)

            def gates_in(j, first):
                for n in range(4):
                    if not first:
                        hold(sp_, e_hg, EF * j - EF + 4 * n + 4)
                    sp_.dma_start(gbc[n], gscr[4 * n:4 * n + 4, bass.ds(CH * j, CH)].partition_broadcast(P))\
                        .then_inc(g_in[n], 16)
            gates_in(0, True)
            with sp_.Fori(1, NCH) as j:
                gates_in(j, False)
            with sp_.Fori(0, NCH) as j:
                hold(sp_, e_x4, 2 * j + 2)
                sp_.dma_start(out_tok[:, bass.ds(4 * j, 4), :], x[:, bass.ds(4 * j, 4), :]).then_inc(stored, 16)
            sp_.wait_ge(stored, 16 * NCH)

        @block.gpsimd
        def _(pool):
            nc.gpsimd.memset(ident[:], 0.0).then_inc(ident_zero, 1)
            nc.gpsimd.memset(neghalf[:], -0.5).then_inc(ident_zero, 1)
            nc.gpsimd.memset(magic[:], MAGIC).then_inc(ident_zero, 1)
            nc.gpsimd.memset(ones1[:], 1.0).then_inc(ident_zero, 1)
            nc.gpsimd.memset(zero[:], 0.0).then_inc(ident_zero, 1)
            nc.gpsimd.memset(sel8[:], 0.0).then_inc(ident_zero, 1)
            nc.gpsimd.iota(iota[:], [[1, EF]], base=0, channel_multiplier=0, allow_small_or_imprecise_dtypes=True)\
                .then_inc(ident_zero, 1)
            pool.wait_ge(ident_zero, 7)
            nc.gpsimd.affine_select(out=sel8[:], in_=sel8[:], compare_op=ALU.not_equal, fill=1.0, base=0,
                                    pattern=[[1, EA], [0, P]], channel_multiplier=-1).then_inc(selz, 1)
            pool.wait_ge(selz, 1)
            nc.gpsimd.affine_select(out=ident[:], in_=ident[:], compare_op=ALU.not_equal, fill=1.0, base=0,
                                    pattern=[[-1, P]], channel_multiplier=1).then_inc(const_ready, 1)

            def ln_pow(b, u, var, rstd):
                pool.wait_ge(var, b + 1)
                nc.gpsimd.tensor_tensor(rs[:, u, :], ve[:, u, :], neghalf[:], ALU.pow).then_inc(rstd, 1)

            pool.wait_ge(const_ready, 1)
            ln_pow(0, 0, a_var, a_rstd)
            pool.wait_ge(wstep, 3)
            wv = wnat.rearrange("p g (c k) -> p (g c) k", k=BLK)
            nc.gpsimd.tensor_tensor(wv, wv, winv[:].unsqueeze(2).to_broadcast([P, 144, BLK]),
                                    ALU.mult).then_inc(wscaled, 1)
            ln_pow(1, 1, a_var, a_rstd)
            with pool.Fori(1, NB // 2) as i:
                for u in range(2):
                    ln_pow(2 * i + u, u, a_var, a_rstd)
            pool.wait_ge(wround, 1)
            nc.gpsimd.tensor_tensor(wv, wv, wabs[:].unsqueeze(2).to_broadcast([P, 144, BLK]),
                                    ALU.mult).then_inc(wdq, 1)
            with pool.Fori(0, NB // 2) as i:
                for u in range(2):
                    ln_pow(2 * i + u, u, f_var, f_rstd)
            for k in range(4):
                w = 2 if k == 1 else 1
                pool.wait_ge(f_pmax, k + 1)
                nc.gpsimd.partition_all_reduce(gmx[:, 0:w], pmax[:, 0:w], P, RMAX).then_inc(f_gmax, 1)

            with pool.Fori(0, NB // 2) as i:
                for u in range(2):
                    ln_pow(2 * i + u, u, c_var, c_rstd)
            pool.wait_ge(c_x3, NB)
            nc.gpsimd.memset(zrow, 0.0).then_inc(z_set, 1)

            def affine(v, b, n, ln_done, w_done, xn_done):
                hold(pool, ln_done, 2 * b + 2)
                nc.gpsimd.tensor_tensor(v, v, ln[:, n, :].unsqueeze(1).to_broadcast([P, 2, D]), ALU.mult)\
                    .then_inc(w_done, 1)
                hold(pool, w_done, b + 1)
                nc.gpsimd.tensor_tensor(v, v, ln[:, n + 1, :].unsqueeze(1).to_broadcast([P, 2, D]), ALU.add)\
                    .then_inc(xn_done, 1)

            def m_in(b, u):
                ln_pow(b, u, m_var, m_rstd)
                ln_pow(b, u, m_var2, m_rstd2)
                affine(xn[:, u], b, 0, m_ln, m_w, m_xn)

            def n_pow(b, u):
                pool.wait_ge(n_var, b + 1)
                nc.gpsimd.tensor_tensor(nrs[:, u, :], nve[:, u, :], neghalf[:], ALU.pow).then_inc(n_rstd, 1)

            def n_affine(b):
                affine(nxn[:, bass.ds(2 * b, 2), :], b, 2, n_ln, n_w, n_xn)

            m_in(0, 0)
            m_in(1, 1)
            m_in(2, 0)
            m_in(3, 1)
            n_pow(0, 0)
            with pool.Fori(0, NB // 2 - 2) as i:
                for u in range(2):
                    b = 2 * i + u
                    n_affine(b)
                    m_in(b + 4, u)
                    n_pow(b + 1, 1 - u)
            for b in range(NB - 4, NB - 2):
                n_affine(b)
                n_pow(b + 1, 1 - b % 2)
            n_affine(NB - 2)
            n_pow(NB - 1, 1)
            n_affine(NB - 1)
            with pool.Fori(0, NB // 2) as i:
                for u in range(2):
                    b = 2 * i + u
                    hold(pool, n_xnT, 2 * b + 2)
                    nc.gpsimd.tensor_tensor(xml[:, :, bass.ds(S * b, S)], xnT[:, u], xmh[:, :, bass.ds(S * b, S)].bitcast(F32),
                                            ALU.subtract).then_inc(n_all, 1)
            pool.wait_ge(w_high, 2)
            nc.gpsimd.tensor_tensor(w2l[:], w2, w2h[:].bitcast(F32), ALU.subtract).then_inc(w_low, 1)

        @block.vector
        def _(dve):
            def ln_stats(src, b, u, chain, var, mv=mv, ve=ve, before=0):
                link = chained(dve, chain, b * 2 + before)
                nc.vector.bn_stats(st[:, 0, :], src[0])
                link(nc.vector.bn_stats(st[:, 1, :], src[1]))
                nc.vector.bn_aggr(mv[:, u, 0, :], st[:, 0, :])
                link(nc.vector.bn_aggr(mv[:, u, 1, :], st[:, 1, :]))
                nc.vector.tensor_scalar(ve[:, u, :], mv[:, u, :, 1], EPS, None, ALU.add).then_inc(var, 1)

            def ln_norm(dst, src, b, u, rstd, done, mv=mv, rs=rs):
                dve.wait_ge(rstd, b + 1)
                for t in range(2):
                    nc.vector.tensor_scalar(dst[t], src[t], mv[:, u, t, 0:1], rs[:, u, t:t + 1],
                                            ALU.subtract, ALU.mult).then_inc(done, 1)

            def tiles(buf, b):
                return [buf[:, 2 * b + t, :] for t in range(2)]

            def a_norm(b, u):
                ln_stats(tiles(x, b), b, u, ln_link, a_var)
                ln_norm([xn[:, u, t, :] for t in range(2)], tiles(x, b), b, u, a_rstd, a_xn)

            def a_fin(b, u):
                dve.wait_ge(a_mm, b + 1)
                xb = x[:, bass.ds(2 * b, 2), :]
                nc.vector.scalar_tensor_tensor(xb, bank2(2 + u), tg[:, 0:1], xb, ALU.mult, ALU.add).then_inc(a_x1, 1)

            dve.wait_ge(ld_x, 64)
            a_norm(0, 0)
            dve.wait_ge(ld_wq, 48)
            wv = wnat.rearrange("p g (c k) -> p (g c) k", k=BLK)
            nc.vector.tensor_reduce(wabs[:], wv, AX.X, ALU.max, apply_absolute_value=True).then_inc(wstep, 1)
            dve.wait_ge(wstep, 1)
            nc.vector.tensor_scalar(wabs[:], wabs[:], 1.0 / 7.0, 1e-12, ALU.mult, ALU.max).then_inc(wstep, 1)
            dve.wait_ge(wstep, 2)
            nc.vector.reciprocal(winv[:], wabs[:]).then_inc(wstep, 1)
            dve.wait_ge(ld_ctxT, 16)
            nc.vector.tensor_reduce(csum[:], ctxT.rearrange("p k (b s) -> p k b s", b=NB), AX.X, ALU.add)\
                .then_inc(csum_ready, 1)
            dve.wait_ge(rb_mm, 1)
            dve.wait_ge(ld_w0, 32)
            nc.vector.scalar_tensor_tensor(rb, ps[0:1, 4:8, :].rearrange("p a (c e) -> p (a c) e", c=2), 1.0 / S,
                                           b0.unsqueeze(1).to_broadcast([1, NB, D]), ALU.mult, ALU.add)\
                .then_inc(rb_ready, 1)
            dve.wait_ge(tanh_ready, 1)
            with dve.Fori(0, NB // 2 - 1) as i:
                for u in range(2):
                    a_norm(2 * i + u + 1, 1 - u)
                    a_fin(2 * i + u, u)
            a_norm(NB - 1, 1)
            a_fin(NB - 2, 0)
            a_fin(NB - 1, 1)
            dve.wait_ge(wscaled, 1)
            nc.vector.tensor_scalar(wnat, wnat, MAGIC, -MAGIC, ALU.add, ALU.add).then_inc(dve0, 1)
            dve.wait_ge(dve0, 1)
            nc.vector.tensor_scalar(wnat, wnat, 7.0, -8.0, ALU.min, ALU.max).then_inc(wround, 1)

            def f_norm(b, u):
                ln_stats(tiles(x, b), b, u, ln_link, f_var, before=2 * NB)
                ln_norm(tiles(lnb, b), tiles(x, b), b, u, f_rstd, f_ln)

            def f_absmax(b):
                hold(dve, f_ln, 2 * b + 2)
                nc.vector.tensor_reduce(amx[:, bass.ds(b, 1)], lnb[:, bass.ds(2 * b, 2), :], AX.XY, ALU.max,
                                        apply_absolute_value=True).then_inc(f_red, 1)

            dve.wait_ge(a_x1, NB)
            f_norm(0, 0)
            with dve.Fori(0, NB // 2 - 1) as i:
                for u in range(2):
                    f_norm(2 * i + u + 1, 1 - u)
                    f_absmax(2 * i + u)
            f_norm(NB - 1, 1)
            f_absmax(NB - 2)
            f_absmax(NB - 1)

            def quant_scale(k, w, srcs, reds, scale, inv):
                dve.wait_ge(f_red, reds)
                for n, s_ in enumerate(srcs):
                    ins = nc.vector.tensor_reduce(pmax[:, n:n + 1], s_, AX.X, ALU.max)
                ins.then_inc(f_pmax, 1)
                dve.wait_ge(f_gmax, k + 1)
                nc.vector.tensor_scalar(scale, gmx[:, 0:w], 1.0 / QMAX, 1e-12, ALU.mult, ALU.max).then_inc(dve0, 1)
                dve.wait_ge(dve0, 2 + k)
                nc.vector.reciprocal(inv, scale).then_inc(f_scale, 1)
                dve.wait_ge(f_scale, k + 1)

            quant_scale(0, 1, [amx[:, 0:NB]], NB, sx[:, 0:1], sx[:, 1:2])
            def x_quant(b, u, first):
                xb = lnb[:, bass.ds(2 * b, 2), :]
                nc.vector.tensor_scalar(xb, xb, sx[:, 1:2], MAGIC, ALU.mult, ALU.add).then_inc(f_q1, 1)
                hold(dve, f_q1, b + 1)
                if not first:
                    hold(dve, f_turned, b - 1)
                nc.vector.tensor_scalar(xn[:, u], xb, -MAGIC, None, ALU.add).then_inc(f_xq, 1)

            x_quant(0, 0, True)
            x_quant(1, 1, True)
            with dve.Fori(1, NB // 2) as i:
                for u in range(2):
                    x_quant(2 * i + u, u, False)
            dve.wait_ge(ld_k, 16)
            for n in range(4):
                part = kvals[:, 4 * n:4 * n + 4, :]
                if n:
                    hold(dve, v_ready, n)
                nc.vector.tensor_scalar(infm, part, -3.4028234663852886e38, None, ALU.is_lt).then_inc(v_inf, 1)
                hold(dve, v_inf, n + 1)
                nc.vector.copy_predicated(part, infm, zero[:].unsqueeze(2).to_broadcast([P, 4, D])).then_inc(v_ready, 1)
            dve.wait_ge(ld_m, 16 * 16)
            for t in range(2):
                nc.vector.tensor_scalar(relx[:, t, :], relx[:, t, :], rele[:, t:t + 1], None, ALU.subtract)\
                    .then_inc(rel_ready, 1)
            with dve.Fori(0, NCH) as j:
                for m in range(2 * KF):
                    hold(dve, f_ev, 2 * KF * j + m + 1)
                    src = (up if m < KF else gate)[:, m % KF, bass.ds(CH * j, CH)]
                    nc.vector.tensor_reduce(amx[:, bass.ds(m * NCH + j, 1)], src, AX.X, ALU.max,
                                            apply_absolute_value=True).then_inc(f_red, 1)
            R1 = NB + NCH * 2 * KF
            quant_scale(1, 2, [amx[:, 0:KF * NCH], amx[:, KF * NCH:2 * KF * NCH]], R1, sug[:, 0, :], sug[:, 1, :])

            def g_dequant(m):
                hold(dve, f_g1, m + 1)
                g = gate[:, m, :]
                nc.vector.tensor_scalar(g, g, -MAGIC, sug[:, 0, 1:2], ALU.add, ALU.mult).then_inc(f_g2, 1)

            def g_prod(m, u):
                hold(dve, f_s1, m + 1)
                nc.vector.tensor_scalar(sig[:, u, :], sig[:, u, :], -MAGIC, 65535.0, ALU.add, ALU.min).then_inc(f_s2, 1)
                hold(dve, f_s2, m + 1)
                g = gate[:, m, :]
                nc.vector.scalar_tensor_tensor(g, sig[:, u, :], 1.0 / 65536.0, g, ALU.mult, ALU.mult).then_inc(f_prod, 1)
                hold(dve, f_prod, m + 1)
                nc.vector.tensor_reduce(amx[:, bass.ds(m, 1)], g, AX.X, ALU.max,
                                        apply_absolute_value=True).then_inc(f_red, 1)

            g_dequant(0)
            with dve.Fori(0, KF // 2 - 1) as i:
                for u in range(2):
                    g_dequant(2 * i + u + 1)
                    g_prod(2 * i + u, u)
            g_dequant(KF - 1)
            g_prod(KF - 2, 0)
            g_prod(KF - 1, 1)
            quant_scale(2, 1, [amx[:, 0:KF]], R1 + KF, sp[:, 0:1], sp[:, 1:2])

            with dve.Fori(0, KF) as m:
                g = gate[:, m, :]
                v = up[:, m, :]
                hold(dve, f_p1, 2 * m + 2)
                nc.vector.tensor_scalar(g, g, -MAGIC, None, ALU.add).then_inc(f_p2, 1)
                hold(dve, f_p2, m + 1)
                nc.vector.scalar_tensor_tensor(g, v, -MAGIC, g, ALU.add, ALU.mult).then_inc(f_o, 1)
                hold(dve, f_o, m + 1)
                nc.vector.tensor_reduce(amx[:, bass.ds(m, 1)], g, AX.X, ALU.max,
                                        apply_absolute_value=True).then_inc(f_red, 1)
            dve.wait_ge(f_red, R1 + 2 * KF)
            nc.vector.tensor_tensor(so[:, 2:3], sp[:, 0:1], sug[:, 0, 0:1], ALU.mult).then_inc(dve0, 1)
            dve.wait_ge(dve0, 5)
            nc.vector.tensor_reduce(pmax[:, 0:1], amx[:, 0:KF], AX.X, ALU.max).then_inc(f_pmax, 1)
            dve.wait_ge(f_gmax, 4)
            nc.vector.tensor_scalar(so[:, 0:1], gmx[:, 0:1], so[:, 2:3], 1.0 / QMAX, ALU.mult, ALU.mult).then_inc(dve0, 1)
            dve.wait_ge(dve0, 6)
            nc.vector.tensor_scalar(so[:, 0:1], so[:, 0:1], 1e-12, None, ALU.max).then_inc(dve0, 1)
            dve.wait_ge(dve0, 7)
            nc.vector.reciprocal(so[:, 1:2], so[:, 0:1]).then_inc(dve0, 1)
            dve.wait_ge(dve0, 8)
            nc.vector.tensor_tensor(so[:, 1:2], so[:, 1:2], so[:, 2:3], ALU.mult).then_inc(f_scale, 1)

            def o_dequant(j, u):
                hold(dve, f_o1, j + 1)
                nc.vector.tensor_scalar(oq[:, u], oq[:, u], -MAGIC, so[:, 0:1], ALU.add, ALU.mult).then_inc(f_oq, 1)

            def f_fin(j, u):
                for h in range(2):
                    hold(dve, f_down, 2 * j + h + 1)
                    xb = x[:, bass.ds(4 * j + 2 * h, 2), :]
                    nc.vector.scalar_tensor_tensor(xb, bank2(2 * u + h), tg[:, 2:3], xb, ALU.mult, ALU.add)\
                        .then_inc(f_x2, 1)

            o_dequant(0, 0)
            with dve.Fori(0, NCH // 2 - 1) as i:
                for u in range(2):
                    o_dequant(2 * i + u + 1, 1 - u)
                    f_fin(2 * i + u, u)
            o_dequant(NCH - 1, 1)
            f_fin(NCH - 2, 0)
            f_fin(NCH - 1, 1)

            dve.wait_ge(f_x2, NB)

            def c_norm(b, u):
                ln_stats(tiles(x, b), b, u, ln_link, c_var, before=4 * NB)
                ln_norm([xn[:, u, t, :] for t in range(2)], tiles(x, b), b, u, c_rstd, c_xn)

            def c_smax(b, u):
                hold(dve, c_smm, b + 1)
                for t in range(2):
                    nc.vector.tensor_scalar(px[:, u, t, :], bank2(3)[:, t, :], float("-inf"), None, ALU.max, ALU.max,
                                            accum_out=cmx[:, u, t:t + 1]).then_inc(c_max, 1)
                hold(dve, c_max, 2 * b + 2)
                nc.vector.tensor_scalar(cnm[:, u, :], cmx[:, u, :], -1.0, None, ALU.mult).then_inc(c_nmax, 1)

            def c_fin(b, u):
                link = chained(dve, c_rz, 2 * b)
                hold(dve, c_exp, 2 * b + 2)
                link(nc.vector.reciprocal(crz[:, u, :], cz[:, u, :]))
                link(nc.vector.tensor_scalar(crz[:, u, :], crz[:, u, :], tg[:, 1:2], None, ALU.mult))
                hold(dve, c_pv, b + 1)
                for t in range(2):
                    xt = x[:, 2 * b + t, :]
                    ins = nc.vector.scalar_tensor_tensor(xt, bank2(5 + u)[:, t, :], crz[:, u, t:t + 1], xt, ALU.mult, ALU.add)
                ins.then_inc(c_x3, 1)

            c_norm(0, 0)
            c_norm(1, 1)
            c_smax(0, 0)
            with dve.Fori(0, NB // 2 - 1) as i:
                for u in range(2):
                    b = 2 * i + u
                    c_norm(b + 2, u)
                    c_smax(b + 1, 1 - u)
                    c_fin(b, u)
            c_smax(NB - 1, 1)
            c_fin(NB - 2, 0)
            c_fin(NB - 1, 1)

            def m_norm(b, u):
                ln_stats(tiles(x, b), b, u, m_st, m_var)
                ln_norm(tiles(inner, b), tiles(x, b), b, u, m_rstd, m_src)
                hold(dve, m_src, 2 * b + 2)
                ln_stats(tiles(inner, b), b, u, m_st2, m_var2)
                ln_norm([xn[:, u, t, :] for t in range(2)], tiles(inner, b), b, u, m_rstd2, m_ln)

            def gating(b, u, ne, log, chain, d, e_, gate_done):
                hold(dve, log, b + 1)
                link = chained(dve, chain, 6 * b)
                lg = [ps[:, 0, ne * t:ne * t + ne] for t in range(2)]
                nc.vector.max(top[:, 0, :], lg[0])
                link(nc.vector.max(top[:, 1, :], lg[1]))
                nc.vector.tensor_tensor(td[:], top[:, :, 1], top[:, :, 0], ALU.subtract).then_inc(d, 1)
                nc.vector.max_index(tidx[:, 0, :], top[:, 0, :], lg[0])
                link(nc.vector.max_index(tidx[:, 1, :], top[:, 1, :], lg[1]))
                link(nc.vector.tensor_copy(tif[:], tidx[:, :, 0:2]))
                nc.vector.tensor_tensor(hot[:, u, :, :, 0:ne].rearrange("p t j e -> p (t j) e"),
                                        iota[:, 0:ne].unsqueeze(1).to_broadcast([P, 4, ne]),
                                        tif[:].rearrange("p t j -> p (t j)").unsqueeze(2).to_broadcast([P, 4, ne]),
                                        ALU.is_equal)
                hold(dve, e_, b + 1)
                link(nc.vector.tensor_scalar(td[:], te[:], 1.0, None, ALU.add))
                link(nc.vector.reciprocal(gj[:, u, :, 0], td[:]))
                nc.vector.tensor_tensor(gj[:, u, :, 1], gj[:, u, :, 0], te[:], ALU.mult)\
                    .then_inc(chain, 1)
                hold(dve, chain, 6 * b + 6)
                nc.vector.tensor_tensor(ghot[:, u, :, :, 0:ne].rearrange("p t j e -> p (t j) e"),
                                        hot[:, u, :, :, 0:ne].rearrange("p t j e -> p (t j) e"),
                                        gj[:, u].rearrange("p t j -> p (t j)").unsqueeze(2).to_broadcast([P, 4, ne]),
                                        ALU.mult).then_inc(gate_done, 1)
                hold(dve, gate_done, 2 * b + 1)
                nc.vector.tensor_tensor(G[:, u, :, 0:ne], ghot[:, u, :, 0, 0:ne], ghot[:, u, :, 1, 0:ne], ALU.add)\
                    .then_inc(gate_done, 1)

            def m_softmax(b):
                hold(dve, m_rin, 16 * b + 16)
                hold(dve, m_smm, b + 1)
                for j in range(2):
                    for t in range(2):
                        n = 2 * j + t
                        nc.vector.tensor_tensor_reduce(pm[:, j, t, :], bank2(6 + j)[:, t, :], B[:, j, t, :], 1.0, -3.0e38,
                                                       ALU.add, ALU.max, mmx[:, n:n + 1]).then_inc(m_max, 1)
                hold(dve, m_max, 4 * b + 4)
                nc.vector.tensor_scalar(mnm[:], mmx[:], -float(HD) ** -0.5, None, ALU.mult).then_inc(m_nmax, 1)

            def m_value(b, u):
                hold(dve, m_vmm, b + 1)
                nc.vector.tensor_tensor(val[:, u], ps[:, 1, 0:2 * HD].rearrange("p (k h) -> p k h", k=2),
                                        vb[:].unsqueeze(1).to_broadcast([P, 2, HD]), ALU.add).then_inc(m_v, 1)

            def m_scale(b, u):
                hold(dve, m_exp, 4 * b + 4)
                link = chained(dve, m_rz, 2 * b)
                link(nc.vector.reciprocal(mrz[:], mz[:]))
                link(nc.vector.tensor_tensor(mrz[:].rearrange("p (j t) -> p j t", j=2), mrz[:].rearrange("p (j t) -> p j t", j=2),
                                             gj[:, u].rearrange("p t j -> p j t"), ALU.mult))
                for n in range(4):
                    nc.vector.tensor_scalar(pm[:, n // 2, n % 2, :], pm[:, n // 2, n % 2, :], mrz[:, n:n + 1], None, ALU.mult)\
                        .then_inc(m_p, 1)

            def m_select(b, u):
                for e in range(EA):
                    hold(dve, m_qmm, 5 * b + e // 2 + 1)
                    data = bank2(2 + e // 2 % 2)[:, e % 2, :].unsqueeze(1).to_broadcast([P, 2, S])
                    if e == 0:
                        ins = nc.vector.tensor_copy(qsel, data)
                    else:
                        hold(dve, m_mask, 8 * b + e + 1)
                        hold(dve, m_qsel, 8 * b + e)
                        ins = nc.vector.copy_predicated(qsel, mask[:, u, e].bitcast(U16), data)
                    ins.then_inc(m_qsel, 1)
                hold(dve, m_qsel, 8 * b + 8)
                hold(dve, m_qmm, 5 * b + 5)
                nc.vector.tensor_tensor(qT, qsel, bank2(2), ALU.add).then_inc(m_qT, 1)

            def m_spread(b, u):
                hold(dve, m_pv, b + 1)
                c = ps[:, 1, :].rearrange("p (j s) -> p j s", j=2)
                nc.vector.tensor_tensor(ctxE, mask[:, u, :, 0, :], c[:, 0, :].unsqueeze(1).to_broadcast([P, EA, S]), ALU.mult)\
                    .then_inc(m_cE, 1)
                hold(dve, m_cE, 2 * b + 1)
                nc.vector.copy_predicated(ctxE, mask[:, u, :, 1, :].bitcast(U16), c[:, 1, :].unsqueeze(1).to_broadcast([P, EA, S]))\
                    .then_inc(m_cE, 1)

            def m_add(b):
                hold(dve, m_omm, b + 1)
                sb_ = inner[:, bass.ds(2 * b, 2), :]
                nc.vector.tensor_tensor(sb_, sb_, bank2(3), ALU.add).then_inc(m_out, 1)

            def m_gating(b, u):
                gating(b, u, EA, m_log, m_top, m_d, m_e, m_gate)

            m_norm(0, 0)
            m_norm(1, 1)
            m_gating(0, 0)
            m_value(0, 0)
            m_select(0, 0)
            m_gating(1, 1)
            m_norm(2, 0)

            def n_stats(b, u):
                hold(dve, m_out, b + 1)
                xb = x[:, bass.ds(2 * b, 2), :]
                nc.vector.scalar_tensor_tensor(xb, inner[:, bass.ds(2 * b, 2), :], tg[:, 3:4], xb, ALU.mult, ALU.add)\
                    .then_inc(n_base, 1)
                ln_stats(tiles(inner, b), b, u, n_st, n_var, nmv, nve)

            def n_norm(b, u):
                ln_norm(tiles(nxn, b), tiles(inner, b), b, u, n_rstd, n_ln, nmv, nrs)

            def m_step(b, u, norm=True, gate_next=True, first=False):
                m_softmax(b)
                if not first:
                    n_norm(b - 1, 1 - u)
                m_value(b + 1, 1 - u)
                m_scale(b, u)
                m_select(b + 1, 1 - u)
                m_spread(b, u)
                if gate_next:
                    m_gating(b + 2, u)
                if norm:
                    m_norm(b + 3, 1 - u)
                m_add(b)
                n_stats(b, u)

            m_step(0, 0, first=True)
            with dve.Fori(0, NB // 2 - 2) as i:
                for u in range(2):
                    m_step(2 * i + u + 1, 1 - u)
            m_step(NB - 3, 1, norm=False)
            m_step(NB - 2, 0, norm=False, gate_next=False)
            m_softmax(NB - 1)
            n_norm(NB - 2, 0)
            m_scale(NB - 1, 1)
            m_spread(NB - 1, 1)
            m_add(NB - 1)
            n_stats(NB - 1, 1)
            n_norm(NB - 1, 1)

            dve.wait_ge(w_high, 1)
            nc.vector.tensor_tensor(w1l[:], w1, w1h[:].bitcast(F32), ALU.subtract).then_inc(w_low, 1)

            lg = ps[:, 3, 0:NT * EF].rearrange("p (t e) -> p t e", e=EF)
            dve.wait_ge(n_log, NB)
            for t in range(NT):
                nc.vector.max(ntop[:, t, :], lg[:, t, :]).then_inc(n_top, 1)
            dve.wait_ge(n_top, NT)
            nc.vector.tensor_tensor(ntd, ntop[:, :, 1], ntop[:, :, 0], ALU.subtract).then_inc(n_d, 1)
            for t in range(NT):
                nc.vector.max_index(ntidx[:, t, :], ntop[:, t, :], lg[:, t, :]).then_inc(n_top, 1)
            dve.wait_ge(n_top, 2 * NT)
            nc.vector.tensor_copy(ntif, ntidx[:, :, 0:2]).then_inc(n_top, 1)
            dve.wait_ge(n_top, 2 * NT + 1)
            flat = "p t j -> p (t j)"
            nhotf = nhot.rearrange("p t j e -> p (t j) e")
            nc.vector.tensor_tensor(nhotf, iota[:].unsqueeze(1).to_broadcast([P, 2 * NT, EF]),
                                    ntif.rearrange(flat).unsqueeze(2).to_broadcast([P, 2 * NT, EF]), ALU.is_equal)
            dve.wait_ge(n_e, 1)
            nc.vector.tensor_scalar(ntd, nte, 1.0, None, ALU.add).then_inc(n_top, 1)
            dve.wait_ge(n_top, 2 * NT + 2)
            nc.vector.reciprocal(ngj[:, :, 0], ntd).then_inc(n_top, 1)
            dve.wait_ge(n_top, 2 * NT + 3)
            nc.vector.tensor_tensor(ngj[:, :, 1], ngj[:, :, 0], nte, ALU.mult).then_inc(n_top, 1)
            dve.wait_ge(n_top, 2 * NT + 4)
            nc.vector.tensor_tensor(nghot.rearrange("p t j e -> p (t j) e"), nhotf,
                                    ngj.rearrange(flat).unsqueeze(2).to_broadcast([P, 2 * NT, EF]),
                                    ALU.mult).then_inc(n_top, 1)
            dve.wait_ge(n_top, 2 * NT + 5)
            nc.vector.tensor_tensor(nG, nghot[:, :, 0, :], nghot[:, :, 1, :], ALU.add).then_inc(n_gate, 1)

            def e_gate(j, e):
                if e % 4 == 0:
                    hold(dve, g_in[e // 4], 16 * j + 16)
                n = EF * j + e
                if e >= 3:
                    hold(dve, e_l, n - 2)
                hold(dve, e_hmm, n + 1)
                nc.vector.scalar_tensor_tensor(hg[:, e % 3, :], bank(e % 3), b1[:, e:e + 1], gbc[e // 4][:, e % 4, :],
                                               ALU.add, ALU.mult).then_inc(e_hg, 1)

            def e_low(j, e):
                hold(dve, e_h, EF * j + e + 1)
                nc.vector.scalar_tensor_tensor(hrl[:, e % 3, :], hg[:, e % 3, :], 0.0, hrh[:, e % 3, :].bitcast(F32),
                                               ALU.max, ALU.subtract).then_inc(e_l, 1)

            dve.wait_ge(n_base, NB)
            with dve.Fori(0, NCH) as j:
                for e in range(EF):
                    e_gate(j, e)
                    if e:
                        e_low(j, e - 1)
                e_low(j, EF - 1)
                for h in range(2):
                    hold(dve, e_yturn, 2 * j + h + 1)
                    xb = x[:, bass.ds(4 * j + 2 * h, 2), :]
                    nc.vector.scalar_tensor_tensor(xb, bank2(6 + h), tg[:, 3:4], xb, ALU.mult, ALU.add).then_inc(e_x4, 1)

        @block.scalar
        def _(act):
            act.wait_ge(ld_g, 32)
            nc.scalar.activation(tg[:], gates[:], ACT.Tanh).then_inc(tanh_ready, 1)

            def a_evac(b, u):
                hold(act, a_turned, b + 1)
                nc.scalar.copy(xnT[:, u].rearrange("p k s -> p (k s)"), bank(u)).then_inc(a_xnT, 1)

            with act.Fori(0, NB // 2) as i:
                for u in range(2):
                    a_evac(2 * i + u, u)
            for n in range(9):
                act.wait_ge(w_turned, n + 1)
                if n < 6:
                    w, h, k = n // 3 % 2, n % 3, 0
                    dst = wT[:, n // 3, :, 256 * h:256 * h + 256]
                    src = bank2(4 + n % 4)
                else:
                    dst = wdT[:, 2 * (n - 6):2 * (n - 6) + 2, :]
                    src = bank2(4 + n % 4)
                nc.scalar.copy(dst, src).then_inc(w_ready, 1)

            act.wait_ge(f_scale, 1)
            with act.Fori(0, NB // 2) as i:
                for u in range(2):
                    b = 2 * i + u
                    hold(act, f_turned, b + 1)
                    nc.scalar.activation(xqT[:, :, bass.ds(S * b, S)], bank2(u), ACT.Copy, scale=sx[:, 0:1])\
                        .then_inc(f_xqT, 1)
            with act.Fori(0, NCH) as j:
                for m in range(2 * KF):
                    hold(act, f_mm, 2 * KF * j + m + 1)
                    dst = (up if m < KF else gate)[:, m % KF, bass.ds(CH * j, CH)]
                    nc.scalar.copy(dst, bank(2 + m % UP_BANKS)).then_inc(f_ev, 1)

            def g_round(m):
                g = gate[:, m, :]
                nc.scalar.activation(g, g, ACT.Identity, scale=sug[:, 1, 1:2], bias=magic[:]).then_inc(f_g1, 1)

            def g_sigmoid(m, u):
                hold(act, f_g2, m + 1)
                nc.scalar.activation(sig[:, u, :], gate[:, m, :], ACT.Sigmoid).then_inc(f_sig, 1)
                hold(act, f_sig, m + 1)
                nc.scalar.activation(sig[:, u, :], sig[:, u, :], ACT.Identity, scale=65536.0, bias=magic[:])\
                    .then_inc(f_s1, 1)

            act.wait_ge(f_scale, 2)
            act.wait_ge(const_ready, 1)
            g_round(0)
            with act.Fori(0, KF // 2 - 1) as i:
                for u in range(2):
                    g_round(2 * i + u + 1)
                    g_sigmoid(2 * i + u, u)
            g_round(KF - 1)
            g_sigmoid(KF - 2, 0)
            g_sigmoid(KF - 1, 1)
            act.wait_ge(f_scale, 3)
            with act.Fori(0, KF) as m:
                g = gate[:, m, :]
                v = up[:, m, :]
                nc.scalar.activation(g, g, ACT.Identity, scale=sp[:, 1:2], bias=magic[:]).then_inc(f_p1, 1)
                nc.scalar.activation(v, v, ACT.Identity, scale=sug[:, 1, 0:1], bias=magic[:]).then_inc(f_p1, 1)
            act.wait_ge(f_scale, 4)

            def o_round(j, u):
                nc.scalar.activation(oq[:, u], gate[:, :, bass.ds(CH * j, CH)], ACT.Identity, scale=so[:, 1:2],
                                     bias=magic[:]).then_inc(f_o1, 1)

            for j in range(2):
                o_round(j, j)
            with act.Fori(1, NCH // 2) as i:
                for u in range(2):
                    j = 2 * i + u
                    hold(act, f_down, 2 * j - 2)
                    o_round(j, u)

            act.wait_ge(ld_c, 32)

            def c_turned_out(b, u):
                hold(act, c_turned, b + 1)
                nc.scalar.copy(xnT[:, u].rearrange("p k s -> p (k s)"), bank(u)).then_inc(c_xnT, 1)

            def c_query(b, u):
                hold(act, c_qmm, b + 1)
                for k in range(KD):
                    nc.scalar.activation(qx[:, u, k, :], bank2(2)[:, k, :], ACT.Identity, bias=b1x[:, k:k + 1]).then_inc(c_q, 1)

            def c_exps(b, u):
                hold(act, c_nmax, b + 1)
                for t in range(2):
                    nc.scalar.activation(px[:, u, t, :], px[:, u, t, :], ACT.Exp, bias=cnm[:, u, t:t + 1],
                                         accum_out=cz[:, u, t:t + 1]).then_inc(c_exp, 1)

            def c_weights(b, u):
                hold(act, c_pturn, b + 1)
                nc.scalar.copy(pxT[:, u].rearrange("p k s -> p (k s)"), bank(4)).then_inc(c_pT, 1)

            c_turned_out(0, 0)
            c_turned_out(1, 1)
            c_query(0, 0)
            c_exps(0, 0)
            with act.Fori(0, NB // 2 - 1) as i:
                for u in range(2):
                    b = 2 * i + u
                    c_query(b + 1, 1 - u)
                    c_weights(b, u)
                    c_exps(b + 1, 1 - u)
                    c_turned_out(b + 2, u)
            c_query(NB - 1, 1)
            c_weights(NB - 2, 0)
            c_exps(NB - 1, 1)
            c_weights(NB - 1, 1)

            def m_turned_out(b, u):
                hold(act, m_turned, b + 1)
                nc.scalar.copy(xnT[:, u].rearrange("p k s -> p (k s)"), bank(0)).then_inc(m_xnT, 1)

            def m_gexp(b):
                hold(act, m_d, b + 1)
                nc.scalar.activation(te[:], td[:], ACT.Exp).then_inc(m_e, 1)

            def m_hots(b, u):
                hold(act, m_hturn, b + 1)
                nc.scalar.copy(hotTb, ps[0:EA, 0, :]).then_inc(m_hT, 1)
                nc.scalar.copy(hotT, ps[0:EA, 0, :]).then_inc(m_hT, 1)
                nc.scalar.copy(GT[:, u, :], ps[0:EA, 1, 0:S]).then_inc(m_hT, 1)

            def m_masks(b, u):
                for e in range(EA):
                    hold(act, m_maskmm, 8 * b + e + 1)
                    nc.scalar.copy(mask[:, u, e], bank2(2 + e % 2)).then_inc(m_mask, 1)

            def m_key(b):
                hold(act, m_kmm, b + 1)
                nc.scalar.activation(kT, ps[:, 0, 0:S], ACT.Identity, bias=kb[:]).then_inc(m_k, 1)

            def m_exps(b):
                hold(act, m_nmax, b + 1)
                for n in range(4):
                    p_ = pm[:, n // 2, n % 2, :]
                    nc.scalar.activation(p_, p_, ACT.Exp, scale=float(HD) ** -0.5, bias=mnm[:, n:n + 1],
                                         accum_out=mz[:, n:n + 1]).then_inc(m_exp, 1)

            def m_weights(b):
                hold(act, m_pturn, b + 1)
                for k in range(2):
                    nc.scalar.copy(pmT[:, k, :], bank(4 + k)).then_inc(m_pT, 1)

            def m_band(b, first):
                hold(act, m_rmm, b + 1)
                if not first:
                    hold(act, m_rout, 32 * b)
                for t in range(2):
                    nc.scalar.copy(R[:, t], ps[:, 4 + t, 0:2 * RELW].rearrange("p (j c) -> p j c", j=2)).then_inc(m_r, 1)

            act.wait_ge(ld_m, 16 * 16)
            m_turned_out(0, 0)
            m_gexp(0)
            m_hots(0, 0)
            m_masks(0, 0)
            m_key(0)
            m_turned_out(1, 1)
            m_band(0, True)
            m_gexp(1)

            def m_step(b, u, more):
                m_hots(b + 1, 1 - u)
                m_masks(b + 1, 1 - u)
                m_exps(b)
                m_key(b + 1)
                m_weights(b)
                if more:
                    m_turned_out(b + 2, u)
                m_band(b + 1, False)
                if more:
                    m_gexp(b + 2)

            with act.Fori(0, NB // 2 - 1) as i:
                for u in range(2):
                    m_step(2 * i + u, u, True)
            m_step(NB - 2, 0, False)
            m_exps(NB - 1)
            m_weights(NB - 1)

            act.wait_ge(ld_e, 48)
            act.wait_ge(m_omm, NB)
            nc.scalar.copy(w1h[:], w1).then_inc(w_high, 1)

            def n_turned_out(b, u, first):
                hold(act, n_turned, b + 1)
                if not first:
                    hold(act, n_all, b - 1)
                    hold(act, n_log, b - 1)
                nc.scalar.copy(xnT[:, u].rearrange("p k s -> p (k s)"), bank(4 + u)).then_inc(n_xnT, 1)
                nc.scalar.copy(xmh[:, :, bass.ds(S * b, S)], bank2(4 + u)).then_inc(n_xnT, 1)

            n_turned_out(0, 0, True)
            n_turned_out(1, 1, True)
            with act.Fori(1, NB // 2) as i:
                for u in range(2):
                    n_turned_out(2 * i + u, u, False)
            act.wait_ge(m_cE, 2 * NB)
            nc.scalar.copy(w2h[:], w2).then_inc(w_high, 1)
            act.wait_ge(n_d, 1)
            nc.scalar.activation(nte, ntd, ACT.Exp).then_inc(n_e, 1)
            with act.Fori(0, NCH) as j:
                hold(act, n_gturn, j + 1)
                nc.scalar.copy(GTa[:, bass.ds(CH * j, CH)], ps[0:EF, 6, :]).then_inc(n_GT, 1)

            with act.Fori(0, NCH) as j:
                for e in range(EF):
                    hold(act, e_hg, EF * j + e + 1)
                    if e >= 3:
                        hold(act, e_ymm, EF * j + e - 2)
                    nc.scalar.activation(hrh[:, e % 3, :], hg[:, e % 3, :], ACT.Relu).then_inc(e_h, 1)
                hold(act, e_ymm, EF * j + EF)
                nc.scalar.copy(yT, ps[:, 4:6, :]).then_inc(e_y, 1)

        @block.tensor
        def _(pe):
            mm = nc.tensor.matmul

            def turn(dst_bank, src, done):
                for k in range(KD):
                    for t in range(2):
                        ins = nc.tensor.transpose(ps[:, dst_bank, k * S + t * P:k * S + t * P + P],
                                                  src[t][:, k * P:(k + 1) * P], ident[:])
                ins.then_inc(done, 1)

            def a_turn(b, u):
                pe.wait_ge(a_xn, 2 * b + 2)
                turn(u, [xn[:, u, t, :] for t in range(2)], a_turned)

            def a_product(b, u):
                pe.wait_ge(a_xnT, b + 1)
                for t in range(2):
                    o = ps[:, 2 + u, t * D:(t + 1) * D]
                    for k in range(KD):
                        mm(o, xnT[:, u, k, t * P:(t + 1) * P], w0[:, k, :], start=(k == 0), stop=False)
                    ins = mm(o, ones1[:], rb[:, b, :], start=False, stop=True)
                ins.then_inc(a_mm, 1)

            pe.wait_ge(const_ready, 1)
            a_turn(0, 0)
            pe.wait_ge(ld_w0, 32)
            pe.wait_ge(csum_ready, 1)
            for b in range(NB):
                for k in range(KD):
                    ins = mm(ps[0:1, 4 + b // 2, b % 2 * D:(b % 2 + 1) * D], csum[:, k, b:b + 1], w0[:, 2 + k, :],
                             start=(k == 0), stop=(k == 1))
            ins.then_inc(rb_mm, 1)
            pe.wait_ge(rb_ready, 1)
            with pe.Fori(0, NB // 2 - 1) as i:
                for u in range(2):
                    a_turn(2 * i + u + 1, 1 - u)
                    a_product(2 * i + u, u)
            a_turn(NB - 1, 1)
            a_product(NB - 2, 0)
            a_product(NB - 1, 1)
            pe.wait_ge(wdq, 1)
            for n in range(9):
                if n >= 4:
                    pe.wait_ge(w_ready, n - 3)
                for k in range(2):
                    for c in range(2):
                        if n < 6:
                            src = wnat[:, 6 * (n // 3) + 2 * (n % 3) + c, k * P:(k + 1) * P]
                        else:
                            m = 2 * (n - 6) + k
                            src = wnat[:, 12 + 3 * c + m // 2, (m % 2) * P:(m % 2 + 1) * P]
                        ins = nc.tensor.transpose(ps[:, 4 + n % 4, k * 256 + c * P:k * 256 + c * P + P], src, ident[:])
                ins.then_inc(w_turned, 1)

            def f_turn(b, u):
                pe.wait_ge(f_xq, b + 1)
                turn(u, [xn[:, u, t, :] for t in range(2)], f_turned)

            f_turn(0, 0)
            f_turn(1, 1)
            with pe.Fori(1, NB // 2) as i:
                for u in range(2):
                    b = 2 * i + u
                    pe.wait_ge(f_xqT, b - 1)
                    f_turn(b, u)

            def upgate(j, first):
                pe.wait_ge(f_xqT, 2 * j + 2)
                for m in range(2 * KF):
                    if not (first and m < UP_BANKS):
                        pe.wait_ge(f_ev, 2 * KF * j + m + 1 - UP_BANKS)
                    for k in range(KD):
                        ins = mm(bank(2 + m % UP_BANKS), wT[:, m // KF, k, m % KF * P:(m % KF + 1) * P],
                                 xqT[:, k, bass.ds(CH * j, CH)], start=(k == 0), stop=(k == KD - 1))
                    ins.then_inc(f_mm, 1)

            pe.wait_ge(w_ready, 9)
            upgate(0, True)
            with pe.Fori(1, NCH) as j:
                upgate(j, False)

            def down(j, u, first):
                pe.wait_ge(f_oq, j + 1)
                for h in range(2):
                    if not first:
                        pe.wait_ge(f_x2, 2 * j + h - 3)
                    for t in range(2):
                        for m in range(KF):
                            c = (2 * h + t) * P
                            ins = mm(ps[:, 2 * u + h, t * D:(t + 1) * D], oq[:, u, m, c:c + P], wdT[:, m, :],
                                     start=(m == 0), stop=(m == KF - 1))
                    ins.then_inc(f_down, 1)

            down(0, 0, True)
            down(1, 1, True)
            with pe.Fori(1, NCH // 2) as i:
                for u in range(2):
                    down(2 * i + u, u, False)

            def c_turn(b, u):
                pe.wait_ge(c_xn, 2 * b + 2)
                turn(u, [xn[:, u, t, :] for t in range(2)], c_turned)

            def c_qproduct(b, u):
                pe.wait_ge(c_xnT, b + 1)
                for h in range(2):
                    for k in range(KD):
                        ins = mm(bank2(2)[:, h, :], w1x[:, k, h * P:(h + 1) * P], xnT[:, u, k, :],
                                 start=(k == 0), stop=(k == 1))
                ins.then_inc(c_qmm, 1)

            def c_scores(b, u):
                pe.wait_ge(c_q, 2 * b + 2)
                for t in range(2):
                    for k in range(KD):
                        ins = mm(bank2(3)[:, t, :], qx[:, u, k, t * P:(t + 1) * P], keysT[:, k, bass.ds(S * b, S)],
                                 start=(k == 0), stop=(k == 1))
                ins.then_inc(c_smm, 1)

            def c_pturns(b, u):
                pe.wait_ge(c_exp, 2 * b + 2)
                turn(4, [px[:, u, t, :] for t in range(2)], c_pturn)

            def c_context(b, u):
                pe.wait_ge(c_pT, b + 1)
                for t in range(2):
                    for k in range(2):
                        ins = mm(bank2(5 + u)[:, t, :], pxT[:, u, k, t * P:(t + 1) * P], kvals[:, 2 * b + k, :],
                                 start=(k == 0), stop=(k == 1))
                ins.then_inc(c_pv, 1)

            c_turn(0, 0)
            c_turn(1, 1)
            pe.wait_ge(ld_c, 32)
            c_qproduct(0, 0)
            pe.wait_ge(ld_kT, 16)
            c_scores(0, 0)
            pe.wait_ge(v_ready, 4)
            with pe.Fori(0, NB // 2 - 1) as i:
                for u in range(2):
                    b = 2 * i + u
                    c_qproduct(b + 1, 1 - u)
                    c_pturns(b, u)
                    c_scores(b + 1, 1 - u)
                    c_context(b, u)
                    c_turn(b + 2, u)
            c_qproduct(NB - 1, 1)
            c_pturns(NB - 2, 0)
            c_scores(NB - 1, 1)
            c_context(NB - 2, 0)
            c_pturns(NB - 1, 1)
            c_context(NB - 1, 1)

            def logits(b, u, w, ne, log):
                for t in range(2):
                    for k in range(KD):
                        ins = mm(ps[:, 0, ne * t:ne * t + ne], xnT[:, u, k, t * P:(t + 1) * P], w[:, k, :],
                                 start=(k == 0), stop=(k == 1))
                ins.then_inc(log, 1)

            def m_input(b, u):
                pe.wait_ge(m_xn, b + 1)
                turn(0, [xn[:, u, t, :] for t in range(2)], m_turned)
                pe.wait_ge(m_xnT, b + 1)
                logits(b, u, gw, EA, m_log)

            def m_hotturn(b, u):
                pe.wait_ge(m_gate, 2 * b + 2)
                for j in range(2):
                    for t in range(2):
                        nc.tensor.transpose(ps[0:EA, 0, j * S + t * P:j * S + t * P + P], hot[:, u, t, j, 0:EA], ident[:])
                for t in range(2):
                    ins = nc.tensor.transpose(ps[0:EA, 1, t * P:t * P + P], G[:, u, t, 0:EA], ident[:])
                ins.then_inc(m_hturn, 1)

            def m_maskproduct(b, u, first):
                pe.wait_ge(m_hT, 3 * b + 1)
                for e in range(EA):
                    if e == 1 and not first:
                        pe.wait_ge(m_out, b - 1)
                    if e >= 2:
                        pe.wait_ge(m_mask, 8 * b + e - 1)
                    mm(bank(2 + e % 2), sel8[:, e, :], hotTb, start=True, stop=True).then_inc(m_maskmm, 1)
                    if e in (1, 2, 3):
                        m_kv(b, u, e - 1)

            def m_kv(b, u, part):
                if part == 0:
                    pe.wait_ge(m_hT, 3 * b + 3)
                for k in range(KD if part == 0 else 0):
                    ins = mm(ps[:, 0, 0:S], kw[:, k, :], xnT[:, u, k, :], start=(k == 0), stop=(k == 1))
                if part == 0:
                    ins.then_inc(m_kmm, 1)
                for t in ((), (0,), (1,))[part]:
                    for k in range(KD):
                        ins = mm(ps[:, 1, t * HD:(t + 1) * HD], xnT[:, u, k, t * P:(t + 1) * P], vw[:, k, :],
                                 start=(k == 0), stop=(k == 1))
                if part == 2:
                    ins.then_inc(m_vmm, 1)

            def m_queries(b, u, half):
                for e in range(4 * half, 4 * half + 4):
                    if e % 2 == 0:
                        if e < 4:
                            pe.wait_ge(m_mask, 8 * b + 7 + e // 2)
                        else:
                            pe.wait_ge(m_qsel, 8 * b + e - 2)
                    for k in range(KD):
                        ins = mm(bank2(2 + e // 2 % 2)[:, e % 2, :], qw[:, k, e * HD:(e + 1) * HD], xnT[:, u, k, :],
                                 start=(k == 0), stop=(k == 1))
                    if e % 2:
                        ins.then_inc(m_qmm, 1)
                if half:
                    pe.wait_ge(m_qsel, 8 * b + 6)
                    mm(bank(2), qb[:], hotT, start=True, stop=True).then_inc(m_qmm, 1)

            def m_bandproduct(b):
                pe.wait_ge(m_qT, b + 1)
                for t in range(2):
                    for j in range(2):
                        ins = mm(ps[:, 4 + t, j * RELW:(j + 1) * RELW], qT[:, j, t * P:(t + 1) * P], relx[:, t, :],
                                 start=True, stop=True)
                ins.then_inc(m_rmm, 1)

            def m_scores(b):
                pe.wait_ge(m_k, b + 1)
                for j in range(2):
                    for t in range(2):
                        ins = mm(bank2(6 + j)[:, t, :], qT[:, j, t * P:(t + 1) * P], kT, start=True, stop=True)
                ins.then_inc(m_smm, 1)

            def m_pturns(b):
                pe.wait_ge(m_p, 4 * b + 4)
                for k in range(2):
                    for n in range(4):
                        ins = nc.tensor.transpose(ps[:, 4 + k, n * P:(n + 1) * P], pm[:, n // 2, n % 2, k * P:(k + 1) * P],
                                                  ident[:])
                ins.then_inc(m_pturn, 1)

            def m_context(b, u):
                pe.wait_ge(m_pT, 2 * b + 2)
                for k in range(2):
                    ins = mm(bank(1), val[:, u, k, :], pmT[:, k, :], start=(k == 0), stop=(k == 1))
                ins.then_inc(m_pv, 1)

            def m_output(b, u):
                pe.wait_ge(m_cE, 2 * b + 2)
                for t in range(2):
                    for e in range(EA):
                        mm(bank2(3)[:, t, :], ctxE[:, e, t * P:(t + 1) * P], ow[:, e, :], start=(e == 0), stop=False)
                    ins = mm(bank2(3)[:, t, :], GT[:, u, t * P:(t + 1) * P], ob[:], start=False, stop=True)
                ins.then_inc(m_omm, 1)

            pe.wait_ge(ld_m, 16 * 16)
            pe.wait_ge(ld_q, 48)
            pe.wait_ge(selz, 1)
            m_input(0, 0)
            m_hotturn(0, 0)
            m_maskproduct(0, 0, True)
            m_queries(0, 0, 0)
            m_queries(0, 0, 1)
            pe.wait_ge(m_k, 1)
            m_input(1, 1)
            m_bandproduct(0)
            m_scores(0)

            def m_step(b, u, more, first):
                m_hotturn(b + 1, 1 - u)
                m_maskproduct(b + 1, 1 - u, first)
                m_queries(b + 1, 1 - u, 0)
                m_pturns(b)
                m_queries(b + 1, 1 - u, 1)
                m_context(b, u)
                if more:
                    pe.wait_ge(m_k, b + 2)
                    m_input(b + 2, u)
                m_bandproduct(b + 1)
                m_scores(b + 1)
                m_output(b, u)

            m_step(0, 0, True, True)
            m_step(1, 1, True, False)
            with pe.Fori(1, NB // 2 - 1) as i:
                for u in range(2):
                    m_step(2 * i + u, u, True, False)
            m_step(NB - 2, 0, False, False)
            m_pturns(NB - 1)
            m_context(NB - 1, 1)
            pe.wait_ge(m_out, NB - 1)
            m_output(NB - 1, 1)

            def n_input(b, u):
                pe.wait_ge(n_xn, b + 1)
                for k in range(KD):
                    for t in range(2):
                        ins = nc.tensor.transpose(ps[:, 4 + u, k * S + t * P:k * S + t * P + P],
                                                  nxn[:, 2 * b + t, k * P:(k + 1) * P], ident[:])
                ins.then_inc(n_turned, 1)

            def n_logits(b, u):
                pe.wait_ge(n_xnT, 2 * b + 2)
                for t in range(2):
                    for k in range(KD):
                        ins = mm(ps[:, 3, bass.ds(EF * (2 * b + t), EF)], xnT[:, u, k, t * P:(t + 1) * P], gw2[:, k, :],
                                 start=(k == 0), stop=(k == 1))
                ins.then_inc(n_log, 1)

            pe.wait_ge(m_out, NB)
            n_input(0, 0)
            n_input(1, 1)
            for b in range(NB):
                n_logits(b, b % 2)
                if b + 2 < NB:
                    n_input(b + 2, b % 2)
            pe.wait_ge(n_gate, 1)
            for j in range(NCH):
                if j:
                    pe.wait_ge(n_GT, j)
                for t in range(4):
                    ins = nc.tensor.transpose(ps[0:EF, 6, t * P:t * P + P], nG[:, 4 * j + t, :], ident[:])
                ins.then_inc(n_gturn, 1)

            def split_product(out_, w, v, start, stop):
                for n, (w_, v_) in enumerate(((0, 0), (1, 0), (0, 1))):
                    ins = mm(out_, w[w_], v[v_], start=start and n == 0, stop=stop and n == 2, skip_group_check=True)
                return ins

            def e_hidden(j, e):
                n = EF * j + e
                if e >= 3:
                    pe.wait_ge(e_hg, n - 2)
                c = bass.ds(CH * j, CH)
                for k in range(KD):
                    ins = split_product(bank(e % 3), [w_[:, k, e * FH:(e + 1) * FH] for w_ in (w1h, w1l)],
                                        [x_[:, k, c] for x_ in (xmh, xml)], k == 0, k == KD - 1)
                ins.then_inc(e_hmm, 1)

            def e_out(j, e):
                pe.wait_ge(e_l, EF * j + e + 1)
                for h in range(2):
                    ins = split_product(bank(4 + h), [w_[:, e, h * P:(h + 1) * P] for w_ in (w2h, w2l)],
                                        [h_[:, e % 3, :] for h_ in (hrh, hrl)], e == 0, False)
                if e == EF - 1:
                    for h in range(2):
                        ins = mm(bank(4 + h), b2[:, h * P:(h + 1) * P], GTa[:, bass.ds(CH * j, CH)], start=False, stop=True,
                                 skip_group_check=True)
                ins.then_inc(e_ymm, 1)

            pe.wait_ge(w_low, 2)
            pe.wait_ge(n_all, NB)
            pe.wait_ge(n_GT, NCH)
            with pe.Fori(0, NCH) as j:
                e_hidden(j, 0)
                e_hidden(j, 1)
                for e in range(EF):
                    if e + 2 < EF:
                        e_hidden(j, e + 2)
                    e_out(j, e)
                pe.wait_ge(e_y, j + 1)
                for t in range(4):
                    for k in range(KD):
                        ins = nc.tensor.transpose(bank2(6 + t // 2)[:, t % 2, k * P:(k + 1) * P], yT[:, k, t * P:(t + 1) * P],
                                                  ident[:])
                    if t % 2:
                        ins.then_inc(e_yturn, 1)


def kernel(**inputs):
    import concourse.bacc as bacc
    from concourse.bass_utils import run_bass_kernel_spmd as run

    a = {k: np.asarray(v) for k, v in inputs.items()}
    a["ctxT"] = np.ascontiguousarray(a["ctx_1024"].reshape(N, D).T)
    a["L0_xattn_WT"] = np.ascontiguousarray(a["L0_xattn_W"].T)
    a["L1_xattn_WT"] = np.ascontiguousarray(a["L1_xattn_W"].T)
    a["xattn1_bT"] = np.ascontiguousarray(a["L1_xattn_b"].reshape(KD, P).T)
    a["ff_b1T"] = np.ascontiguousarray(a["L1_ffn_ff_b1"].T)
    relT = a["L1_ffn_rel_table"].T
    band = [np.clip(np.arange(RELW) - (P - 1), -MAXP, MAXP) + MAXP, np.clip(np.arange(RELW) - MAXP, -MAXP, MAXP) + MAXP]
    a["relx"] = np.ascontiguousarray(relT[:, np.stack(band)])
    a["rele"] = np.ascontiguousarray(relT[:, [2 * MAXP, 0]])
    names = ["x", "g_xattn", "g_ffn", "ctxT", "L0_xattn_WT", "L0_xattn_b", "L0_ffn_w_up", "L0_ffn_w_gate",
             "L0_ffn_w_down", "L1_xattn_WT", "xattn1_bT", "ctx_1024", "ff_b1T", "relx", "rele"]
    names += ["L1_ffn_" + n for n in ("ln1_w", "ln1_b", "ln2_w", "ln2_b", "attn_gate_w", "q_w", "q_b", "k_w", "k_b", "v_w",
                                      "v_b", "o_w", "o_b", "ff_gate_w", "ff_w1", "ff_w2", "ff_b2")]
    nc = bacc.Bacc("TRN2", target_bir_lowering=False, num_devices=1)
    arrays, args = {}, {}
    for name in names:
        v = np.ascontiguousarray(a[name])
        arrays[f"in_{name}"] = v
        args[name] = nc.dram_tensor(f"in_{name}", v.shape, mybir.dt.from_np(v.dtype), kind="ExternalInput").ap()
    args["skew"] = nc.dram_tensor("skew", (4, P, RELROW), F32, kind="Internal").ap()
    args["gscr"] = nc.dram_tensor("gscr", (EF, N), F32, kind="Internal").ap()
    out = nc.dram_tensor("out", (NB, S, D), F32, kind="ExternalOutput").ap()
    gated_block_kernel(nc, args, out)
    r = run(nc, [arrays], core_ids=[0])
    return r.results[0]["out"]
```

```python
from contextlib import ExitStack

import numpy as np

import concourse.bass as bass
from concourse import mybir

F32 = mybir.dt.float32
BF16 = mybir.dt.bfloat16
U16 = mybir.dt.uint16
U32 = mybir.dt.uint32
F32R = mybir.dt.float32r
ALU = mybir.AluOpType
ACT = mybir.ActivationFunctionType
AX = mybir.AxisListType
RMAX = bass.bass_isa.ReduceOp.max

P = 128
NB, S, D = 8, 256, 256
N = NB * S
NT = N // P
KD = D // P
FF = 768
KF = FF // P
BLK = 32
EA, HD, MAXP = 8, 128, 64
EF, FH = 16, 128
EPS = 1e-5
MAGIC = 12582912.0
QMAX = 32767.0
CH = 512
NCH = N // CH
RELW = 192
RELROW = 384
UP_BANKS = 6


def hold(eng, sem, value):
    eng.wait_ge(sem, value)
    eng.nop(nofuse=True)


def chained(eng, sem, before):
    count = [0]

    def link(ins):
        count[0] += 1
        ins.then_inc(sem, 1)
        hold(eng, sem, before + count[0])
    return link


def weave(*parts):
    parts = list(parts)
    while parts:
        for part in list(parts):
            if next(part, "end") == "end":
                parts.remove(part)


def gated_block_kernel(nc, a, out):
    with ExitStack() as ctx:
        base = {}

        def sb(name, shape, dt=F32):
            base[name] = -(-nc.sbuf_base // 32) * 32
            return ctx.enter_context(nc.sbuf_tensor(name, shape, dt))

        def over(name, shape, at, floats=0):
            return nc.alloc_sbuf_tensor_at(name, shape, F32R, offset=base[at] + 4 * floats)

        def sem(name):
            return ctx.enter_context(nc.semaphore(name))

        ps = ctx.enter_context(nc.psum_tensor("ps", [P, 8, 512], F32))
        x = sb("x", [P, NT, D])
        lnb = sb("lnb", [P, NT, D])
        xqT = sb("xqT", [P, KD, N])
        up = sb("up", [P, KF, N])
        gate = sb("gate", [P, KF, N])
        ctxT = gate[:, 0:2, :]
        w0 = gate[:, 2, 0:4 * D].rearrange("p (k e) -> p k e", k=4)
        b0 = gate[0:NB, 3, 0:D]
        rb = gate[0:NB, 3, D:2 * D]
        rbl = gate[0:NB, 3, 2 * D:3 * D]
        w0h = over("w0h", [P, KD, D], "gate", 4 * N); w0l = over("w0l", [P, KD, D], "gate", 4 * N + 512)
        xTh = over("xTh", [P, 2, KD, S], "gate", 4 * N + 1024); xTl = over("xTl", [P, 2, KD, S], "gate", 5 * N)
        rbh = over("rbh", [NB, D], "gate", 5 * N + 1280)
        ones = over("ones", [NB, P], "gate", 5 * N + 1024)
        rbdh = over("rbdh", [NB, NB, D], "up"); rbdl = over("rbdl", [NB, NB, D], "up", 4 * N)
        csum = sb("csum", [P, KD, NB])
        gates = sb("gates", [P, 4])
        tg = sb("tg", [P, 4])
        wnat = up[:, 1:4, :].rearrange("p m n -> p (m n)")[:, 0:18 * D].rearrange("p (g n) -> p g n", n=D)
        wabs = sb("wabs", [P, 144])
        winv = sb("winv", [P, 144])
        wT = sb("wT", [P, 2, KD, FF])
        wdT = sb("wdT", [P, KF, D])
        ident = sb("ident", [P, P])
        ones1 = sb("ones1", [NB, P])
        magic = sb("magic", [P, 1]); one = sb("one", [P, 1])
        neghalf = sb("neghalf", [P, 2])
        st = sb("st", [P, 2, 6])
        mv = sb("mv", [P, 2, 2, 2])
        ve = sb("ve", [P, 2, 2])
        rs = sb("rs", [P, 2, 2])
        xn = sb("xn", [P, 2, 2, D])
        xnT = sb("xnT", [P, 2, KD, S])
        ln = sb("ln", [P, 4, D])
        w1x = sb("w1x", [P, KD, D])
        kw = sb("kw", [P, KD, HD]); vw = sb("vw", [P, KD, HD])
        st16 = sb("st16", [P, NT, 6]); mv16 = sb("mv16", [P, NT, 2]); ve16 = sb("ve16", [P, NT]); rs16 = sb("rs16", [P, NT])
        amx = sb("amx", [P, 64])
        pmax = sb("pmax", [P, 2])
        gmx = sb("gmx", [P, 2])
        sx = sb("sx", [P, 2])
        sug = sb("sug", [P, 2, 2])
        sp = sb("sp", [P, 2])
        so = sb("so", [P, 4])
        sig = sb("sig", [P, 2, N])
        xqh = over("xqh", [P, KD, N], "xqT"); xql = over("xql", [P, KD, N], "sig")
        wTh = over("wTh", [P, 2, KD, FF], "wT"); wTl = over("wTl", [P, 2, KD, FF], "xnT")
        orn = sig.rearrange("p u n -> p (u n)")[:, 0:KF * CH].rearrange("p (h m c) -> p h m c", h=2, m=KF // 2)
        oqh = over("oqh", [P, 2, KF, CH], "up"); oql = over("oql", [P, 2, KF, CH], "up", 2 * KF * CH)
        wdh = over("wdh", [P, KF, D], "wT"); wdl = over("wdl", [P, KF, D], "wdT")

        kvals = lnb
        keysT = xqT
        b1x = sb("b1x", [P, KD])
        infm = xn.rearrange("p u t d -> p (u t d)").bitcast(U32).rearrange("p (t d) -> p t d", t=4)
        zero = sb("zero", [P, 1])
        c_buf = sig.rearrange("p u n -> p (u n)")
        qx = c_buf[:, 0:1024].rearrange("p (u e s) -> p u e s", u=2, e=KD)
        px = c_buf[:, 1024:2048].rearrange("p (u t s) -> p u t s", u=2, t=2)
        pxT = c_buf[:, 2048:3072].rearrange("p (u k s) -> p u k s", u=2, k=2)
        cmx = sb("cmx", [P, 2, 2]); cnm = sb("cnm", [P, 2, 2]); cz = sb("cz", [P, 2, 2]); crz = sb("crz", [P, 2, 2])
        gflat = gate.rearrange("p m n -> p (m n)")
        qw = gflat[:, 0:2048].rearrange("p (k e) -> p k e", k=KD)
        ow = gflat[:, 2048:4096].rearrange("p (e d) -> p e d", e=EA)
        w1 = gflat[:, 4096:8192].rearrange("p (k f) -> p k f", k=KD)
        w2 = gflat[:, 8192:12288].rearrange("p (e d) -> p e d", e=EF)
        inner = up[:, 0:2, :].rearrange("p a n -> p (a n)").rearrange("p (t d) -> p t d", d=D)
        nxn = up[:, 2:4, :].rearrange("p a n -> p (a n)").rearrange("p (t d) -> p t d", d=D)
        gw = sb("gw", [P, KD, EA])
        gw2 = sb("gw2", [P, KD, EF]); qb = sb("qb", [EA, HD]); ob = sb("ob", [EA, D]); b2 = sb("b2", [EF, D])
        kb = sb("kb", [P, 1]); vb = sb("vb", [P, HD]); b1 = sb("b1", [P, EF])
        relx = sb("relx", [P, 2, RELW]); rele = sb("rele", [P, 2])
        iota = sb("iota", [P, EF]); sel8 = sb("sel8", [EA, EA, P], BF16)
        ghot = sb("ghot", [P, 2, 2, 2, EF])
        G = sb("G", [P, 2, 2, EF])
        hot = sb("hot", [P, 2, 2, 2, EF])
        top = sb("top", [P, 2, 8]); tidx = sb("tidx", [P, 2, 8], U32); tif = sb("tif", [P, 2, 2])
        td = sb("td", [P, 2]); te = sb("te", [P, 2]); gj = sb("gj", [P, 2, 2, 2])
        wdflat = wdT.rearrange("p m d -> p (m d)")
        hotT = wdflat[0:EA, 0:512]; hotTb = wdflat[0:EA, 512:768].bitcast(BF16)
        GT = wdflat[0:EA, 768:1280].rearrange("p (u s) -> p u s", u=2)
        xnTh = over("xnTh", [P, 2, KD, S], "xnT"); xnTl = over("xnTl", [P, 2, KD, S], "xqT", 3072)
        qwh = over("qwh", [P, KD, EA * HD], "wT"); qwl = over("qwl", [P, KD, EA * HD], "gate")
        kwh = over("kwh", [P, KD, HD], "wT", 2048); kwl = over("kwl", [P, KD, HD], "kw")
        vwh = over("vwh", [P, KD, HD], "wT", 2304); vwl = over("vwl", [P, KD, HD], "vw")
        gwh = over("gwh", [P, KD, EA], "st16", 64); gwl = over("gwl", [P, KD, EA], "st16", 80)
        mask = up[:, 4:6, :].rearrange("p a n -> p (a n)").bitcast(BF16)\
            .rearrange("p (u e j s) -> p u e j s", u=2, e=EA, j=2)
        lflat = lnb.rearrange("p t d -> p (t d)")
        xflat = xqT.rearrange("p k n -> p (k n)")
        qsel = lflat[:, 0:512].rearrange("p (j s) -> p j s", j=2)
        qT = lflat[:, 512:1024].rearrange("p (j s) -> p j s", j=2)
        kT = lflat[:, 1024:1280]
        val = lflat[:, 1280:1792].rearrange("p (u k h) -> p u k h", u=2, k=2)
        R = lflat[:, 1792:2560].rearrange("p (t j c) -> p t j c", t=2, j=2)
        B = xflat[:, 0:1024].rearrange("p (j t s) -> p j t s", j=2, t=2)
        pm = xflat[:, 1024:2048].rearrange("p (j t s) -> p j t s", j=2, t=2)
        pmT = xflat[:, 2048:3072].rearrange("p (k c) -> p k c", k=2)
        ctxE = c_buf[:, 0:2048].rearrange("p (e s) -> p e s", e=EA)
        zrow = c_buf[:, 2048:2048 + RELW]
        w1h = over("w1h", [P, KD, EF * FH], "gate"); w1l = over("w1l", [P, KD, EF * FH], "gate", 4096)
        w2h = over("w2h", [P, EF, D], "up", 4 * N); w2l = over("w2l", [P, EF, D], "gate", 8192)
        xmh = over("xmh", [P, KD, N], "wT"); xml = over("xml", [P, KD, N], "up")
        hrh = over("hrh", [P, 3, CH], "sig", 3 * CH); hrl = over("hrl", [P, 3, CH], "xn")
        nmv = sb("nmv", [P, 2, 2, 2]); nve = sb("nve", [P, 2, 2]); nrs = sb("nrs", [P, 2, 2])
        nhot = xn[:, 0].rearrange("p t d -> p (t d)").rearrange("p (t j e) -> p t j e", t=NT, j=2)
        nghot = xn[:, 1].rearrange("p t d -> p (t d)").rearrange("p (t j e) -> p t j e", t=NT, j=2)
        def piece(at, floats):
            return c_buf[:, at:at + floats]
        ntop = piece(0, 128).rearrange("p (t m) -> p t m", t=NT)
        ntidx = piece(128, 128).bitcast(U32).rearrange("p (t m) -> p t m", t=NT)
        ntif = piece(256, 32).rearrange("p (t j) -> p t j", t=NT)
        ngj = piece(288, 32).rearrange("p (t j) -> p t j", t=NT)
        ntd = piece(320, 16); nte = piece(336, 16)
        nG = piece(352, 256).rearrange("p (t e) -> p t e", t=NT)
        mmx = sb("mmx", [P, 4]); mnm = sb("mnm", [P, 4]); mz = sb("mz", [P, 4]); mrz = sb("mrz", [P, 4])
        GTa = up[0:EF, 2, :]
        gbc = [xflat[:, 2048 * n:2048 * n + 2048] for n in range(2)] + [lflat[:, 2048 * n:2048 * n + 2048] for n in range(2)]
        gbc = [g_.rearrange("p (e c) -> p e c", e=4) for g_ in gbc]
        hg = c_buf[:, 0:3 * CH].rearrange("p (r c) -> p r c", r=3)
        yT = up[:, 3, 0:KD * CH].rearrange("p (k c) -> p k c", k=KD)
        skew = a["skew"]
        gscr = a["gscr"]

        ld_k = sem("ld_k"); ld_kT = sem("ld_kT"); ld_m = sem("ld_m"); ld_q = sem("ld_q")
        ld_e = sem("ld_e"); z_dma = sem("z_dma"); z_set = sem("z_set")
        v_step = sem("v_step")
        c_var = sem("c_var"); c_rstd = sem("c_rstd"); c_xn = sem("c_xn"); c_turned = sem("c_turned")
        c_xnT = sem("c_xnT"); c_qmm = sem("c_qmm"); c_q = sem("c_q"); c_smm = sem("c_smm"); c_max = sem("c_max")
        c_nmax = sem("c_nmax"); c_exp = sem("c_exp"); c_pturn = sem("c_pturn"); c_pT = sem("c_pT"); c_pv = sem("c_pv")
        c_rz = sem("c_rz"); c_x3 = sem("c_x3")
        m_link = sem("m_link"); m_var = sem("m_var"); m_rstd = sem("m_rstd"); m_src = sem("m_src")
        m_var2 = sem("m_var2"); m_rstd2 = sem("m_rstd2"); m_ln = sem("m_ln"); m_w = sem("m_w"); m_xn = sem("m_xn")
        m_turned = sem("m_turned"); m_xnT = sem("m_xnT"); m_xl = sem("m_xl"); m_log = sem("m_log"); m_top = sem("m_top")
        m_d = sem("m_d"); m_e = sem("m_e"); m_gate = sem("m_gate"); m_hturn = sem("m_hturn"); m_hT = sem("m_hT")
        m_maskmm = sem("m_maskmm"); m_mask = sem("m_mask"); m_kmm = sem("m_kmm"); m_k = sem("m_k"); m_vmm = sem("m_vmm")
        m_qmm = sem("m_qmm"); m_qsel = sem("m_qsel"); m_qT = sem("m_qT"); m_rmm = sem("m_rmm")
        m_r = sem("m_r"); m_rout = sem("m_rout"); m_rin = sem("m_rin"); m_smm = sem("m_smm"); m_max = sem("m_max")
        m_nmax = sem("m_nmax"); m_exp = sem("m_exp"); m_rz = sem("m_rz"); m_p = sem("m_p"); m_pturn = sem("m_pturn")
        m_pT = sem("m_pT"); m_pv = sem("m_pv"); m_cE = sem("m_cE"); m_omm = sem("m_omm"); m_out = sem("m_out")
        n_st = sem("n_st"); n_var = sem("n_var"); n_rstd = sem("n_rstd"); n_ln = sem("n_ln"); n_w = sem("n_w")
        n_xn = sem("n_xn"); n_turned = sem("n_turned"); n_xnT = sem("n_xnT"); n_all = sem("n_all"); n_log = sem("n_log")
        e_l = sem("e_l"); n_top = sem("n_top")
        w_high = sem("w_high"); w_low = sem("w_low"); n_d = sem("n_d"); n_e = sem("n_e"); n_gate = sem("n_gate"); n_gturn = sem("n_gturn")
        n_GT = sem("n_GT"); n_base = sem("n_base"); g_out = sem("g_out")
        g_in = [sem(f"g_in{n}") for n in range(4)]
        e_hmm = sem("e_hmm"); e_hg = sem("e_hg"); e_h = sem("e_h"); e_ymm = sem("e_ymm"); e_y = sem("e_y")
        e_yturn = sem("e_yturn"); e_x4 = sem("e_x4")
        ld_x = [sem(f"ld_x{h}") for h in range(4)]; a_xl = sem("a_xl"); a_w0 = sem("a_w0"); f_xl = sem("f_xl"); w_low0 = sem("w_low0")
        ld_w0 = sem("ld_w0"); ld_ctxT = sem("ld_ctxT"); ld_g = sem("ld_g")
        ld_wq = sem("ld_wq")
        const_ready = sem("const_ready"); ident_zero = sem("ident_zero")
        tanh_ready = sem("tanh_ready")
        dve0 = sem("dve0")
        csum_ready = sem("csum_ready"); rb_mm = sem("rb_mm"); rb_ready = sem("rb_ready")
        wstep = sem("wstep"); wdq = sem("wdq")
        w_turned = sem("w_turned"); w_ready = sem("w_ready")
        ln_link = sem("ln_link"); a_var = sem("a_var"); a_rstd = sem("a_rstd"); a_xn = sem("a_xn")
        a_turned = sem("a_turned"); a_xnT = sem("a_xnT"); a_ctr = sem("a_ctr"); a_mm = sem("a_mm"); a_x1 = sem("a_x1")
        f_var = sem("f_var"); f_rstd = sem("f_rstd"); f_ln = sem("f_ln")
        f_red = sem("f_red"); f_pmax = sem("f_pmax"); f_gmax = sem("f_gmax"); f_scale = sem("f_scale")
        f_q1 = sem("f_q1"); f_xq = sem("f_xq"); f_turned = sem("f_turned"); f_xqT = sem("f_xqT")
        f_mm = sem("f_mm"); f_ev = sem("f_ev")
        f_g1 = sem("f_g1"); f_g2 = sem("f_g2"); f_sig = sem("f_sig"); f_s1 = sem("f_s1")
        f_prod = sem("f_prod"); f_p1 = sem("f_p1"); f_uq = sem("f_uq")
        f_o1 = sem("f_o1"); f_oq = sem("f_oq"); f_down = sem("f_down"); f_x2 = sem("f_x2")
        stored = sem("stored")

        x_tok = a["x"].rearrange("b (t p) d -> p (b t) d", p=P)
        out_tok = out.rearrange("b (t p) d -> p (b t) d", p=P)

        def bank(n):
            return ps[:, n, :]

        def bank2(n):
            return ps[:, n, :].rearrange("p (a c) -> p a c", a=2)

        block = ctx.enter_context(nc.Block())

        @block.sync
        def _(sp_):
            for h in range(4):
                sp_.dma_start(x[:, 4 * h:4 * h + 4, :], x_tok[:, 4 * h:4 * h + 4, :]).then_inc(ld_x[h], 16)
                if h == 0:
                    sp_.dma_start(gates[:, 0:2], a["g_xattn"].partition_broadcast(P)).then_inc(ld_g, 16)
                    sp_.dma_start(gates[:, 2:4], a["g_ffn"].partition_broadcast(P)).then_inc(ld_g, 16)
                    sp_.dma_start(ctxT, a["ctxT"].rearrange("(k p) n -> p k n", p=P)).then_inc(ld_ctxT, 16)
                    sp_.dma_start(w0, a["L0_xattn_WT"].rearrange("(k p) e -> p k e", p=P)).then_inc(ld_w0, 16)
                    sp_.dma_start(b0, a["L0_xattn_b"].partition_broadcast(NB)).then_inc(ld_w0, 16)
            for n, name in enumerate(("L0_ffn_w_up", "L0_ffn_w_gate")):
                sp_.dma_start(wnat[:, 6 * n:6 * n + 6, :], a[name].rearrange("(g p) n -> p g n", p=P)).then_inc(ld_wq, 16)
            sp_.dma_start(wnat[:, 12:18, :].rearrange("p (h m) n -> p h (m n)", h=2),
                          a["L0_ffn_w_down"].rearrange("(h p) i -> p h i", p=P)).then_inc(ld_wq, 16)
            sp_.wait_ge(f_xq, NB)
            sp_.dma_start(kvals[:], a["ctx_1024"].rearrange("b (t p) d -> p (b t) d", p=P)).then_inc(ld_k, 16)
            sp_.wait_ge(f_mm, 2 * KF * NCH)
            sp_.dma_start(w1x[:], a["L1_xattn_WT"].rearrange("(k p) e -> p k e", p=P)).then_inc(ld_m, 16)
            sp_.dma_start(b1x[:], a["xattn1_bT"]).then_inc(ld_m, 16)
            for n, name in enumerate(("ln1_w", "ln1_b", "ln2_w", "ln2_b")):
                sp_.dma_start(ln[:, n, :], a["L1_ffn_" + name].partition_broadcast(P)).then_inc(ld_m, 16)
            for dst, name in ((gw, "attn_gate_w"), (kw, "k_w"), (vw, "v_w"), (gw2, "ff_gate_w")):
                sp_.dma_start(dst[:], a["L1_ffn_" + name].rearrange("(k p) e -> p k e", p=P)).then_inc(ld_m, 16)
            for dst, name in ((qb, "q_b"), (ob, "o_b"), (b2, "ff_b2")):
                sp_.dma_start(dst[:], a["L1_ffn_" + name]).then_inc(ld_m, 16)
            sp_.dma_start(kb[:], a["L1_ffn_k_b"].rearrange("(h a) -> h a", a=1)).then_inc(ld_m, 16)
            sp_.dma_start(vb[:], a["L1_ffn_v_b"].partition_broadcast(P)).then_inc(ld_m, 16)
            sp_.dma_start(b1[:], a["ff_b1T"]).then_inc(ld_m, 16)
            sp_.dma_start(relx[:], a["relx"]).then_inc(ld_m, 16)
            sp_.dma_start(rele[:], a["rele"]).then_inc(ld_m, 16)
            sp_.dma_start(keysT[:], a["ctxT"].rearrange("(k p) n -> p k n", p=P)).then_inc(ld_kT, 16)
            sp_.wait_ge(f_o1, 2 * NCH)
            sp_.dma_start(qw.rearrange("p k (e h) -> p k e h", e=EA)[:, 0], a["L1_ffn_q_w"][:, 0:P, :].rearrange("e p h -> p e h")).then_inc(ld_q, 16)
            sp_.dma_start(qw.rearrange("p k (e h) -> p k e h", e=EA)[:, 1], a["L1_ffn_q_w"][:, P:D, :].rearrange("e p h -> p e h")).then_inc(ld_q, 16)
            sp_.dma_start(ow, a["L1_ffn_o_w"].rearrange("e h d -> h e d")).then_inc(ld_q, 16)
            for k in range(KD):
                sp_.dma_start(w1[:, k, :].rearrange("p (e f) -> p e f", e=EF),
                              a["L1_ffn_ff_w1"][:, k * P:(k + 1) * P, :].rearrange("e p f -> p e f")).then_inc(ld_e, 16)
            sp_.dma_start(w2, a["L1_ffn_ff_w2"].rearrange("e f d -> f e d")).then_inc(ld_e, 16)
            sp_.wait_ge(z_set, 1)
            for jt in range(4):
                lo = (1 - jt % 2) * RELW
                sp_.dma_start(skew[jt, :, lo:lo + RELW - jt % 2], zrow[:, 0:RELW - jt % 2]).then_inc(z_dma, 16)
            sp_.wait_ge(z_dma, 64)

            def skew_batch(b, first):
                for t in range(2):
                    lo = t * (RELW - 1)
                    hold(sp_, m_r, 2 * b + t + 1)
                    if not first and t == 0:
                        hold(sp_, m_rin, 16 * b)
                    sp_.dma_start(skew.rearrange("(j t) q c -> t q j c", t=2)[t, :, :, lo:lo + RELW], R[:, t])\
                        .then_inc(m_rout, 16)
                hold(sp_, m_rout, 32 * b + 32)
                if not first:
                    hold(sp_, m_max, 4 * b)
                sp_.dma_start(B.rearrange("p j t s -> p (j t) s"),
                              bass.AP(tensor=skew.tensor, offset=skew.offset + P - 1,
                                      ap=[[RELROW - 1, P], [P * RELROW, 4], [1, S]])).then_inc(m_rin, 16)

            skew_batch(0, True)
            with sp_.Fori(1, NB) as b:
                skew_batch(b, False)

            sp_.wait_ge(n_GT, 1)
            sp_.dma_start(gscr[:, 0:CH], GTa[:, 0:CH]).then_inc(g_out, 16)
            sp_.wait_ge(g_out, 16)

            def gates_in(j, first):
                for n in range(4):
                    if not first:
                        hold(sp_, e_hg, EF * j - EF + 4 * n + 4)
                    sp_.dma_start(gbc[n], gscr[4 * n:4 * n + 4, bass.ds(CH * j, CH)].partition_broadcast(P))\
                        .then_inc(g_in[n], 16)
            gates_in(0, True)
            sp_.wait_ge(n_GT, NCH)
            sp_.dma_start(gscr[:, CH:N], GTa[:, CH:N]).then_inc(g_out, 16)
            sp_.wait_ge(g_out, 32)
            with sp_.Fori(1, NCH) as j:
                gates_in(j, False)
            with sp_.Fori(0, NCH) as j:
                hold(sp_, e_x4, 2 * j + 2)
                sp_.dma_start(out_tok[:, bass.ds(4 * j, 4), :], x[:, bass.ds(4 * j, 4), :]).then_inc(stored, 16)
            sp_.wait_ge(stored, 16 * NCH)

        @block.gpsimd
        def _(pool):
            nc.gpsimd.memset(ident[:], 0.0).then_inc(ident_zero, 1)
            nc.gpsimd.memset(neghalf[:], -0.5).then_inc(ident_zero, 1)
            nc.gpsimd.memset(magic[:], MAGIC).then_inc(ident_zero, 1)
            nc.gpsimd.memset(one[:], 1.0).then_inc(ident_zero, 1)
            nc.gpsimd.memset(ones1[:], 1.0).then_inc(ident_zero, 1)
            nc.gpsimd.memset(zero[:], 0.0).then_inc(ident_zero, 1)
            nc.gpsimd.memset(sel8[:], 0.0).then_inc(ident_zero, 1)
            nc.gpsimd.iota(iota[:], [[1, EF]], base=0, channel_multiplier=0, allow_small_or_imprecise_dtypes=True)\
                .then_inc(ident_zero, 1)
            pool.wait_ge(ident_zero, 8)
            nc.gpsimd.affine_select(out=sel8[:], in_=sel8[:], compare_op=ALU.not_equal, fill=1.0, base=0,
                                    pattern=[[1, EA], [0, P]], channel_multiplier=-1)
            nc.gpsimd.affine_select(out=ident[:], in_=ident[:], compare_op=ALU.not_equal, fill=1.0, base=0,
                                    pattern=[[-1, P]], channel_multiplier=1).then_inc(const_ready, 1)

            def ln_pow(b, u, var, rstd):
                pool.wait_ge(var, b + 1)
                nc.gpsimd.tensor_tensor(rs[:, u, :], ve[:, u, :], neghalf[:], ALU.pow).then_inc(rstd, 1)

            pool.wait_ge(const_ready, 1)
            pool.wait_ge(a_var, 1)
            nc.gpsimd.tensor_tensor(rs16[:], ve16[:], neghalf[:, 0:1].to_broadcast([P, NT]), ALU.pow).then_inc(a_rstd, 1)
            pool.wait_ge(a_rstd, 1)

            def a_norm(b, u, first=False):
                if not first:
                    hold(pool, a_turned, b - 1)
                nc.gpsimd.tensor_tensor(xn[:, u], x[:, bass.ds(2 * b, 2), :],
                                        mv16[:, bass.ds(2 * b, 2), 0:1].to_broadcast([P, 2, D]), ALU.subtract)\
                    .then_inc(a_ctr, 1)
                hold(pool, a_ctr, b + 1)
                nc.gpsimd.tensor_tensor(xn[:, u], xn[:, u], rs16[:, bass.ds(2 * b, 2)].unsqueeze(2).to_broadcast([P, 2, D]),
                                        ALU.mult).then_inc(a_xn, 1)

            a_norm(0, 0, True)
            a_norm(1, 1, True)
            def a_steps(first, end):
                with pool.Fori(first, end) as i:
                    for u in range(2):
                        a_norm(2 * i + u + 2, u)
                        ln_pow(2 * i + u, u, f_var, f_rstd)
            wv = wnat.rearrange("p g (c k) -> p (g c) k", k=BLK)
            pool.wait_ge(wstep, 3)
            nc.gpsimd.tensor_tensor(wv, wv, winv[:].unsqueeze(2).to_broadcast([P, 144, BLK]), ALU.mult).then_inc(wstep, 1)
            a_steps(0, NB // 2 - 1)
            pool.wait_ge(wstep, 6)
            nc.gpsimd.tensor_tensor(wv, wv, wabs[:].unsqueeze(2).to_broadcast([P, 144, BLK]),
                                    ALU.mult).then_inc(wdq, 1)
            ln_pow(NB - 2, 0, f_var, f_rstd)
            ln_pow(NB - 1, 1, f_var, f_rstd)
            for k in range(4):
                w = 2 if k == 1 else 1
                if k == 2:
                    pool.wait_ge(f_scale, 2)
                    for m in range(KF):
                        pool.wait_ge(f_g1, m + 1)
                        nc.gpsimd.tensor_scalar(gate[:, m, :], gate[:, m, :], -MAGIC, sug[:, 0, 1:2], ALU.add, ALU.mult)\
                            .then_inc(f_g2, 1)
                        nc.gpsimd.tensor_scalar(up[:, m, :], up[:, m, :], sug[:, 1, 0:1], MAGIC, ALU.mult, ALU.add)\
                            .then_inc(f_uq, 1)
                        pool.wait_ge(f_uq, 2 * m + 1)
                        nc.gpsimd.tensor_scalar(up[:, m, :], up[:, m, :], -MAGIC, one[:], ALU.add, ALU.mult).then_inc(f_uq, 1)
                pool.wait_ge(f_pmax, k + 1)
                nc.gpsimd.partition_all_reduce(gmx[:, 0:w], pmax[:, 0:w], P, RMAX).then_inc(f_gmax, 1)

            with pool.Fori(0, NB // 2) as i:
                for u in range(2):
                    ln_pow(2 * i + u, u, c_var, c_rstd)
            def affine(v, b, n, ln_done, w_done, xn_done):
                hold(pool, ln_done, 2 * b + 2)
                nc.gpsimd.tensor_tensor(v, v, ln[:, n, :].unsqueeze(1).to_broadcast([P, 2, D]), ALU.mult)\
                    .then_inc(w_done, 1)
                hold(pool, w_done, b + 1)
                nc.gpsimd.tensor_tensor(v, v, ln[:, n + 1, :].unsqueeze(1).to_broadcast([P, 2, D]), ALU.add)\
                    .then_inc(xn_done, 1)

            def m_in(b, u):
                ln_pow(b, u, m_var, m_rstd)
                ln_pow(b, u, m_var2, m_rstd2)
                affine(xn[:, u], b, 0, m_ln, m_w, m_xn)

            def n_pow(b, u):
                pool.wait_ge(n_var, b + 1)
                nc.gpsimd.tensor_tensor(nrs[:, u, :], nve[:, u, :], neghalf[:], ALU.pow).then_inc(n_rstd, 1)

            def n_affine(b):
                affine(nxn[:, bass.ds(2 * b, 2), :], b, 2, n_ln, n_w, n_xn)

            m_in(0, 0)
            pool.wait_ge(c_x3, NB)
            nc.gpsimd.memset(zrow, 0.0).then_inc(z_set, 1)
            m_in(1, 1)
            m_in(2, 0)
            m_in(3, 1)
            n_pow(0, 0)
            with pool.Fori(0, NB // 2 - 2) as i:
                for u in range(2):
                    b = 2 * i + u
                    m_in(b + 4, u)
                    n_affine(b)
                    n_pow(b + 1, 1 - u)
            for b in range(NB - 4, NB - 2):
                n_affine(b)
                n_pow(b + 1, 1 - b % 2)
            n_affine(NB - 2)
            n_pow(NB - 1, 1)
            n_affine(NB - 1)
            for n, (low, w_, high) in enumerate(((w1l, w1, w1h), (w2l, w2, w2h))):
                pool.wait_ge(w_high, 5 + n)
                nc.gpsimd.tensor_tensor(low[:], w_, high[:].bitcast(F32), ALU.subtract).then_inc(w_low, 1)

        @block.vector
        def _(dve):
            def ln_stats(src, b, u, chain, var, mv=mv, ve=ve, before=0):
                link = chained(dve, chain, b * 2 + before)
                nc.vector.bn_stats(st[:, 0, :], src[0])
                link(nc.vector.bn_stats(st[:, 1, :], src[1]))
                nc.vector.bn_aggr(mv[:, u, 0, :], st[:, 0, :])
                link(nc.vector.bn_aggr(mv[:, u, 1, :], st[:, 1, :]))
                nc.vector.tensor_scalar(ve[:, u, :], mv[:, u, :, 1], EPS, None, ALU.add).then_inc(var, 1)

            def ln_norm(dst, src, b, u, rstd, done, mv=mv, rs=rs):
                dve.wait_ge(rstd, b + 1)
                for t in range(2):
                    nc.vector.tensor_scalar(dst[t], src[t], mv[:, u, t, 0:1], rs[:, u, t:t + 1],
                                            ALU.subtract, ALU.mult).then_inc(done, 1)

            def tiles(buf, b):
                return [buf[:, 2 * b + t, :] for t in range(2)]

            for h in range(4):
                dve.wait_ge(ld_x[h], 16)
                for t in range(4 * h, 4 * h + 4):
                    nc.vector.bn_stats(st16[:, t, :], x[:, t, :]).then_inc(ln_link, 1)
                dve.wait_ge(ln_link, 4 * h + 4)
                for t in range(4 * h, 4 * h + 4):
                    ins = nc.vector.bn_aggr(mv16[:, t, :], st16[:, t, :])
            ins.then_inc(dve0, 1)
            dve.wait_ge(dve0, 1)
            nc.vector.tensor_scalar(ve16[:], mv16[:, :, 1], EPS, None, ALU.add).then_inc(a_var, 1)
            dve.wait_ge(a_w0, 1)
            nc.vector.tensor_tensor(w0l[:], w0[:, 0:2, :], w0h[:].bitcast(F32), ALU.subtract).then_inc(a_w0, 1)

            dve.wait_ge(rb_mm, 1)
            dve.wait_ge(ld_w0, 32)
            nc.vector.scalar_tensor_tensor(rb, ps[0:NB, 4, 0:D], 1.0 / S, b0, ALU.mult, ALU.add).then_inc(rb_ready, 1)

            dve.wait_ge(ld_wq, 48)
            wv = wnat.rearrange("p g (c k) -> p (g c) k", k=BLK)
            nc.vector.tensor_reduce(wabs[:], wv, AX.X, ALU.max, apply_absolute_value=True).then_inc(wstep, 1)
            dve.wait_ge(wstep, 1)
            nc.vector.tensor_scalar(wabs[:], wabs[:], 1.0 / 7.0, 1e-12, ALU.mult, ALU.max).then_inc(wstep, 1)
            dve.wait_ge(wstep, 2)
            nc.vector.reciprocal(winv[:], wabs[:]).then_inc(wstep, 1)
            dve.wait_ge(rb_ready, 2)
            nc.vector.tensor_tensor(rbl, rb, rbh[:].bitcast(F32), ALU.subtract).then_inc(rb_ready, 1)

            def a_low(b, u):
                hold(dve, a_xnT, b + 1)
                nc.vector.tensor_tensor(xTl[:, u].rearrange("p k s -> p (k s)"), bank(u),
                                        xTh[:, u].rearrange("p k s -> p (k s)").bitcast(F32), ALU.subtract).then_inc(a_xl, 1)

            def a_fin(b, u):
                hold(dve, a_mm, b + 1)
                xb = x[:, bass.ds(2 * b, 2), :]
                nc.vector.scalar_tensor_tensor(xb, bank2(2 + u), tg[:, 0:1], xb, ALU.mult, ALU.add).then_inc(a_x1, 1)
                hold(dve, a_x1, b + 1)

            def f_stats(b, u):
                ln_stats(tiles(x, b), b, u, ln_link, f_var, before=NT)

            def f_norm(b, u):
                ln_norm(tiles(lnb, b), tiles(x, b), b, u, f_rstd, f_ln)
                hold(dve, f_ln, 2 * b + 2)
                nc.vector.tensor_reduce(amx[:, bass.ds(b, 1)], lnb[:, bass.ds(2 * b, 2), :], AX.XY, ALU.max,
                                        apply_absolute_value=True).then_inc(f_red, 1)

            def a_step(b, u):
                a_low(b + 1, 1 - u)
                a_fin(b, u)
                f_stats(b, u)
                f_norm(b - 1, 1 - u)

            dve.wait_ge(tanh_ready, 1)
            a_low(0, 0)
            a_low(1, 1)
            a_fin(0, 0)
            f_stats(0, 0)
            dve.wait_ge(wstep, 4)
            nc.vector.tensor_scalar(wnat, wnat, MAGIC, -MAGIC, ALU.add, ALU.add).then_inc(wstep, 1)
            dve.wait_ge(wstep, 5)
            nc.vector.tensor_scalar(wnat, wnat, 7.0, -8.0, ALU.min, ALU.max).then_inc(wstep, 1)
            with dve.Fori(0, NB // 2 - 1) as i:
                for u in range(2):
                    a_step(2 * i + u + 1, 1 - u)
            a_fin(NB - 1, 1)
            f_stats(NB - 1, 1)
            f_norm(NB - 2, 0)
            for n in range(6):
                dve.wait_ge(w_ready, n + 1)
                piece_ = (slice(None), n // 3, slice(None), slice(256 * (n % 3), 256 * (n % 3) + 256))
                nc.vector.tensor_tensor(wTl[piece_], bank2(4 + n % 4), wTh[piece_].bitcast(F32), ALU.subtract).then_inc(w_low0, 1)
            f_norm(NB - 1, 1)

            def quant_scale(k, w, srcs, reds, scale, inv):
                dve.wait_ge(f_red, reds)
                for n, s_ in enumerate(srcs):
                    ins = nc.vector.tensor_reduce(pmax[:, n:n + 1], s_, AX.X, ALU.max)
                ins.then_inc(f_pmax, 1)
                dve.wait_ge(f_gmax, k + 1)
                nc.vector.tensor_scalar(scale, gmx[:, 0:w], 1.0 / QMAX, 1e-12, ALU.mult, ALU.max).then_inc(dve0, 1)
                dve.wait_ge(dve0, 2 + k)
                nc.vector.reciprocal(inv, scale).then_inc(f_scale, 1)
                dve.wait_ge(f_scale, k + 1)

            quant_scale(0, 1, [amx[:, 0:NB]], NB, sx[:, 0:1], sx[:, 1:2])
            def x_quant(b, u, first):
                xb = lnb[:, bass.ds(2 * b, 2), :]
                nc.vector.tensor_scalar(xb, xb, sx[:, 1:2], MAGIC, ALU.mult, ALU.add).then_inc(f_q1, 1)
                hold(dve, f_q1, b + 1)
                if not first:
                    hold(dve, f_turned, b - 1)
                nc.vector.tensor_scalar(xn[:, u], xb, -MAGIC, None, ALU.add).then_inc(f_xq, 1)

            def x_low(b, u):
                hold(dve, f_xqT, b + 1)
                c = bass.ds(S * b, S)
                nc.vector.scalar_tensor_tensor(xql[:, :, c], bank2(u), sx[:, 0:1], xqh[:, :, c].bitcast(F32),
                                               ALU.mult, ALU.subtract).then_inc(f_xl, 1)

            x_quant(0, 0, True)
            x_quant(1, 1, True)
            with dve.Fori(0, NB // 2 - 1) as i:
                for u in range(2):
                    x_low(2 * i + u, u)
                    x_quant(2 * i + u + 2, u, False)
            x_low(NB - 2, 0)
            x_low(NB - 1, 1)
            with dve.Fori(0, NCH) as j:
                for m in range(2 * KF):
                    hold(dve, f_ev, 2 * KF * j + m + 1)
                    src = (up if m < KF else gate)[:, m % KF, bass.ds(CH * j, CH)]
                    nc.vector.tensor_reduce(amx[:, bass.ds(m * NCH + j, 1)], src, AX.X, ALU.max,
                                            apply_absolute_value=True).then_inc(f_red, 1)
            R1 = NB + NCH * 2 * KF
            quant_scale(1, 2, [amx[:, 0:KF * NCH], amx[:, KF * NCH:2 * KF * NCH]], R1, sug[:, 0, :], sug[:, 1, :])

            def g_prod(m, u):
                dve.wait_ge(f_s1, m + 1)
                nc.vector.tensor_scalar(sig[:, u, :], sig[:, u, :], -MAGIC, 65535.0, ALU.add, ALU.min).then_inc(f_prod, 1)
                dve.wait_ge(f_prod, 2 * m + 1)
                g = gate[:, m, :]
                nc.vector.scalar_tensor_tensor(g, sig[:, u, :], 1.0 / 65536.0, g, ALU.mult, ALU.mult).then_inc(f_prod, 1)
                dve.wait_ge(f_prod, 2 * m + 2)
                nc.vector.tensor_reduce(amx[:, m:m + 1], g, AX.X, ALU.max, apply_absolute_value=True).then_inc(f_red, 1)

            dve.wait_ge(ld_k, 16)
            for n in range(4):
                part = kvals[:, 4 * n:4 * n + 4, :]
                if n:
                    dve.wait_ge(v_step, 2 * n)
                nc.vector.tensor_scalar(infm, part, -3.4028234663852886e38, None, ALU.is_lt).then_inc(v_step, 1)
                dve.wait_ge(v_step, 2 * n + 1)
                nc.vector.copy_predicated(part, infm, zero[:].unsqueeze(2).to_broadcast([P, 4, D])).then_inc(v_step, 1)
            for m in range(KF):
                g_prod(m, m % 2)
            quant_scale(2, 1, [amx[:, 0:KF]], R1 + KF, sp[:, 0:1], sp[:, 1:2])

            def o_product(m, u):
                g = gate[:, m, :]
                dve.wait_ge(f_p1, m + 1)
                dve.wait_ge(f_uq, 2 * m + 2)
                nc.vector.scalar_tensor_tensor(g, g, -MAGIC, up[:, m, :], ALU.add, ALU.mult).then_inc(f_prod, 1)
                dve.wait_ge(f_prod, 2 * KF + m + 1)
                nc.vector.tensor_reduce(amx[:, m:m + 1], g, AX.X, ALU.max, apply_absolute_value=True).then_inc(f_red, 1)

            for m in range(KF):
                o_product(m, m % 2)
            dve.wait_ge(f_red, R1 + 2 * KF)
            nc.vector.tensor_tensor(so[:, 2:3], sp[:, 0:1], sug[:, 0, 0:1], ALU.mult).then_inc(dve0, 1)
            dve.wait_ge(dve0, 5)
            nc.vector.tensor_reduce(pmax[:, 0:1], amx[:, 0:KF], AX.X, ALU.max).then_inc(f_pmax, 1)
            dve.wait_ge(f_gmax, 4)
            nc.vector.tensor_scalar(so[:, 0:1], gmx[:, 0:1], so[:, 2:3], 1.0 / QMAX, ALU.mult, ALU.mult).then_inc(dve0, 1)
            dve.wait_ge(dve0, 6)
            nc.vector.tensor_scalar(so[:, 0:1], so[:, 0:1], 1e-12, None, ALU.max).then_inc(dve0, 1)
            dve.wait_ge(dve0, 7)
            nc.vector.reciprocal(so[:, 1:2], so[:, 0:1]).then_inc(dve0, 1)
            dve.wait_ge(dve0, 8)
            nc.vector.tensor_tensor(so[:, 1:2], so[:, 1:2], so[:, 2:3], ALU.mult).then_inc(f_scale, 1)

            nc.vector.tensor_tensor(so[:, 3:4], so[:, 0:1], tg[:, 2:3], ALU.mult).then_inc(dve0, 1)
            dve.wait_ge(w_ready, 10)
            nc.vector.tensor_tensor(wdl[:], wdT[:], wdh[:].bitcast(F32), ALU.subtract).then_inc(w_low0, 1)
            dve.wait_ge(dve0, 9)

            def o_split(j, u, first=False):
                for h in range(2):
                    m = slice(KF // 2 * h, KF // 2 * h + KF // 2)
                    hold(dve, f_o1, 2 * j + h + 1)
                    if not first:
                        hold(dve, f_down, 2 * j - 2)
                    nc.vector.tensor_scalar(oqh[:, u, m], orn[:, h], -MAGIC, None, ALU.add).then_inc(f_prod, 1)
                    hold(dve, f_prod, 3 * KF + 2 * j + h + 1)
                    nc.vector.scalar_tensor_tensor(oql[:, u, m], orn[:, h], -MAGIC, oqh[:, u, m].bitcast(F32),
                                                   ALU.add, ALU.subtract).then_inc(f_oq, 1)

            def f_fin(j, u):
                for h in range(2):
                    hold(dve, f_down, 2 * j + h + 1)
                    xb = x[:, bass.ds(4 * j + 2 * h, 2), :]
                    nc.vector.scalar_tensor_tensor(xb, bank2(2 * u + h), so[:, 3:4], xb, ALU.mult, ALU.add)\
                        .then_inc(f_x2, 1)

            o_split(0, 0, True)
            o_split(1, 1, True)
            dve.wait_ge(ld_m, 16 * 18)
            for t in range(2):
                nc.vector.tensor_scalar(relx[:, t, :], relx[:, t, :], rele[:, t:t + 1], None, ALU.subtract)\
                    .then_inc(v_step, 1)
            with dve.Fori(0, NCH // 2 - 1) as i:
                for u in range(2):
                    f_fin(2 * i + u, u)
                    o_split(2 * i + u + 2, u)
            def c_norm(b, u):
                ln_stats(tiles(x, b), b, u, ln_link, c_var, before=NT + 2 * NB)
                ln_norm([xn[:, u, t, :] for t in range(2)], tiles(x, b), b, u, c_rstd, c_xn)

            dve.wait_ge(f_x2, 2)
            c_norm(0, 0)
            f_fin(NCH - 2, 0)
            c_norm(1, 1)
            f_fin(NCH - 1, 1)

            def c_smax(b, u):
                hold(dve, c_smm, b + 1)
                for t in range(2):
                    nc.vector.tensor_scalar(px[:, u, t, :], bank2(3)[:, t, :], float("-inf"), None, ALU.max, ALU.max,
                                            accum_out=cmx[:, u, t:t + 1]).then_inc(c_max, 1)
                hold(dve, c_max, 2 * b + 2)
                nc.vector.tensor_scalar(cnm[:, u, :], cmx[:, u, :], -1.0, None, ALU.mult).then_inc(c_nmax, 1)

            def c_fin(b, u):
                link = chained(dve, c_rz, 2 * b)
                hold(dve, c_exp, 2 * b + 2)
                link(nc.vector.reciprocal(crz[:, u, :], cz[:, u, :]))
                link(nc.vector.tensor_scalar(crz[:, u, :], crz[:, u, :], tg[:, 1:2], None, ALU.mult))
                hold(dve, c_pv, b + 1)
                for t in range(2):
                    xt = x[:, 2 * b + t, :]
                    ins = nc.vector.scalar_tensor_tensor(xt, bank2(5 + u)[:, t, :], crz[:, u, t:t + 1], xt, ALU.mult, ALU.add)
                ins.then_inc(c_x3, 1)

            c_smax(0, 0)
            dve.wait_ge(f_x2, NB)
            c_norm(2, 0)

            def c_step(b, u, norm=True):
                c_smax(b + 1, 1 - u)
                if norm:
                    c_norm(b + 3, 1 - u)
                c_fin(b, u)

            with dve.Fori(0, NB // 2 - 2) as i:
                for u in range(2):
                    c_step(2 * i + u, u)
            c_step(NB - 4, 0)
            c_step(NB - 3, 1, False)
            c_smax(NB - 1, 1)

            def m_norm(b, u, behind=0):
                for _ in range(behind):
                    yield
                tiles_ = [inner[:, 2 * b + t, :] for t in range(2)]
                for k, (src, var, rstd) in enumerate(((tiles(x, b), m_var, m_rstd), (tiles_, m_var2, m_rstd2))):
                    if k:
                        hold(dve, m_src, 2 * b + 2)
                    nc.vector.bn_stats(st[:, 0, :], src[0])
                    nc.vector.bn_stats(st[:, 1, :], src[1]).then_inc(m_link, 1)
                    yield
                    hold(dve, m_link, 4 * b + 2 * k + 1)
                    nc.vector.bn_aggr(mv[:, u, 0, :], st[:, 0, :])
                    nc.vector.bn_aggr(mv[:, u, 1, :], st[:, 1, :]).then_inc(m_link, 1)
                    yield
                    hold(dve, m_link, 4 * b + 2 * k + 2)
                    nc.vector.tensor_scalar(ve[:, u, :], mv[:, u, :, 1], EPS, None, ALU.add).then_inc(var, 1)
                    yield
                    yield
                    yield
                    if k:
                        ln_norm([xn[:, u, t, :] for t in range(2)], src, b, u, rstd, m_ln)
                    else:
                        ln_norm(tiles_, src, b, u, rstd, m_src)
                    yield

            weave(m_norm(0, 0))
            c_fin(NB - 2, 0)
            c_fin(NB - 1, 1)

            def m_gating(b, u):
                hold(dve, m_log, b + 1)
                lg = [ps[:, 0, EA * t:EA * t + EA] for t in range(2)]
                nc.vector.max(top[:, 0, :], lg[0])
                nc.vector.max(top[:, 1, :], lg[1]).then_inc(m_top, 1)
                yield
                hold(dve, m_top, 6 * b + 1)
                nc.vector.tensor_tensor(td[:], top[:, :, 1], top[:, :, 0], ALU.subtract).then_inc(m_d, 1)
                nc.vector.max_index(tidx[:, 0, :], top[:, 0, :], lg[0])
                nc.vector.max_index(tidx[:, 1, :], top[:, 1, :], lg[1]).then_inc(m_top, 1)
                yield
                hold(dve, m_top, 6 * b + 2)
                nc.vector.tensor_copy(tif[:], tidx[:, :, 0:2]).then_inc(m_top, 1)
                yield
                hold(dve, m_top, 6 * b + 3)
                hot_ = hot[:, u, :, :, 0:EA].rearrange("p t j e -> p (t j) e")
                nc.vector.tensor_tensor(hot_, iota[:, 0:EA].unsqueeze(1).to_broadcast([P, 4, EA]),
                                        tif[:].rearrange("p t j -> p (t j)").unsqueeze(2).to_broadcast([P, 4, EA]),
                                        ALU.is_equal)
                hold(dve, m_e, b + 1)
                nc.vector.tensor_scalar(td[:], te[:], 1.0, None, ALU.add).then_inc(m_top, 1)
                yield
                hold(dve, m_top, 6 * b + 4)
                nc.vector.reciprocal(gj[:, u, :, 0], td[:]).then_inc(m_top, 1)
                yield
                hold(dve, m_top, 6 * b + 5)
                nc.vector.tensor_tensor(gj[:, u, :, 1], gj[:, u, :, 0], te[:], ALU.mult).then_inc(m_top, 1)
                yield
                hold(dve, m_top, 6 * b + 6)
                nc.vector.tensor_tensor(ghot[:, u, :, :, 0:EA].rearrange("p t j e -> p (t j) e"), hot_,
                                        gj[:, u].rearrange("p t j -> p (t j)").unsqueeze(2).to_broadcast([P, 4, EA]),
                                        ALU.mult).then_inc(m_gate, 1)
                yield
                hold(dve, m_gate, 2 * b + 1)
                nc.vector.tensor_tensor(G[:, u, :, 0:EA], ghot[:, u, :, 0, 0:EA], ghot[:, u, :, 1, 0:EA], ALU.add)\
                    .then_inc(m_gate, 1)
                yield

            def m_softmax(b):
                hold(dve, m_rin, 16 * b + 16)
                hold(dve, m_smm, b + 1)
                for j in range(2):
                    for t in range(2):
                        n = 2 * j + t
                        nc.vector.tensor_tensor_reduce(pm[:, j, t, :], bank2(6 + j)[:, t, :], B[:, j, t, :], 1.0, -3.0e38,
                                                       ALU.add, ALU.max, mmx[:, n:n + 1]).then_inc(m_max, 1)
                yield
                hold(dve, m_max, 4 * b + 4)
                nc.vector.tensor_scalar(mnm[:], mmx[:], -float(HD) ** -0.5, None, ALU.mult).then_inc(m_nmax, 1)

            def m_value(b, u):
                hold(dve, m_vmm, b + 1)
                nc.vector.tensor_tensor(val[:, u], ps[:, 1, 0:2 * HD].rearrange("p (k h) -> p k h", k=2),
                                        vb[:].unsqueeze(1).to_broadcast([P, 2, HD]), ALU.add)

            def m_scale(b, u):
                hold(dve, m_exp, 4 * b + 4)
                link = chained(dve, m_rz, 2 * b)
                link(nc.vector.reciprocal(mrz[:], mz[:]))
                link(nc.vector.tensor_tensor(mrz[:].rearrange("p (j t) -> p j t", j=2), mrz[:].rearrange("p (j t) -> p j t", j=2),
                                             gj[:, u].rearrange("p t j -> p j t"), ALU.mult))
                for n in range(4):
                    nc.vector.tensor_scalar(pm[:, n // 2, n % 2, :], pm[:, n // 2, n % 2, :], mrz[:, n:n + 1], None, ALU.mult)\
                        .then_inc(m_p, 1)

            def m_select(b, u):
                for e in range(EA):
                    hold(dve, m_qmm, 5 * b + e // 2 + 1)
                    data = bank2(3 - e // 2 % 2)[:, e % 2, :].unsqueeze(1).to_broadcast([P, 2, S])
                    if e == 0:
                        ins = nc.vector.tensor_copy(qsel, data)
                    else:
                        hold(dve, m_mask, 8 * b + e + 1)
                        hold(dve, m_qsel, 8 * b + e)
                        ins = nc.vector.copy_predicated(qsel, mask[:, u, e].bitcast(U16), data)
                    ins.then_inc(m_qsel, 1)
                hold(dve, m_qsel, 8 * b + 8)
                hold(dve, m_qmm, 5 * b + 5)
                nc.vector.tensor_tensor(qT, qsel, bank2(3), ALU.add).then_inc(m_qT, 1)

            def m_low(b, u):
                hold(dve, m_xnT, b + 1)
                nc.vector.tensor_tensor(xnTl[:, u].rearrange("p k s -> p (k s)"), bank(0),
                                        xnTh[:, u].rearrange("p k s -> p (k s)").bitcast(F32), ALU.subtract).then_inc(m_xl, 1)

            def m_spread(b, u, low=False):
                hold(dve, m_pv, b + 1)
                c = ps[:, 1, :].rearrange("p (j s) -> p j s", j=2)
                for h in range(2):
                    e = slice(4 * h, 4 * h + 4)
                    nc.vector.tensor_tensor(ctxE[:, e], mask[:, u, e, 0, :], c[:, 0, :].unsqueeze(1).to_broadcast([P, 4, S]),
                                            ALU.mult).then_inc(m_cE, 1)
                    if low and h == 0:
                        m_low(b + 2, u)
                    hold(dve, m_cE, 4 * b + 2 * h + 1)
                    nc.vector.copy_predicated(ctxE[:, e], mask[:, u, e, 1, :].bitcast(U16),
                                              c[:, 1, :].unsqueeze(1).to_broadcast([P, 4, S])).then_inc(m_cE, 1)

            def m_add(b):
                hold(dve, m_omm, b + 1)
                sb_ = inner[:, bass.ds(2 * b, 2), :]
                nc.vector.tensor_tensor(sb_, sb_, bank2(3), ALU.add).then_inc(m_out, 1)

            def m_gates_scores(b, u, gate_next, scores):
                if gate_next:
                    yield from m_gating(b + 1, 1 - u)
                if scores:
                    yield from m_softmax(b)

            for n, (low, w_, high) in enumerate(((qwl, qw, qwh), (kwl, kw, kwh), (vwl, vw, vwh), (gwl, gw, gwh))):
                dve.wait_ge(w_high, n + 1)
                nc.vector.tensor_tensor(low[:], w_ if w_ is qw else w_[:], high[:].bitcast(F32), ALU.subtract).then_inc(w_low, 1)
            m_low(0, 0)
            weave(m_gating(0, 0))
            weave(m_norm(1, 1))
            m_value(0, 0)
            m_select(0, 0)
            m_low(1, 1)
            weave(m_gates_scores(0, 0, True, True))
            weave(m_norm(2, 0))
            m_scale(0, 0)

            def n_stats(b, u):
                hold(dve, m_out, b + 1)
                xb = x[:, bass.ds(2 * b, 2), :]
                nc.vector.scalar_tensor_tensor(xb, inner[:, bass.ds(2 * b, 2), :], tg[:, 3:4], xb, ALU.mult, ALU.add)\
                    .then_inc(n_base, 1)
                ln_stats(tiles(inner, b), b, u, n_st, n_var, nmv, nve)

            def n_norm(b, u):
                ln_norm(tiles(nxn, b), tiles(inner, b), b, u, n_rstd, n_ln, nmv, nrs)

            def m_step(b, u, norm=True, gate_next=True, first=False):
                m_value(b + 1, 1 - u)
                m_select(b + 1, 1 - u)
                m_spread(b, u, gate_next)
                weave(m_gates_scores(b + 1, 1 - u, gate_next, True), *([m_norm(b + 3, 1 - u, 1)] if norm else []))
                if not first:
                    n_norm(b - 1, 1 - u)
                m_add(b)
                m_scale(b + 1, 1 - u)
                n_stats(b, u)

            m_step(0, 0, first=True)
            with dve.Fori(0, NB // 2 - 2) as i:
                for u in range(2):
                    m_step(2 * i + u + 1, 1 - u)
            m_step(NB - 3, 1, norm=False)
            m_step(NB - 2, 0, norm=False, gate_next=False)
            n_norm(NB - 2, 0)
            m_spread(NB - 1, 1)
            m_add(NB - 1)
            n_stats(NB - 1, 1)
            n_norm(NB - 1, 1)

            with dve.Fori(0, NB // 2) as i:
                for u in range(2):
                    b = 2 * i + u
                    c = bass.ds(S * b, S)
                    hold(dve, n_xnT, 2 * b + 2)
                    nc.vector.tensor_tensor(xml[:, :, c], bank2(4 + u), xmh[:, :, c].bitcast(F32), ALU.subtract)\
                        .then_inc(n_all, 1)

            lg = ps[:, 3, 0:NT * EF].rearrange("p (t e) -> p t e", e=EF)
            dve.wait_ge(n_log, NB)
            for t in range(NT):
                nc.vector.max(ntop[:, t, :], lg[:, t, :]).then_inc(n_top, 1)
            dve.wait_ge(n_top, NT)
            nc.vector.tensor_tensor(ntd, ntop[:, :, 1], ntop[:, :, 0], ALU.subtract).then_inc(n_d, 1)
            for t in range(NT):
                nc.vector.max_index(ntidx[:, t, :], ntop[:, t, :], lg[:, t, :]).then_inc(n_top, 1)
            dve.wait_ge(n_top, 2 * NT)
            nc.vector.tensor_copy(ntif, ntidx[:, :, 0:2]).then_inc(n_top, 1)
            dve.wait_ge(n_top, 2 * NT + 1)
            flat = "p t j -> p (t j)"
            nhotf = nhot.rearrange("p t j e -> p (t j) e")
            nc.vector.tensor_tensor(nhotf, iota[:].unsqueeze(1).to_broadcast([P, 2 * NT, EF]),
                                    ntif.rearrange(flat).unsqueeze(2).to_broadcast([P, 2 * NT, EF]), ALU.is_equal)
            dve.wait_ge(n_e, 1)
            nc.vector.tensor_scalar(ntd, nte, 1.0, None, ALU.add).then_inc(n_top, 1)
            dve.wait_ge(n_top, 2 * NT + 2)
            nc.vector.reciprocal(ngj[:, :, 0], ntd).then_inc(n_top, 1)
            dve.wait_ge(n_top, 2 * NT + 3)
            nc.vector.tensor_tensor(ngj[:, :, 1], ngj[:, :, 0], nte, ALU.mult).then_inc(n_top, 1)
            dve.wait_ge(n_top, 2 * NT + 4)
            nc.vector.tensor_tensor(nghot.rearrange("p t j e -> p (t j) e"), nhotf,
                                    ngj.rearrange(flat).unsqueeze(2).to_broadcast([P, 2 * NT, EF]),
                                    ALU.mult).then_inc(n_top, 1)
            dve.wait_ge(n_top, 2 * NT + 5)
            nc.vector.tensor_tensor(nG, nghot[:, :, 0, :], nghot[:, :, 1, :], ALU.add).then_inc(n_gate, 1)

            def e_gate(j, e):
                if e % 4 == 0:
                    hold(dve, g_in[e // 4], 16 * j + 16)
                n = EF * j + e
                if e >= 3:
                    hold(dve, e_l, n - 2)
                hold(dve, e_hmm, n + 1)
                nc.vector.scalar_tensor_tensor(hg[:, e % 3, :], bank(e % 3), b1[:, e:e + 1], gbc[e // 4][:, e % 4, :],
                                               ALU.add, ALU.mult).then_inc(e_hg, 1)

            def e_low(j, e):
                hold(dve, e_h, EF * j + e + 1)
                nc.vector.scalar_tensor_tensor(hrl[:, e % 3, :], hg[:, e % 3, :], 0.0, hrh[:, e % 3, :].bitcast(F32),
                                               ALU.max, ALU.subtract).then_inc(e_l, 1)

            dve.wait_ge(n_base, NB)
            dve.wait_ge(n_gturn, NCH)
            with dve.Fori(0, NCH) as j:
                for e in range(EF):
                    e_gate(j, e)
                    if e:
                        e_low(j, e - 1)
                e_low(j, EF - 1)
                for h in range(2):
                    hold(dve, e_yturn, 2 * j + h + 1)
                    xb = x[:, bass.ds(4 * j + 2 * h, 2), :]
                    nc.vector.scalar_tensor_tensor(xb, bank2(6 + h), tg[:, 3:4], xb, ALU.mult, ALU.add).then_inc(e_x4, 1)

        @block.scalar
        def _(act):
            act.wait_ge(ld_g, 32)
            nc.scalar.activation(tg[:], gates[:], ACT.Tanh).then_inc(tanh_ready, 1)

            act.wait_ge(const_ready, 1)
            nc.scalar.copy(ones[:], ones1[:])
            act.wait_ge(ld_w0, 32)
            nc.scalar.copy(w0h[:], w0[:, 0:2, :]).then_inc(a_w0, 1)
            act.wait_ge(ld_ctxT, 16)
            for b in range(NB):
                for k in range(KD):
                    nc.scalar.activation(ctxT[:, k, S * b:S * b + S], ctxT[:, k, S * b:S * b + S], ACT.Copy, accum_out=csum[:, k, b:b + 1])\
                        .then_inc(csum_ready, 1)
            act.wait_ge(rb_ready, 1)
            for b in range(NB):
                ins = nc.scalar.activation(rbdh[:, b, :], rb, ACT.Copy, scale=ident[0:NB, b:b + 1])
            nc.scalar.copy(rbh[:], rb).then_inc(rb_ready, 1)

            def a_evac(b, u):
                hold(act, a_turned, b + 1)
                nc.scalar.copy(xTh[:, u].rearrange("p k s -> p (k s)"), bank(u)).then_inc(a_xnT, 1)

            a_evac(0, 0)
            a_evac(1, 1)
            act.wait_ge(rb_ready, 3)
            for b in range(NB):
                ins = nc.scalar.activation(rbdl[:, b, :], rbl, ACT.Copy, scale=ident[0:NB, b:b + 1])
            ins.then_inc(rb_ready, 1)
            with act.Fori(1, NB // 2) as i:
                for u in range(2):
                    a_evac(2 * i + u, u)
            for n in range(9):
                act.wait_ge(w_turned, n + 1)
                if n < 6:
                    w, h, k = n // 3 % 2, n % 3, 0
                    dst = wTh[:, n // 3, :, 256 * h:256 * h + 256]
                    src = bank2(4 + n % 4)
                else:
                    dst = wdT[:, 2 * (n - 6):2 * (n - 6) + 2, :]
                    src = bank2(4 + n % 4)
                nc.scalar.copy(dst, src).then_inc(w_ready, 1)

            act.wait_ge(f_scale, 1)
            with act.Fori(0, NB // 2) as i:
                for u in range(2):
                    b = 2 * i + u
                    hold(act, f_turned, b + 1)
                    nc.scalar.activation(xqh[:, :, bass.ds(S * b, S)], bank2(u), ACT.Copy, scale=sx[:, 0:1])\
                        .then_inc(f_xqT, 1)
            with act.Fori(0, NCH) as j:
                for m in range(2 * KF):
                    hold(act, f_mm, 2 * KF * j + m + 1)
                    dst = (up if m < KF else gate)[:, m % KF, bass.ds(CH * j, CH)]
                    nc.scalar.copy(dst, bank(2 + m % UP_BANKS)).then_inc(f_ev, 1)

            def g_round(m):
                g = gate[:, m, :]
                nc.scalar.activation(g, g, ACT.Identity, scale=sug[:, 1, 1:2], bias=magic[:]).then_inc(f_g1, 1)

            def g_sigmoid(m, u):
                act.wait_ge(f_g2, m + 1)
                if m >= 2:
                    act.wait_ge(f_prod, 2 * m - 2)
                nc.scalar.activation(sig[:, u, :], gate[:, m, :], ACT.Sigmoid).then_inc(f_sig, 1)
                act.wait_ge(f_sig, m + 1)
                nc.scalar.activation(sig[:, u, :], sig[:, u, :], ACT.Identity, scale=65536.0, bias=magic[:])\
                    .then_inc(f_s1, 1)

            act.wait_ge(f_scale, 2)
            act.wait_ge(const_ready, 1)
            g_round(0)
            g_round(1)
            for m in range(KF):
                g_sigmoid(m, m % 2)
                if m + 2 < KF:
                    g_round(m + 2)
            nc.scalar.copy(wdh[:], wdT[:]).then_inc(w_ready, 1)
            act.wait_ge(f_scale, 3)
            for m in range(KF):
                g = gate[:, m, :]
                nc.scalar.activation(g, g, ACT.Identity, scale=sp[:, 1:2], bias=magic[:]).then_inc(f_p1, 1)
            act.wait_ge(f_scale, 4)

            def o_round(j, first=False):
                for h in range(2):
                    if not first:
                        hold(act, f_oq, 2 * j + h - 1)
                    nc.scalar.activation(orn[:, h], gate[:, KF // 2 * h:KF // 2 * h + KF // 2, bass.ds(CH * j, CH)],
                                         ACT.Identity, scale=so[:, 1:2], bias=magic[:]).then_inc(f_o1, 1)

            o_round(0, True)
            with act.Fori(1, NCH) as j:
                o_round(j)

            act.wait_ge(ld_m, 16 * 18)

            def c_turned_out(b, u):
                hold(act, c_turned, b + 1)
                nc.scalar.copy(xnT[:, u].rearrange("p k s -> p (k s)"), bank(u)).then_inc(c_xnT, 1)

            def c_query(b, u):
                hold(act, c_qmm, b + 1)
                for k in range(KD):
                    nc.scalar.activation(qx[:, u, k, :], bank2(2)[:, k, :], ACT.Identity, bias=b1x[:, k:k + 1]).then_inc(c_q, 1)

            def c_exps(b, u):
                hold(act, c_nmax, b + 1)
                for t in range(2):
                    nc.scalar.activation(px[:, u, t, :], px[:, u, t, :], ACT.Exp, bias=cnm[:, u, t:t + 1],
                                         accum_out=cz[:, u, t:t + 1]).then_inc(c_exp, 1)

            def c_weights(b, u):
                hold(act, c_pturn, b + 1)
                nc.scalar.copy(pxT[:, u].rearrange("p k s -> p (k s)"), bank(4)).then_inc(c_pT, 1)

            c_turned_out(0, 0)
            c_turned_out(1, 1)
            c_query(0, 0)
            c_exps(0, 0)
            with act.Fori(0, NB // 2 - 1) as i:
                for u in range(2):
                    b = 2 * i + u
                    c_query(b + 1, 1 - u)
                    c_weights(b, u)
                    c_turned_out(b + 2, u)
                    c_exps(b + 1, 1 - u)
            c_query(NB - 1, 1)
            c_weights(NB - 2, 0)
            c_exps(NB - 1, 1)
            c_weights(NB - 1, 1)

            def m_turned_out(b, u):
                hold(act, m_turned, b + 1)
                nc.scalar.copy(xnTh[:, u].rearrange("p k s -> p (k s)"), bank(0)).then_inc(m_xnT, 1)

            def m_gexp(b):
                hold(act, m_d, b + 1)
                nc.scalar.activation(te[:], td[:], ACT.Exp).then_inc(m_e, 1)

            def m_hots(b, u):
                hold(act, m_hturn, b + 1)
                nc.scalar.copy(hotTb, ps[0:EA, 0, :]).then_inc(m_hT, 1)
                nc.scalar.copy(hotT, ps[0:EA, 0, :]).then_inc(m_hT, 1)
                nc.scalar.copy(GT[:, u, :], ps[0:EA, 1, 0:S]).then_inc(m_hT, 1)

            def m_masks(b, u):
                for e in range(EA):
                    hold(act, m_maskmm, 8 * b + e + 1)
                    nc.scalar.copy(mask[:, u, e], bank2((2, 4, 5)[e % 3])).then_inc(m_mask, 1)

            def m_key(b):
                hold(act, m_kmm, b + 1)
                nc.scalar.activation(kT, ps[:, 0, 0:S], ACT.Identity, bias=kb[:]).then_inc(m_k, 1)

            def m_exps(b):
                hold(act, m_nmax, b + 1)
                for n in range(4):
                    p_ = pm[:, n // 2, n % 2, :]
                    nc.scalar.activation(p_, p_, ACT.Exp, scale=float(HD) ** -0.5, bias=mnm[:, n:n + 1],
                                         accum_out=mz[:, n:n + 1]).then_inc(m_exp, 1)

            def m_weights(b):
                hold(act, m_pturn, b + 1)
                for k in range(2):
                    nc.scalar.copy(pmT[:, k, :], bank(4 + k)).then_inc(m_pT, 1)

            def m_band(b, first):
                hold(act, m_rmm, b + 1)
                if not first:
                    hold(act, m_rout, 32 * b)
                for t in range(2):
                    nc.scalar.copy(R[:, t], ps[:, 4 + t, 0:2 * RELW].rearrange("p (j c) -> p j c", j=2)).then_inc(m_r, 1)

            act.wait_ge(ld_m, 16 * 18)
            act.wait_ge(ld_q, 48)
            for high, w_ in ((qwh, qw), (kwh, kw), (vwh, vw), (gwh, gw)):
                nc.scalar.copy(high[:], w_ if w_ is qw else w_[:]).then_inc(w_high, 1)
            m_turned_out(0, 0)
            m_gexp(0)
            m_hots(0, 0)
            m_masks(0, 0)
            m_key(0)
            m_turned_out(1, 1)
            m_band(0, True)
            m_gexp(1)
            m_hots(1, 1)
            m_exps(0)

            def m_step(b, u, more):
                m_masks(b + 1, 1 - u)
                m_key(b + 1)
                m_weights(b)
                if more:
                    m_turned_out(b + 2, u)
                m_band(b + 1, False)
                if more:
                    m_gexp(b + 2)
                    m_hots(b + 2, u)
                m_exps(b + 1)

            with act.Fori(0, NB // 2 - 1) as i:
                for u in range(2):
                    m_step(2 * i + u, u, True)
            m_step(NB - 2, 0, False)
            m_weights(NB - 1)

            act.wait_ge(ld_e, 48)
            act.wait_ge(m_omm, NB)
            nc.scalar.copy(w1h[:], w1).then_inc(w_high, 1)

            def n_turned_out(b, u, first):
                hold(act, n_turned, b + 1)
                if not first:
                    hold(act, n_log, b - 1)
                nc.scalar.copy(xnT[:, u].rearrange("p k s -> p (k s)"), bank(4 + u)).then_inc(n_xnT, 1)
                nc.scalar.copy(xmh[:, :, bass.ds(S * b, S)], bank2(4 + u)).then_inc(n_xnT, 1)

            n_turned_out(0, 0, True)
            n_turned_out(1, 1, True)
            with act.Fori(1, NB // 2) as i:
                for u in range(2):
                    n_turned_out(2 * i + u, u, False)
            act.wait_ge(m_cE, 4 * NB)
            nc.scalar.copy(w2h[:], w2).then_inc(w_high, 1)
            act.wait_ge(n_d, 1)
            nc.scalar.activation(nte, ntd, ACT.Exp).then_inc(n_e, 1)
            for j in range(NCH):
                act.wait_ge(n_gturn, j + 1)
                nc.scalar.copy(GTa[:, CH * j:CH * j + CH], ps[0:EF, 6 + j % 2, :]).then_inc(n_GT, 1)

            with act.Fori(0, NCH) as j:
                for e in range(EF):
                    hold(act, e_hg, EF * j + e + 1)
                    if e >= 3:
                        hold(act, e_ymm, EF * j + e - 2)
                    nc.scalar.activation(hrh[:, e % 3, :], hg[:, e % 3, :], ACT.Relu).then_inc(e_h, 1)
                hold(act, e_ymm, EF * j + EF)
                nc.scalar.copy(yT, ps[:, 4:6, :]).then_inc(e_y, 1)

        @block.tensor
        def _(pe):
            mm = nc.tensor.matmul

            def turn(dst_bank, src, done):
                for k in range(KD):
                    for t in range(2):
                        ins = nc.tensor.transpose(ps[:, dst_bank, k * S + t * P:k * S + t * P + P],
                                                  src[t][:, k * P:(k + 1) * P], ident[:])
                ins.then_inc(done, 1)

            def split_product(out_, w, v, start, stop):
                for n, (w_, v_) in enumerate(((0, 0), (1, 0), (0, 1))):
                    ins = mm(out_, w[w_], v[v_], start=start and n == 0, stop=stop and n == 2, skip_group_check=True)
                return ins

            def a_turn(b, u):
                pe.wait_ge(a_xn, b + 1)
                turn(u, [xn[:, u, t, :] for t in range(2)], a_turned)

            def a_product(b, u):
                pe.wait_ge(a_xl, b + 1)
                for t in range(2):
                    o = ps[:, 2 + u, t * D:(t + 1) * D]
                    for k in range(KD):
                        split_product(o, [x_[:, u, k, t * P:(t + 1) * P] for x_ in (xTh, xTl)],
                                      [w_[:, k, :] for w_ in (w0h, w0l)], k == 0, False)
                    for r_ in (rbdh, rbdl):
                        ins = mm(o, ones[:], r_[:, b, :], start=False, stop=r_ is rbdl, skip_group_check=True)
                ins.then_inc(a_mm, 1)

            pe.wait_ge(const_ready, 1)
            pe.wait_ge(ld_w0, 32)
            pe.wait_ge(csum_ready, NB * KD)
            for k in range(KD):
                ins = mm(ps[0:NB, 4, 0:D], csum[:, k, :], w0[:, 2 + k, :], start=(k == 0), stop=(k == 1))
            ins.then_inc(rb_mm, 1)
            a_turn(0, 0)
            a_turn(1, 1)
            pe.wait_ge(a_w0, 2)
            pe.wait_ge(rb_ready, 4)
            with pe.Fori(0, NB // 2 - 1) as i:
                for u in range(2):
                    a_product(2 * i + u, u)
                    a_turn(2 * i + u + 2, u)
            a_product(NB - 2, 0)
            a_product(NB - 1, 1)
            pe.wait_ge(wdq, 1)
            for n in range(9):
                if n >= 4:
                    pe.wait_ge(w_low0, n - 3)
                for k in range(2):
                    for c in range(2):
                        if n < 6:
                            src = wnat[:, 6 * (n // 3) + 2 * (n % 3) + c, k * P:(k + 1) * P]
                        else:
                            m = 2 * (n - 6) + k
                            src = wnat[:, 12 + 3 * c + m // 2, (m % 2) * P:(m % 2 + 1) * P]
                        ins = nc.tensor.transpose(ps[:, 4 + n % 4, k * 256 + c * P:k * 256 + c * P + P], src, ident[:])
                ins.then_inc(w_turned, 1)

            def f_turn(b, u):
                pe.wait_ge(f_xq, b + 1)
                turn(u, [xn[:, u, t, :] for t in range(2)], f_turned)

            f_turn(0, 0)
            f_turn(1, 1)
            with pe.Fori(1, NB // 2) as i:
                for u in range(2):
                    b = 2 * i + u
                    pe.wait_ge(f_xl, b - 1)
                    f_turn(b, u)

            def upgate(j, first):
                pe.wait_ge(f_xl, 2 * j + 2)
                for m in range(2 * KF):
                    if not (first and m < UP_BANKS):
                        pe.wait_ge(f_ev, 2 * KF * j + m + 1 - UP_BANKS)
                    for k in range(KD):
                        ins = split_product(bank(2 + m % UP_BANKS),
                                            [w_[:, m // KF, k, m % KF * P:(m % KF + 1) * P] for w_ in (wTh, wTl)],
                                            [x_[:, k, bass.ds(CH * j, CH)] for x_ in (xqh, xql)], k == 0, k == KD - 1)
                    ins.then_inc(f_mm, 1)

            pe.wait_ge(w_ready, 9)
            pe.wait_ge(w_low0, 6)
            upgate(0, True)
            with pe.Fori(1, NCH) as j:
                upgate(j, False)

            def down(j, u, first):
                pe.wait_ge(f_oq, 2 * j + 2)
                for h in range(2):
                    if not first:
                        pe.wait_ge(f_x2, 2 * j + h - 3)
                    for t in range(2):
                        for m in range(KF):
                            c = (2 * h + t) * P
                            ins = split_product(ps[:, 2 * u + h, t * D:(t + 1) * D], [o_[:, u, m, c:c + P] for o_ in (oqh, oql)],
                                                [w_[:, m, :] for w_ in (wdh, wdl)], m == 0, m == KF - 1)
                    ins.then_inc(f_down, 1)

            pe.wait_ge(w_low0, 7)
            down(0, 0, True)
            down(1, 1, True)
            with pe.Fori(1, NCH // 2) as i:
                for u in range(2):
                    down(2 * i + u, u, False)

            def c_turn(b, u):
                pe.wait_ge(c_xn, 2 * b + 2)
                turn(u, [xn[:, u, t, :] for t in range(2)], c_turned)

            def c_qproduct(b, u):
                pe.wait_ge(c_xnT, b + 1)
                for h in range(2):
                    for k in range(KD):
                        ins = mm(bank2(2)[:, h, :], w1x[:, k, h * P:(h + 1) * P], xnT[:, u, k, :],
                                 start=(k == 0), stop=(k == 1))
                ins.then_inc(c_qmm, 1)

            def c_scores(b, u):
                pe.wait_ge(c_q, 2 * b + 2)
                for t in range(2):
                    for k in range(KD):
                        ins = mm(bank2(3)[:, t, :], qx[:, u, k, t * P:(t + 1) * P], keysT[:, k, bass.ds(S * b, S)],
                                 start=(k == 0), stop=(k == 1))
                ins.then_inc(c_smm, 1)

            def c_pturns(b, u):
                pe.wait_ge(c_exp, 2 * b + 2)
                turn(4, [px[:, u, t, :] for t in range(2)], c_pturn)

            def c_context(b, u):
                pe.wait_ge(c_pT, b + 1)
                for t in range(2):
                    for k in range(2):
                        ins = mm(bank2(5 + u)[:, t, :], pxT[:, u, k, t * P:(t + 1) * P], kvals[:, 2 * b + k, :],
                                 start=(k == 0), stop=(k == 1))
                ins.then_inc(c_pv, 1)

            pe.wait_ge(f_x2, NB - 2)
            c_turn(0, 0)
            c_turn(1, 1)
            pe.wait_ge(f_x2, NB)
            pe.wait_ge(ld_m, 16 * 18)
            c_qproduct(0, 0)
            pe.wait_ge(ld_kT, 16)
            c_scores(0, 0)
            pe.wait_ge(v_step, 10)
            with pe.Fori(0, NB // 2 - 1) as i:
                for u in range(2):
                    b = 2 * i + u
                    c_qproduct(b + 1, 1 - u)
                    c_pturns(b, u)
                    c_turn(b + 2, u)
                    c_scores(b + 1, 1 - u)
                    c_context(b, u)
            c_qproduct(NB - 1, 1)
            c_pturns(NB - 2, 0)
            c_scores(NB - 1, 1)
            c_context(NB - 2, 0)
            c_pturns(NB - 1, 1)
            c_context(NB - 1, 1)

            def m_logits(b, u):
                pe.wait_ge(m_xl, b + 1)
                for t in range(2):
                    for k in range(KD):
                        ins = split_product(ps[:, 0, EA * t:EA * t + EA], [x_[:, u, k, t * P:(t + 1) * P] for x_ in (xnTh, xnTl)],
                                            [w_[:, k, :] for w_ in (gwh, gwl)], k == 0, k == KD - 1)
                ins.then_inc(m_log, 1)

            def m_input(b, u):
                pe.wait_ge(m_xn, b + 1)
                turn(0, [xn[:, u, t, :] for t in range(2)], m_turned)

            def m_hotturn(b, u):
                pe.wait_ge(m_gate, 2 * b + 2)
                for j in range(2):
                    for t in range(2):
                        nc.tensor.transpose(ps[0:EA, 0, j * S + t * P:j * S + t * P + P], hot[:, u, t, j, 0:EA], ident[:])
                for t in range(2):
                    ins = nc.tensor.transpose(ps[0:EA, 1, t * P:t * P + P], G[:, u, t, 0:EA], ident[:])
                ins.then_inc(m_hturn, 1)

            def m_maskproduct(b, u, first):
                pe.wait_ge(m_hT, 3 * b + 1)
                if not first:
                    pe.wait_ge(m_r, 2 * b)
                for e in range(EA):
                    if e >= 3:
                        pe.wait_ge(m_mask, 8 * b + e - 2)
                    mm(bank((2, 4, 5)[e % 3]), sel8[:, e, :], hotTb, start=True, stop=True).then_inc(m_maskmm, 1)
                    if e in (2, 3, 4):
                        m_kv(b, u, e - 2)

            def m_kv(b, u, part):
                if part == 0:
                    pe.wait_ge(m_hT, 3 * b + 3)
                for k in range(KD):
                    keys_, x_ = [w_[:, k, :] for w_ in (kwh, kwl)], [x_[:, u, k, :] for x_ in (xnTh, xnTl)]
                    if part == 0:
                        ins = split_product(ps[:, 0, 0:S], keys_, x_, k == 0, k == KD - 1)
                    else:
                        t = part - 1
                        ins = split_product(ps[:, 1, t * HD:(t + 1) * HD], [v_[:, t * P:(t + 1) * P] for v_ in x_],
                                            [w_[:, k, :] for w_ in (vwh, vwl)], k == 0, k == KD - 1)
                if part == 0:
                    ins.then_inc(m_kmm, 1)
                if part == 2:
                    ins.then_inc(m_vmm, 1)

            def m_queries(b, u, half, first=False):
                for e in range(4 * half, 4 * half + 4):
                    if e % 2 == 0:
                        if e == 0:
                            if not first:
                                pe.wait_ge(m_out, b - 1)
                        elif e == 2:
                            pe.wait_ge(m_mask, 8 * b + 7)
                        else:
                            pe.wait_ge(m_qsel, 8 * b + e - 2)
                    for k in range(KD):
                        ins = split_product(bank2(3 - e // 2 % 2)[:, e % 2, :],
                                            [w_[:, k, e * HD:(e + 1) * HD] for w_ in (qwh, qwl)],
                                            [x_[:, u, k, :] for x_ in (xnTh, xnTl)], k == 0, k == KD - 1)
                    if e % 2:
                        ins.then_inc(m_qmm, 1)
                if half:
                    pe.wait_ge(m_qsel, 8 * b + 6)
                    mm(bank(3), qb[:], hotT, start=True, stop=True).then_inc(m_qmm, 1)

            def m_bandproduct(b):
                pe.wait_ge(m_qT, b + 1)
                for t in range(2):
                    for j in range(2):
                        ins = mm(ps[:, 4 + t, j * RELW:(j + 1) * RELW], qT[:, j, t * P:(t + 1) * P], relx[:, t, :],
                                 start=True, stop=True)
                ins.then_inc(m_rmm, 1)

            def m_scores(b):
                pe.wait_ge(m_k, b + 1)
                for j in range(2):
                    for t in range(2):
                        ins = mm(bank2(6 + j)[:, t, :], qT[:, j, t * P:(t + 1) * P], kT, start=True, stop=True)
                ins.then_inc(m_smm, 1)

            def m_pturns(b, last=False):
                if not last:
                    pe.wait_ge(m_mask, 8 * b + 16)
                pe.wait_ge(m_p, 4 * b + 4)
                for k in range(2):
                    for n in range(4):
                        ins = nc.tensor.transpose(ps[:, 4 + k, n * P:(n + 1) * P], pm[:, n // 2, n % 2, k * P:(k + 1) * P],
                                                  ident[:])
                ins.then_inc(m_pturn, 1)

            def m_context(b, u):
                pe.wait_ge(m_pT, 2 * b + 2)
                for k in range(2):
                    ins = mm(bank(1), val[:, u, k, :], pmT[:, k, :], start=(k == 0), stop=(k == 1))
                ins.then_inc(m_pv, 1)

            def m_output(b, u, hots=False):
                pe.wait_ge(m_cE, 4 * b + 2)
                tile_ = bank2(3)
                for t in range(2):
                    mm(tile_[:, t, :], GT[:, u, t * P:(t + 1) * P], ob[:], start=True, stop=False, skip_group_check=True)
                    if t and hots:
                        m_hotturn(b + 2, u)
                    for e in range(EA):
                        if t == 0 and e == 4:
                            pe.wait_ge(m_cE, 4 * b + 4)
                        ins = mm(tile_[:, t, :], ctxE[:, e, t * P:(t + 1) * P], ow[:, e, :], start=False, stop=(e == EA - 1),
                                 skip_group_check=True)
                ins.then_inc(m_omm, 1)

            pe.wait_ge(ld_m, 16 * 18)
            pe.wait_ge(ld_q, 48)
            m_input(0, 0)
            pe.wait_ge(w_low, 4)
            m_logits(0, 0)
            m_hotturn(0, 0)
            m_maskproduct(0, 0, True)
            m_queries(0, 0, 0, True)
            m_queries(0, 0, 1)
            pe.wait_ge(m_k, 1)
            m_input(1, 1)
            m_bandproduct(0)
            m_scores(0)
            m_logits(1, 1)
            m_hotturn(1, 1)

            def m_step(b, u, more, first):
                m_maskproduct(b + 1, 1 - u, False)
                m_queries(b + 1, 1 - u, 0, first)
                m_pturns(b)
                m_queries(b + 1, 1 - u, 1)
                m_context(b, u)
                if more:
                    pe.wait_ge(m_k, b + 2)
                    m_input(b + 2, u)
                m_bandproduct(b + 1)
                m_scores(b + 1)
                if more:
                    m_logits(b + 2, u)
                m_output(b, u, more)

            m_step(0, 0, True, True)
            m_step(1, 1, True, False)
            with pe.Fori(1, NB // 2 - 1) as i:
                for u in range(2):
                    m_step(2 * i + u, u, True, False)
            m_step(NB - 2, 0, False, False)
            m_pturns(NB - 1, True)
            m_context(NB - 1, 1)
            pe.wait_ge(m_out, NB - 1)
            m_output(NB - 1, 1)

            def n_input(b, u):
                pe.wait_ge(n_xn, b + 1)
                if b >= 2:
                    pe.wait_ge(n_all, b - 1)
                for k in range(KD):
                    for t in range(2):
                        ins = nc.tensor.transpose(ps[:, 4 + u, k * S + t * P:k * S + t * P + P],
                                                  nxn[:, 2 * b + t, k * P:(k + 1) * P], ident[:])
                ins.then_inc(n_turned, 1)

            def n_logits(b, u):
                pe.wait_ge(n_xnT, 2 * b + 2)
                for t in range(2):
                    for k in range(KD):
                        ins = mm(ps[:, 3, bass.ds(EF * (2 * b + t), EF)], xnT[:, u, k, t * P:(t + 1) * P], gw2[:, k, :],
                                 start=(k == 0), stop=(k == 1))
                ins.then_inc(n_log, 1)

            pe.wait_ge(m_out, NB)
            n_input(0, 0)
            n_input(1, 1)
            for b in range(NB):
                n_logits(b, b % 2)
                if b + 2 < NB:
                    n_input(b + 2, b % 2)

            def n_gateturn(j):
                pe.wait_ge(n_gate, 1)
                if j >= 2:
                    pe.wait_ge(n_GT, j - 1)
                for t in range(4):
                    ins = nc.tensor.transpose(ps[0:EF, 6 + j % 2, t * P:t * P + P], nG[:, 4 * j + t, :], ident[:])
                ins.then_inc(n_gturn, 1)

            def e_hidden(j, e, first=False):
                n = EF * j + e
                if e >= 3:
                    pe.wait_ge(e_hg, n - 2)
                elif e == 0 and not first:
                    pe.wait_ge(e_hg, n)
                c = bass.ds(CH * j, CH)
                for k in range(KD):
                    ins = split_product(bank(e % 3), [w_[:, k, e * FH:(e + 1) * FH] for w_ in (w1h, w1l)],
                                        [x_[:, k, c] for x_ in (xmh, xml)], k == 0, k == KD - 1)
                ins.then_inc(e_hmm, 1)

            def e_out(j, e):
                pe.wait_ge(e_l, EF * j + e + 1)
                for h in range(2):
                    ins = split_product(bank(4 + h), [w_[:, e, h * P:(h + 1) * P] for w_ in (w2h, w2l)],
                                        [h_[:, e % 3, :] for h_ in (hrh, hrl)], e == 0, False)
                if e == EF - 1:
                    for h in range(2):
                        ins = mm(bank(4 + h), b2[:, h * P:(h + 1) * P], GTa[:, bass.ds(CH * j, CH)], start=False, stop=True,
                                 skip_group_check=True)
                ins.then_inc(e_ymm, 1)

            def e_chunk(j, more=True):
                for e in range(EF):
                    if e + 2 < EF:
                        e_hidden(j, e + 2)
                    elif more:
                        e_hidden(j + 1, e + 2 - EF)
                    e_out(j, e)
                pe.wait_ge(e_y, j + 1)
                for t in range(4):
                    for k in range(KD):
                        ins = nc.tensor.transpose(bank2(6 + t // 2)[:, t % 2, k * P:(k + 1) * P], yT[:, k, t * P:(t + 1) * P],
                                                  ident[:])
                    if t % 2:
                        ins.then_inc(e_yturn, 1)

            pe.wait_ge(n_all, NB)
            n_gateturn(0)
            n_gateturn(1)
            pe.wait_ge(w_low, 5)
            e_hidden(0, 0, True)
            e_hidden(0, 1, True)
            n_gateturn(2)
            n_gateturn(3)
            pe.wait_ge(w_low, 6)
            pe.wait_ge(n_GT, NCH)
            with pe.Fori(0, NCH - 1) as j:
                e_chunk(j)
            e_chunk(NCH - 1, False)


def kernel(**inputs):
    import concourse.bacc as bacc
    from concourse.bass_utils import run_bass_kernel_spmd as run

    a = {k: np.asarray(v) for k, v in inputs.items()}
    a["ctxT"] = np.ascontiguousarray(a["ctx_1024"].reshape(N, D).T)
    a["L0_xattn_WT"] = np.ascontiguousarray(a["L0_xattn_W"].T)
    a["L1_xattn_WT"] = np.ascontiguousarray(a["L1_xattn_W"].T)
    a["xattn1_bT"] = np.ascontiguousarray(a["L1_xattn_b"].reshape(KD, P).T)
    a["ff_b1T"] = np.ascontiguousarray(a["L1_ffn_ff_b1"].T)
    relT = a["L1_ffn_rel_table"].T
    band = [np.clip(np.arange(RELW) - (P - 1), -MAXP, MAXP) + MAXP, np.clip(np.arange(RELW) - MAXP, -MAXP, MAXP) + MAXP]
    a["relx"] = np.ascontiguousarray(relT[:, np.stack(band)])
    a["rele"] = np.ascontiguousarray(relT[:, [2 * MAXP, 0]])
    names = ["x", "g_xattn", "g_ffn", "ctxT", "L0_xattn_WT", "L0_xattn_b", "L0_ffn_w_up", "L0_ffn_w_gate",
             "L0_ffn_w_down", "L1_xattn_WT", "xattn1_bT", "ctx_1024", "ff_b1T", "relx", "rele"]
    names += ["L1_ffn_" + n for n in ("ln1_w", "ln1_b", "ln2_w", "ln2_b", "attn_gate_w", "q_w", "q_b", "k_w", "k_b", "v_w",
                                      "v_b", "o_w", "o_b", "ff_gate_w", "ff_w1", "ff_w2", "ff_b2")]
    nc = bacc.Bacc("TRN2", target_bir_lowering=False, num_devices=1)
    arrays, args = {}, {}
    for name in names:
        v = np.ascontiguousarray(a[name])
        arrays[f"in_{name}"] = v
        args[name] = nc.dram_tensor(f"in_{name}", v.shape, mybir.dt.from_np(v.dtype), kind="ExternalInput").ap()
    args["skew"] = nc.dram_tensor("skew", (4, P, RELROW), F32, kind="Internal").ap()
    args["gscr"] = nc.dram_tensor("gscr", (EF, N), F32, kind="Internal").ap()
    out = nc.dram_tensor("out", (NB, S, D), F32, kind="ExternalOutput").ap()
    gated_block_kernel(nc, args, out)
    r = run(nc, [arrays], core_ids=[0])
    return r.results[0]["out"]
```
